# Optimizing a Trainium2 kernel written in Bass

```python
import numpy as np
import jax
import jax.numpy as jnp

def _softmax(x, axis=-1):
    return jax.nn.softmax(x, axis=axis)

def _gelu(x):
    return jax.nn.gelu(x, approximate=True)

def _silu(x):
    return jax.nn.silu(x)

def _sigmoid(x):
    return jax.nn.sigmoid(x)

def _layernorm(x, axis=-1, eps=1e-05):
    m = jnp.mean(x, axis=axis, keepdims=True)
    v = jnp.var(x, axis=axis, keepdims=True)
    return (x - m) / jnp.sqrt(v + eps)

def _scatter_add(tgt, idx, src, axis=0):
    return tgt.at[idx].add(src)

def _segment_sum(src, seg, n):
    return jax.ops.segment_sum(src, seg, n)
kernel_name = 'mk_flamingo_gated_d4_seqx_r4_05bc7f'

def setup_inputs(seed: int=0):
    np.random.seed(seed)
    _w = jnp.asarray

    def _rec_inputs():
        import jax
        import jax.numpy as jnp
        _rk = jax.random.key(seed)
        x = 0.002226 + 0.9996 * jax.random.normal(jax.random.fold_in(_rk, 1), (8, 512, 256), jnp.float32)
        _lenS = 512 - jax.random.randint(jax.random.fold_in(_rk, 7), (8,), 0, max(1, 512 // 4) + 1, jnp.int32)
        _lenS2 = 512 - jax.random.randint(jax.random.fold_in(_rk, 8), (8,), 0, max(1, 512 // 4) + 1, jnp.int32)
        _ctx_1024P = jax.random.normal(jax.random.fold_in(_rk, 11), (8, 16, 256), jnp.float32)
        _ctx_1024c = jax.random.dirichlet(jax.random.fold_in(_rk, 511), 0.3 * jnp.ones((16,), jnp.float32), (8, 512))
        _ctx_1024t = jnp.einsum('bsk,bkd->bsd', _ctx_1024c, _ctx_1024P)
        _ctx_1024t = _ctx_1024t * jax.lax.rsqrt(jnp.mean(jnp.square(_ctx_1024t)) + 1e-12) * 0.953939
        ctx_1024 = -7.10856e-05 + 0.999911 * (_ctx_1024t + 0.3 * jax.random.normal(jax.random.fold_in(_rk, 611), (8, 512, 256), jnp.float32))
        _validS = jnp.arange(512)[None, :] < _lenS[:, None]
        _validS2 = jnp.arange(512)[None, :] < _lenS2[:, None]
        _causal = jnp.tril(jnp.ones((512, 512), dtype=bool))
        mask_1x1xSxS2_ik0 = jnp.where(jnp.broadcast_to(_validS2[0:1, None, None, :], (1, 1, 512, 512)), 0, 1).astype(jnp.int32)
        _g = jax.random.normal(jax.random.fold_in(_rk, 9001), (2, 4), jnp.float32)
        _g = jnp.sign(_g) * jnp.maximum(jnp.abs(_g), 1.0) + (_g == 0) * 1.0
        g_xattn = _g[0]
        g_ffn = _g[1]
        return (x, ctx_1024, mask_1x1xSxS2_ik0, g_xattn, g_ffn)
    x, ctx_1024, mask_1x1xSxS2_ik0, g_xattn, g_ffn = _rec_inputs()

    def _L0_xattn_setup():
        import jax, jax.numpy as jnp
        import numpy as np
        DIM = 256
        HEAD_DIM = 64
        NUM_HEADS = 8
        INNER = HEAD_DIM * NUM_HEADS
        ROT_DIM = HEAD_DIM
        ROPE_BASE = 10000.0
        EPS = 1e-05

        def layer_norm(x, g, b):
            mu = jnp.mean(x, axis=-1, keepdims=True)
            var = jnp.var(x, axis=-1, keepdims=True)
            return (x - mu) * jax.lax.rsqrt(var + EPS) * g + b

        def rope_rotate_k(k):
            n = k.shape[1]
            half = ROT_DIM // 2
            inv_freq = 1.0 / ROPE_BASE ** (jnp.arange(0, ROT_DIM, 2, dtype=jnp.float32) / ROT_DIM)
            theta = jnp.arange(n, dtype=jnp.float32)[:, None] * inv_freq[None, :]
            angles = jnp.concatenate([theta, theta], axis=-1)
            cos = jnp.cos(angles)[None, :, None, :].astype(k.dtype)
            sin = jnp.sin(angles)[None, :, None, :].astype(k.dtype)
            k_rope, k_pass = (k[..., :ROT_DIM], k[..., ROT_DIM:])
            neg_half = jnp.concatenate([-k_rope[..., half:], k_rope[..., :half]], axis=-1)
            k_rope = k_rope * cos + neg_half * sin
            return jnp.concatenate([k_rope, k_pass], axis=-1)
        key = jax.random.key(seed)
        ks = jax.random.split(key, 5)
        b, n, m = (8, 2048, 64)
        s = 1.0 / np.sqrt(DIM)
        return {'x': jax.random.normal(ks[0], (b, n, DIM), jnp.float32), 'latents': jax.random.normal(ks[1], (b, m, DIM), jnp.float32), 'gamma_x': jnp.ones((DIM,), jnp.float32), 'beta_x': jnp.zeros((DIM,), jnp.float32), 'gamma_l': jnp.ones((DIM,), jnp.float32), 'beta_l': jnp.zeros((DIM,), jnp.float32), 'Wq': jax.random.normal(ks[2], (DIM, INNER), jnp.float32) * s, 'Wkv': jax.random.normal(ks[3], (DIM, 2 * INNER), jnp.float32) * s, 'Wo': jax.random.normal(ks[4], (INNER, DIM), jnp.float32) * (1.0 / np.sqrt(INNER))}
    _L0_xattn_all = _L0_xattn_setup()
    _L0_xattn_in = {k: v for k, v in _L0_xattn_all.items() if k in ('gamma_x', 'beta_x', 'gamma_l', 'beta_l', 'Wq', 'Wkv', 'Wo')}
    del _L0_xattn_all

    def _L0_ffn_setup():
        import jax, jax.numpy as jnp
        import numpy as np
        D_MODEL, D_FF, RANK = (256, 1024, 64)
        B, S = (4, 1024)
        key = jax.random.key(seed)
        ks = jax.random.split(key, 7)
        return {'x': jax.random.normal(ks[0], (B, S, D_MODEL), dtype=jnp.float32), 'U1': jax.random.normal(ks[1], (D_MODEL, RANK), dtype=jnp.float32) * 0.02, 'V1': jax.random.normal(ks[2], (RANK, D_FF), dtype=jnp.float32) * 0.02, 'b1': jnp.zeros((D_FF,), dtype=jnp.float32), 'U2': jax.random.normal(ks[3], (D_FF, RANK), dtype=jnp.float32) * 0.02, 'V2': jax.random.normal(ks[4], (RANK, D_MODEL), dtype=jnp.float32) * 0.02, 'b2': jnp.zeros((D_MODEL,), dtype=jnp.float32)}
    _L0_ffn_all = _L0_ffn_setup()
    _L0_ffn_in = {k: v for k, v in _L0_ffn_all.items() if k in ('U1', 'V1', 'b1', 'U2', 'V2', 'b2')}
    del _L0_ffn_all

    def _L1_xattn_setup():
        import jax, jax.numpy as jnp
        import numpy as np
        DIM = 256
        NUM_HEADS = 8
        HEAD_DIM = 64
        INNER = NUM_HEADS * HEAD_DIM
        key = jax.random.key(seed)
        ks = jax.random.split(key, 7)
        B, N, M = (8, 128, 1024)
        x = jax.random.normal(ks[0], (B, N, DIM), dtype=jnp.float32)
        context = jax.random.normal(ks[1], (B, M, DIM), dtype=jnp.float32)
        s_in = 1.0 / np.sqrt(DIM)
        s_inner = 1.0 / np.sqrt(INNER)
        Wq = jax.random.normal(ks[2], (DIM, INNER), dtype=jnp.float32) * s_in
        Wk = jax.random.normal(ks[3], (DIM, INNER), dtype=jnp.float32) * s_in
        Wv = jax.random.normal(ks[4], (DIM, INNER), dtype=jnp.float32) * s_in
        Wo = jax.random.normal(ks[5], (INNER, DIM), dtype=jnp.float32) * s_inner
        bo = jax.random.normal(ks[6], (DIM,), dtype=jnp.float32) * 0.01
        return {'x': x, 'context': context, 'Wq': Wq, 'Wk': Wk, 'Wv': Wv, 'Wo': Wo, 'bo': bo}
    _L1_xattn_all = _L1_xattn_setup()
    _L1_xattn_in = {k: v for k, v in _L1_xattn_all.items() if k in ('Wq', 'Wk', 'Wv', 'Wo', 'bo')}
    del _L1_xattn_all

    def _L1_ffn_setup():
        import jax, jax.numpy as jnp
        import numpy as np
        T, Z, D_DIM = (8, 512, 256)
        N_EXP, P_SLOT, H = (64, 32, 256)
        LN_EPS = 1e-05
        key = jax.random.key(seed)
        k = jax.random.split(key, 5)
        s = 0.02
        return {'x': jax.random.normal(k[0], (T, Z, D_DIM), dtype=jnp.float32), 'phi_w': jax.random.normal(k[1], (N_EXP * P_SLOT, D_DIM), dtype=jnp.float32) * s, 'phi_b': jax.random.normal(k[2], (N_EXP * P_SLOT,), dtype=jnp.float32) * s, 'expert_w': jax.random.normal(k[3], (N_EXP, D_DIM, H), dtype=jnp.float32) * s, 'expert_b': jax.random.normal(k[4], (N_EXP, H), dtype=jnp.float32) * s}
    _L1_ffn_all = _L1_ffn_setup()
    _L1_ffn_in = {k: v for k, v in _L1_ffn_all.items() if k in ('phi_w', 'phi_b', 'expert_w', 'expert_b')}
    del _L1_ffn_all

    def _L2_xattn_setup():
        import jax, jax.numpy as jnp
        import numpy as np
        B, S, D, H = (2, 512, 256, 16)
        DK = D // H

        def rope_tables(seq_len, d_k):
            inv_freq = 1.0 / 10000.0 ** (jnp.arange(0, d_k, 2, dtype=jnp.float32) / d_k)
            t = jnp.arange(seq_len, dtype=jnp.float32)
            freqs = jnp.einsum('i,j->ij', t, inv_freq)
            emb = jnp.concatenate([freqs, freqs], axis=-1)
            return (jnp.cos(emb), jnp.sin(emb))

        def apply_rope(x, cos, sin):
            b, h, s, dk = x.shape
            xr = x.reshape(b, h, s, dk // 2, 2)
            cr = cos.reshape(1, 1, s, dk // 2, 2)
            sr = sin.reshape(1, 1, s, dk // 2, 2)
            out = jnp.stack([xr[..., 0] * cr[..., 0] - xr[..., 1] * sr[..., 0], xr[..., 0] * sr[..., 1] + xr[..., 1] * cr[..., 1]], axis=-1)
            return out.reshape(b, h, s, dk)
        key = jax.random.key(seed)
        ks = jax.random.split(key, 7)
        scale = 1.0 / np.sqrt(D)
        q = jax.random.normal(ks[0], (B, S, D), dtype=jnp.float32)
        k = jax.random.normal(ks[1], (B, S, D), dtype=jnp.float32)
        v = jax.random.normal(ks[2], (B, S, D), dtype=jnp.float32)
        mask = jnp.tril(jnp.ones((S, S), dtype=jnp.int32))[None, None]
        wq = jax.random.normal(ks[3], (D, D), dtype=jnp.float32) * scale
        wk = jax.random.normal(ks[4], (D, D), dtype=jnp.float32) * scale
        wv = jax.random.normal(ks[5], (D, D), dtype=jnp.float32) * scale
        wo = jax.random.normal(ks[6], (D, D), dtype=jnp.float32) * scale
        return {'q': q, 'k': k, 'v': v, 'mask': mask, 'wq': wq, 'wk': wk, 'wv': wv, 'wo': wo}
    _L2_xattn_all = _L2_xattn_setup()
    _L2_xattn_in = {k: v for k, v in _L2_xattn_all.items() if k in ('wq', 'wk', 'wv', 'wo')}
    del _L2_xattn_all

    def _L2_ffn_setup():
        import jax, jax.numpy as jnp
        import numpy as np
        DIM = 256
        NUM_EXPERTS = 6
        TOP_K = 2
        HIDDEN = DIM * 2
        key = jax.random.key(seed)
        ks = jax.random.split(key, 7)
        s_in = 1.0 / np.sqrt(DIM)
        s_h = 1.0 / np.sqrt(HIDDEN)
        x = jax.random.normal(ks[0], (4, 512, DIM), dtype=jnp.float32)
        Wg = jax.random.uniform(ks[1], (DIM, NUM_EXPERTS), jnp.float32, -s_in, s_in)
        bg = jax.random.uniform(ks[2], (NUM_EXPERTS,), jnp.float32, -s_in, s_in)
        W1 = jax.random.uniform(ks[3], (NUM_EXPERTS, DIM, HIDDEN), jnp.float32, -s_in, s_in)
        b1 = jax.random.uniform(ks[4], (NUM_EXPERTS, HIDDEN), jnp.float32, -s_in, s_in)
        W2 = jax.random.uniform(ks[5], (NUM_EXPERTS, HIDDEN, DIM), jnp.float32, -s_h, s_h)
        b2 = jax.random.uniform(ks[6], (NUM_EXPERTS, DIM), jnp.float32, -s_h, s_h)
        return {'x': x, 'Wg': Wg, 'bg': bg, 'W1': W1, 'b1': b1, 'W2': W2, 'b2': b2}
    _L2_ffn_all = _L2_ffn_setup()
    _L2_ffn_in = {k: v for k, v in _L2_ffn_all.items() if k in ('Wg', 'bg', 'W1', 'b1', 'W2', 'b2')}
    del _L2_ffn_all

    def _L3_xattn_setup():
        import jax, jax.numpy as jnp
        import numpy as np
        EMBED_DIM = 256
        NUM_HEADS = 16
        HEAD_DIM = EMBED_DIM // NUM_HEADS
        SCALE = HEAD_DIM ** (-0.5)
        key = jax.random.key(seed)
        ks = jax.random.split(key, 8)
        B, Nq, Nkv, C = (2, 512, 512, EMBED_DIM)
        s = C ** (-0.5)
        return {'q': jax.random.normal(ks[0], (B, Nq, C), dtype=jnp.float32), 'kv': jax.random.normal(ks[1], (B, Nkv, C), dtype=jnp.float32), 'w_q': jax.random.normal(ks[2], (C, C), dtype=jnp.float32) * s, 'b_q': jnp.zeros((C,), dtype=jnp.float32), 'w_kv': jax.random.normal(ks[3], (C, 2 * C), dtype=jnp.float32) * s, 'b_kv': jnp.zeros((2 * C,), dtype=jnp.float32), 'w_out': jax.random.normal(ks[4], (C, C), dtype=jnp.float32) * s, 'b_out': jnp.zeros((C,), dtype=jnp.float32)}
    _L3_xattn_all = _L3_xattn_setup()
    _L3_xattn_in = {k: v for k, v in _L3_xattn_all.items() if k in ('w_q', 'b_q', 'w_kv', 'b_kv', 'w_out', 'b_out')}
    del _L3_xattn_all

    def _L3_ffn_setup():
        import jax, jax.numpy as jnp
        import numpy as np
        BEST_K = 2

        def _expert(xf, w1, w3, w2):
            return jax.nn.silu(xf @ w1) * (xf @ w3) @ w2
        key = jax.random.key(seed)
        ks = jax.random.split(key, 9)
        E, S_sh, D, H = (8, 2, 256, 128)
        B, S = (2, 512)
        w = lambda k, shape: jax.random.normal(k, shape, dtype=jnp.float32) * 0.02
        return {'x': jax.random.normal(ks[0], (B, S, D), dtype=jnp.float32), 'router_w': w(ks[1], (D, E)), 'router_b': jnp.zeros((E,), dtype=jnp.float32), 'routed_w1': w(ks[2], (E, D, H)), 'routed_w3': w(ks[3], (E, D, H)), 'routed_w2': w(ks[4], (E, H, D)), 'shared_w1': w(ks[5], (S_sh, D, H)), 'shared_w3': w(ks[6], (S_sh, D, H)), 'shared_w2': w(ks[7], (S_sh, H, D))}
    _L3_ffn_all = _L3_ffn_setup()
    _L3_ffn_in = {k: v for k, v in _L3_ffn_all.items() if k in ('router_w', 'router_b', 'routed_w1', 'routed_w3', 'routed_w2', 'shared_w1', 'shared_w3', 'shared_w2')}
    del _L3_ffn_all
    return {'x': x, 'ctx_1024': ctx_1024, 'mask_1x1xSxS2_ik0': mask_1x1xSxS2_ik0, 'g_xattn': g_xattn, 'g_ffn': g_ffn, 'L0_xattn_gamma_x': _L0_xattn_in['gamma_x'], 'L0_xattn_beta_x': _L0_xattn_in['beta_x'], 'L0_xattn_gamma_l': _L0_xattn_in['gamma_l'], 'L0_xattn_beta_l': _L0_xattn_in['beta_l'], 'L0_xattn_Wq': _L0_xattn_in['Wq'], 'L0_xattn_Wkv': _L0_xattn_in['Wkv'], 'L0_xattn_Wo': _L0_xattn_in['Wo'], 'L0_ffn_U1': _L0_ffn_in['U1'], 'L0_ffn_V1': _L0_ffn_in['V1'], 'L0_ffn_b1': _L0_ffn_in['b1'], 'L0_ffn_U2': _L0_ffn_in['U2'], 'L0_ffn_V2': _L0_ffn_in['V2'], 'L0_ffn_b2': _L0_ffn_in['b2'], 'L1_xattn_Wq': _L1_xattn_in['Wq'], 'L1_xattn_Wk': _L1_xattn_in['Wk'], 'L1_xattn_Wv': _L1_xattn_in['Wv'], 'L1_xattn_Wo': _L1_xattn_in['Wo'], 'L1_xattn_bo': _L1_xattn_in['bo'], 'L1_ffn_phi_w': _L1_ffn_in['phi_w'], 'L1_ffn_phi_b': _L1_ffn_in['phi_b'], 'L1_ffn_expert_w': _L1_ffn_in['expert_w'], 'L1_ffn_expert_b': _L1_ffn_in['expert_b'], 'L2_xattn_wq': _L2_xattn_in['wq'], 'L2_xattn_wk': _L2_xattn_in['wk'], 'L2_xattn_wv': _L2_xattn_in['wv'], 'L2_xattn_wo': _L2_xattn_in['wo'], 'L2_ffn_Wg': _L2_ffn_in['Wg'], 'L2_ffn_bg': _L2_ffn_in['bg'], 'L2_ffn_W1': _L2_ffn_in['W1'], 'L2_ffn_b1': _L2_ffn_in['b1'], 'L2_ffn_W2': _L2_ffn_in['W2'], 'L2_ffn_b2': _L2_ffn_in['b2'], 'L3_xattn_w_q': _L3_xattn_in['w_q'], 'L3_xattn_b_q': _L3_xattn_in['b_q'], 'L3_xattn_w_kv': _L3_xattn_in['w_kv'], 'L3_xattn_b_kv': _L3_xattn_in['b_kv'], 'L3_xattn_w_out': _L3_xattn_in['w_out'], 'L3_xattn_b_out': _L3_xattn_in['b_out'], 'L3_ffn_router_w': _L3_ffn_in['router_w'], 'L3_ffn_router_b': _L3_ffn_in['router_b'], 'L3_ffn_routed_w1': _L3_ffn_in['routed_w1'], 'L3_ffn_routed_w3': _L3_ffn_in['routed_w3'], 'L3_ffn_routed_w2': _L3_ffn_in['routed_w2'], 'L3_ffn_shared_w1': _L3_ffn_in['shared_w1'], 'L3_ffn_shared_w3': _L3_ffn_in['shared_w3'], 'L3_ffn_shared_w2': _L3_ffn_in['shared_w2']}

def reference(x, ctx_1024, mask_1x1xSxS2_ik0, g_xattn, g_ffn, L0_xattn_gamma_x, L0_xattn_beta_x, L0_xattn_gamma_l, L0_xattn_beta_l, L0_xattn_Wq, L0_xattn_Wkv, L0_xattn_Wo, L0_ffn_U1, L0_ffn_V1, L0_ffn_b1, L0_ffn_U2, L0_ffn_V2, L0_ffn_b2, L1_xattn_Wq, L1_xattn_Wk, L1_xattn_Wv, L1_xattn_Wo, L1_xattn_bo, L1_ffn_phi_w, L1_ffn_phi_b, L1_ffn_expert_w, L1_ffn_expert_b, L2_xattn_wq, L2_xattn_wk, L2_xattn_wv, L2_xattn_wo, L2_ffn_Wg, L2_ffn_bg, L2_ffn_W1, L2_ffn_b1, L2_ffn_W2, L2_ffn_b2, L3_xattn_w_q, L3_xattn_b_q, L3_xattn_w_kv, L3_xattn_b_kv, L3_xattn_w_out, L3_xattn_b_out, L3_ffn_router_w, L3_ffn_router_b, L3_ffn_routed_w1, L3_ffn_routed_w3, L3_ffn_routed_w2, L3_ffn_shared_w1, L3_ffn_shared_w3, L3_ffn_shared_w2):
    import jax
    import jax.numpy as jnp

    def _L0_xattn_ref(x, latents, gamma_x, beta_x, gamma_l, beta_l, Wq, Wkv, Wo):
        import jax, jax.numpy as jnp
        import numpy as np
        DIM = 256
        HEAD_DIM = 64
        NUM_HEADS = 8
        INNER = HEAD_DIM * NUM_HEADS
        ROT_DIM = HEAD_DIM
        ROPE_BASE = 10000.0
        EPS = 1e-05

        def layer_norm(x, g, b):
            mu = jnp.mean(x, axis=-1, keepdims=True)
            var = jnp.var(x, axis=-1, keepdims=True)
            return (x - mu) * jax.lax.rsqrt(var + EPS) * g + b

        def rope_rotate_k(k):
            n = k.shape[1]
            half = ROT_DIM // 2
            inv_freq = 1.0 / ROPE_BASE ** (jnp.arange(0, ROT_DIM, 2, dtype=jnp.float32) / ROT_DIM)
            theta = jnp.arange(n, dtype=jnp.float32)[:, None] * inv_freq[None, :]
            angles = jnp.concatenate([theta, theta], axis=-1)
            cos = jnp.cos(angles)[None, :, None, :].astype(k.dtype)
            sin = jnp.sin(angles)[None, :, None, :].astype(k.dtype)
            k_rope, k_pass = (k[..., :ROT_DIM], k[..., ROT_DIM:])
            neg_half = jnp.concatenate([-k_rope[..., half:], k_rope[..., :half]], axis=-1)
            k_rope = k_rope * cos + neg_half * sin
            return jnp.concatenate([k_rope, k_pass], axis=-1)
        b, n, _ = x.shape
        m = latents.shape[1]
        h, d = (NUM_HEADS, HEAD_DIM)
        scale = d ** (-0.5)
        xn = layer_norm(x, gamma_x, beta_x)
        ln = layer_norm(latents, gamma_l, beta_l)
        q = (ln @ Wq).reshape(b, m, h, d)
        kv_x = xn @ Wkv
        k_x, v_x = (kv_x[..., :INNER], kv_x[..., INNER:])
        kv_l = ln @ Wkv
        k_l, v_l = (kv_l[..., :INNER], kv_l[..., INNER:])
        k_x = k_x.reshape(b, n, h, d)
        v_x = v_x.reshape(b, n, h, d)
        k_x = rope_rotate_k(k_x)
        q = jnp.transpose(q, (0, 2, 1, 3)) * scale
        k_x = jnp.transpose(k_x, (0, 2, 1, 3))
        v_x = jnp.transpose(v_x, (0, 2, 1, 3))
        k_l = jnp.transpose(k_l.reshape(b, m, h, d), (0, 2, 1, 3))
        v_l = jnp.transpose(v_l.reshape(b, m, h, d), (0, 2, 1, 3))
        k = jnp.concatenate([k_x, k_l], axis=2)
        v = jnp.concatenate([v_x, v_l], axis=2)
        sim = jnp.einsum('bhid,bhjd->bhij', q, k)
        attn = jax.nn.softmax(sim, axis=-1)
        out = jnp.einsum('bhij,bhjd->bhid', attn, v)
        out = jnp.transpose(out, (0, 2, 1, 3)).reshape(b, m, INNER)
        return out @ Wo

    def _L0_ffn_ref(x, U1, V1, b1, U2, V2, b2):
        import jax, jax.numpy as jnp
        import numpy as np
        D_MODEL, D_FF, RANK = (256, 1024, 64)
        B, S = (4, 1024)
        P = jnp.einsum('bsd,dr->bsr', x, U1)
        H = jax.nn.gelu(jnp.einsum('bsr,rf->bsf', P, V1) + b1)
        Q = jnp.einsum('bsf,fr->bsr', H, U2)
        return jnp.einsum('bsr,rd->bsd', Q, V2) + b2

    def _L1_xattn_ref(x, context, Wq, Wk, Wv, Wo, bo):
        import jax, jax.numpy as jnp
        import numpy as np
        DIM = 256
        NUM_HEADS = 8
        HEAD_DIM = 64
        INNER = NUM_HEADS * HEAD_DIM
        B, N, _ = x.shape
        M = context.shape[1]
        scale = HEAD_DIM ** (-0.5)
        q = (x @ Wq).reshape(B, N, NUM_HEADS, HEAD_DIM).transpose(0, 2, 1, 3)
        k = (context @ Wk).reshape(B, M, NUM_HEADS, HEAD_DIM).transpose(0, 2, 1, 3)
        v = (context @ Wv).reshape(B, M, NUM_HEADS, HEAD_DIM).transpose(0, 2, 1, 3)
        attn = jax.nn.softmax(jnp.einsum('bhnd,bhmd->bhnm', q, k) * scale, axis=-1)
        out = jnp.einsum('bhnm,bhmd->bhnd', attn, v)
        out = out.transpose(0, 2, 1, 3).reshape(B, N, INNER)
        return out @ Wo + bo

    def _L1_ffn_ref(x, phi_w, phi_b, expert_w, expert_b):
        import jax, jax.numpy as jnp
        import numpy as np
        T, Z, D_DIM = (8, 512, 256)
        N_EXP, P_SLOT, H = (64, 32, 256)
        LN_EPS = 1e-05
        t, z, d = x.shape
        n = expert_w.shape[0]
        p = phi_w.shape[0] // n
        logits = (jnp.einsum('tzd,ed->tze', x, phi_w) + phi_b).reshape(t, z, n, p)
        D = jax.nn.softmax(logits, axis=3)
        C = jax.nn.softmax(logits, axis=2)
        X_tilde = jnp.einsum('tznp,tzd->npd', D, x)
        X_tilde = jnp.clip(X_tilde, -33000.0, 65000.0)
        mu = jnp.mean(X_tilde, axis=-1, keepdims=True)
        var = jnp.mean(jnp.square(X_tilde - mu), axis=-1, keepdims=True)
        X_tilde = (X_tilde - mu) * jax.lax.rsqrt(var + LN_EPS)
        X_tilde = jnp.tanh(X_tilde)
        Y_tilde = jnp.einsum('npd,ndH->npH', X_tilde, expert_w) + expert_b[:, None, :]
        Y = jnp.einsum('tznp,npH->tzH', C, Y_tilde)
        return Y

    def _L2_xattn_ref(q, k, v, mask, wq, wk, wv, wo):
        import jax, jax.numpy as jnp
        import numpy as np
        B, S, D, H = (2, 512, 256, 16)
        DK = D // H

        def rope_tables(seq_len, d_k):
            inv_freq = 1.0 / 10000.0 ** (jnp.arange(0, d_k, 2, dtype=jnp.float32) / d_k)
            t = jnp.arange(seq_len, dtype=jnp.float32)
            freqs = jnp.einsum('i,j->ij', t, inv_freq)
            emb = jnp.concatenate([freqs, freqs], axis=-1)
            return (jnp.cos(emb), jnp.sin(emb))

        def apply_rope(x, cos, sin):
            b, h, s, dk = x.shape
            xr = x.reshape(b, h, s, dk // 2, 2)
            cr = cos.reshape(1, 1, s, dk // 2, 2)
            sr = sin.reshape(1, 1, s, dk // 2, 2)
            out = jnp.stack([xr[..., 0] * cr[..., 0] - xr[..., 1] * sr[..., 0], xr[..., 0] * sr[..., 1] + xr[..., 1] * cr[..., 1]], axis=-1)
            return out.reshape(b, h, s, dk)
        b, s, d = q.shape
        query = jnp.einsum('bsd,od->bso', q, wq).reshape(b, s, H, DK).transpose(0, 2, 1, 3)
        key_ = jnp.einsum('bsd,od->bso', k, wk).reshape(b, s, H, DK).transpose(0, 2, 1, 3)
        value = jnp.einsum('bsd,od->bso', v, wv).reshape(b, s, H, DK).transpose(0, 2, 1, 3)
        cos, sin = rope_tables(s, DK)
        query = apply_rope(query, cos, sin)
        key_ = apply_rope(key_, cos, sin)
        scores = jnp.einsum('bhqd,bhkd->bhqk', query, key_) / jnp.sqrt(jnp.float32(DK))
        scores = jnp.where(mask == 0, jnp.float32(-1000000000.0), scores)
        attn = jax.nn.softmax(scores, axis=-1)
        x = jnp.einsum('bhqk,bhkd->bhqd', attn, value)
        x = x.transpose(0, 2, 1, 3).reshape(b, s, H * DK)
        return jnp.einsum('bsd,od->bso', x, wo)

    def _L2_ffn_ref(x, Wg, bg, W1, b1, W2, b2):
        import jax, jax.numpy as jnp
        import numpy as np
        DIM = 256
        NUM_EXPERTS = 6
        TOP_K = 2
        HIDDEN = DIM * 2
        gate_logits = jnp.einsum('bsd,de->bse', x, Wg) + bg
        topk_w, topk_idx = jax.lax.top_k(gate_logits, TOP_K)
        topk_w = jax.nn.softmax(topk_w, axis=-1)
        combine = jnp.sum(jax.nn.one_hot(topk_idx, NUM_EXPERTS, dtype=x.dtype) * topk_w[..., None], axis=-2)
        h = jnp.einsum('bsd,edh->ebsh', x, W1) + b1[:, None, None, :]
        h = jax.nn.gelu(h, approximate=False)
        y = jnp.einsum('ebsh,ehd->ebsd', h, W2) + b2[:, None, None, :]
        out = jnp.einsum('ebsd,bse->bsd', y, combine)
        return out

    def _L3_xattn_ref(q, kv, w_q, b_q, w_kv, b_kv, w_out, b_out):
        import jax, jax.numpy as jnp
        import numpy as np
        EMBED_DIM = 256
        NUM_HEADS = 16
        HEAD_DIM = EMBED_DIM // NUM_HEADS
        SCALE = HEAD_DIM ** (-0.5)
        B, Nq, C = q.shape
        _, Nkv, _ = kv.shape
        H, D = (NUM_HEADS, HEAD_DIM)
        qp = (q @ w_q + b_q).reshape(B, Nq, H, D).transpose(0, 2, 1, 3)
        kvp = (kv @ w_kv + b_kv).reshape(B, Nkv, 2, H, D).transpose(2, 0, 3, 1, 4)
        kp, vp = (kvp[0], kvp[1])
        attn = jnp.einsum('bhqd,bhkd->bhqk', qp, kp) * SCALE
        attn = jax.nn.softmax(attn, axis=-1)
        out = jnp.einsum('bhqk,bhkd->bhqd', attn, vp)
        out = out.transpose(0, 2, 1, 3).reshape(B, Nq, C)
        return out @ w_out + b_out

    def _L3_ffn_ref(x, router_w, router_b, routed_w1, routed_w3, routed_w2, shared_w1, shared_w3, shared_w2):
        import jax, jax.numpy as jnp
        import numpy as np
        BEST_K = 2

        def _expert(xf, w1, w3, w2):
            return jax.nn.silu(xf @ w1) * (xf @ w3) @ w2
        B, S, D = x.shape
        T = B * S
        xf = x.reshape(T, D)
        logits = xf @ router_w + router_b
        topk_vals, topk_idx = jax.lax.top_k(logits, BEST_K)
        sparse = jnp.full_like(logits, -jnp.inf)
        sparse = sparse.at[jnp.arange(T)[:, None], topk_idx].set(topk_vals)
        gates = jax.nn.softmax(sparse, axis=-1)
        routed = jax.vmap(_expert, in_axes=(None, 0, 0, 0))(xf, routed_w1, routed_w3, routed_w2)
        routed_out = jnp.einsum('etd,te->td', routed, gates)
        shared_out = jax.vmap(_expert, in_axes=(None, 0, 0, 0))(xf, shared_w1, shared_w3, shared_w2).sum(axis=0)
        return (routed_out + shared_out).reshape(B, S, D)
    x = x + jnp.tanh(g_xattn[0]) * _L0_xattn_ref(ctx_1024, _layernorm(x, axis=-1), L0_xattn_gamma_x, L0_xattn_beta_x, L0_xattn_gamma_l, L0_xattn_beta_l, L0_xattn_Wq, L0_xattn_Wkv, L0_xattn_Wo)
    x = x + jnp.tanh(g_ffn[0]) * _L0_ffn_ref(_layernorm(x, axis=-1), L0_ffn_U1, L0_ffn_V1, L0_ffn_b1, L0_ffn_U2, L0_ffn_V2, L0_ffn_b2)
    x = x + jnp.tanh(g_xattn[1]) * _L1_xattn_ref(_layernorm(x, axis=-1), ctx_1024, L1_xattn_Wq, L1_xattn_Wk, L1_xattn_Wv, L1_xattn_Wo, L1_xattn_bo)
    x = x + jnp.tanh(g_ffn[1]) * _L1_ffn_ref(_layernorm(x, axis=-1), L1_ffn_phi_w, L1_ffn_phi_b, L1_ffn_expert_w, L1_ffn_expert_b)
    x = x + jnp.tanh(g_xattn[2]) * _L2_xattn_ref(_layernorm(x, axis=-1), ctx_1024, ctx_1024, mask_1x1xSxS2_ik0, L2_xattn_wq, L2_xattn_wk, L2_xattn_wv, L2_xattn_wo)
    x = x + jnp.tanh(g_ffn[2]) * _L2_ffn_ref(_layernorm(x, axis=-1), L2_ffn_Wg, L2_ffn_bg, L2_ffn_W1, L2_ffn_b1, L2_ffn_W2, L2_ffn_b2)
    x = x + jnp.tanh(g_xattn[3]) * _L3_xattn_ref(_layernorm(x, axis=-1), ctx_1024, L3_xattn_w_q, L3_xattn_b_q, L3_xattn_w_kv, L3_xattn_b_kv, L3_xattn_w_out, L3_xattn_b_out)
    x = x + jnp.tanh(g_ffn[3]) * _L3_ffn_ref(_layernorm(x, axis=-1), L3_ffn_router_w, L3_ffn_router_b, L3_ffn_routed_w1, L3_ffn_routed_w3, L3_ffn_routed_w2, L3_ffn_shared_w1, L3_ffn_shared_w3, L3_ffn_shared_w2)
    return x

_drawn_inputs = setup_inputs


def setup_inputs(seed=0):
    import zlib

    import numpy as np

    out = dict(_drawn_inputs(seed))
    spreads = {'L0_xattn_gamma_x': (1.0, 0.2),
     'L0_xattn_beta_x': (0.0, 0.1),
     'L0_xattn_gamma_l': (1.0, 0.6),
     'L0_xattn_beta_l': (0.0, 0.1),
     'L0_ffn_b1': (0.0, 0.597),
     'L0_ffn_b2': (0.0, 0.1),
     'L3_xattn_b_q': (0.0, 0.776),
     'L3_xattn_b_kv': (0.0, 0.1),
     'L3_xattn_b_out': (0.0, 0.1),
     'L3_ffn_router_b': (0.0, 0.8)}
    factors = {'g_ffn': 21.584,
     'L0_ffn_U1': 8.0,
     'L0_ffn_V1': 8.0,
     'L0_ffn_U2': 3.928,
     'L0_ffn_V2': 4.41,
     'L1_ffn_phi_b': 8.0,
     'L2_ffn_bg': 3.704,
     'L2_ffn_b1': 8.0,
     'L2_ffn_b2': 5.869,
     'L3_ffn_router_w': 8.0,
     'L3_ffn_routed_w1': 8.0,
     'L3_ffn_routed_w3': 8.0,
     'L3_ffn_routed_w2': 8.0,
     'L3_ffn_shared_w1': 5.787,
     'L3_ffn_shared_w3': 5.785,
     'L3_ffn_shared_w2': 5.768,
     'L1_xattn_bo': 3.009}
    for name, (base, spread) in spreads.items():
        noise = np.random.default_rng([zlib.crc32(name.encode()), seed]).standard_normal(out[name].shape)
        drawn = base * np.exp(spread * noise) if base else spread * noise
        out[name] = jnp.asarray(drawn.astype(out[name].dtype))
    for name, factor in factors.items():
        out[name] = (out[name] * factor).astype(out[name].dtype)
    return out
```

```python
from contextlib import ExitStack

import numpy as np

import concourse.bass as bass
from concourse import mybir

ALU = mybir.AluOpType
ACT = mybir.ActivationFunctionType
AX = mybir.AxisListType
F32 = mybir.dt.float32
BF16 = mybir.dt.bfloat16
I32 = mybir.dt.int32

P = 128
B, S, D = 8, 512, 256
T = S // P
DC = D // P
ROW = T * D
EPS = 1e-5
RSQRT_SEED = 0x5F3759DF
HALF = 64
MASKED = -1e9


class Chain:

    def __init__(self, eng, sem, per=0, b=None, ahead=0):
        self.eng, self.sem, self.per, self.b, self.n, self.ahead = eng, sem, per, b, 0, ahead

    def value(self):
        return self.n if self.b is None else self.b * self.per + (self.n + self.ahead)

    def step(self, ins):
        self.n += 1
        ins.then_inc(self.sem, 1)

    def settle(self):
        self.eng.wait_ge(self.sem, self.value())

    def link(self, ins):
        self.step(ins)
        self.settle()

    def done(self):
        assert self.n == self.per, f"this loop's steps are {self.n}"


def rsqrt_steps(nc, ch, v, y, h, t):
    ch.link(nc.vector.tensor_scalar(v, v, EPS, None, ALU.add))
    ch.link(nc.vector.tensor_scalar(t.bitcast(I32), v.bitcast(I32), 1, None, ALU.logical_shift_right))
    ch.link(nc.vector.tensor_scalar(y.bitcast(I32), t.bitcast(I32), -1.0, float(RSQRT_SEED), ALU.mult, ALU.add))
    for _ in range(4):
        ch.link(nc.vector.tensor_tensor(t, y, y, ALU.mult))
        ch.link(nc.vector.tensor_tensor(t, t, v, ALU.mult))
        ch.link(nc.vector.tensor_scalar(t, t, -0.5, 1.5, ALU.mult, ALU.add))
        ch.link(nc.vector.tensor_tensor(y, y, t, ALU.mult))


LN_STEPS = T + T + 19 + T


def layer_norm(nc, ch, src, dst, st, keep=None):
    ch.eng.sem_inc(st["beat"], 1)
    for t in range(T):
        ch.step(nc.vector.bn_stats(st["six"][:, 6 * t:6 * t + 6], src(t)))
    ch.settle()
    ch.eng.sem_inc(st["beat"], 1)
    for t in range(T):
        ch.step(nc.vector.bn_aggr(st["mv"][:, 2 * t:2 * t + 2], st["six"][:, 6 * t:6 * t + 6]))
    ch.settle()
    var = st["mv"][:, :].rearrange("p (t s) -> p t s", s=2)[:, :, 1]
    rsqrt_steps(nc, ch, var, st["y"][:, 0:T], None, st["t"][:, 0:T])
    if keep is not None:
        ch.link(nc.vector.tensor_tensor(st["y"][:, 0:T], st["y"][:, 0:T], keep, ALU.mult))
    for t in range(T):
        ch.step(nc.vector.tensor_scalar(dst(t), src(t), st["mv"][:, 2 * t:2 * t + 1], st["y"][:, t:t + 1],
                                        ALU.subtract, ALU.mult))
    ch.settle()


class Fills:

    def __init__(self, g, banks, name, steps, ahead):
        self.banks, self.steps, self.ahead = banks, steps, ahead
        self.at = {s: i for i, s in enumerate(steps)}
        assert len(self.at) == len(steps)
        self.per = len(steps)
        self.filled, self.emptied = g.semaphore(name + "_filled"), g.semaphore(name + "_emptied")

    def bank(self, step):
        return self.banks[self.at[step] % len(self.banks)]

    def wait_room(self, pe, b, step):
        i, n = self.at[step], len(self.banks)
        pe.wait_ge(self.emptied, b * self.per + (self.ahead + max(i + 1, n)))

    def wait_filled(self, eng, b, step):
        eng.wait_ge(self.filled, b * self.per + (self.ahead + self.at[step] + 1))

    def wait_emptied(self, eng, b, step):
        eng.wait_ge(self.emptied, b * self.per + (self.ahead + len(self.banks) + self.at[step] + 1))


def attention_script(NS, G, KC, KH, NBK, early, rope_k, rope_q, lag):
    proj = []
    for gp in range(NBK):
        steps = []
        for half in range(KH):
            if rope_k and half == 0:
                steps += [("k", gp, half), ("kp", gp, half), ("hi", "k", gp, half), ("lo", "k", gp, half)]
            else:
                steps += [("k", gp, half), ("hi", "k", gp, half), ("lo", "k", gp, half)]
        steps += [("q", gp, 0)] + ([("qp", gp, 0)] if rope_q else []) + [("hi", "q", gp, 0), ("lo", "q", gp, 0)]
        proj.append(steps)
    vs = [("v", kt) for kt in range(KC)]
    NT = (2 if G == 1 else G) * KC
    W = NT // KC
    first = proj[0]
    rest = [s for p in proj[1:early] for s in p] + vs
    script = list(first)
    fills_left = [s for s in rest if s[0] in ("k", "kp", "q", "qp", "v")]
    per_fill = -(-NT // max(len(fills_left) - 2, 1))
    k = seen = 0
    for s in rest:
        script.append(s)
        if s[0] in ("k", "kp", "q", "qp", "v"):
            seen += 1
            if seen > 2:
                for _ in range(per_fill):
                    if k < NT:
                        script.append(("mx", 0, k))
                        k += 1
    script += [("mx", 0, i) for i in range(k, NT)] + [("mr", 0)]
    late = [p for p in proj[early:]]
    for q in range(NS * KC + lag):
        s, kc = q // KC, q % KC
        if q < NS * KC:
            for j in range(W):
                n = kc * W + j
                script.append(("st", s, n))
                if s + 1 < NS and n < NT // 2:
                    script += [("mx", s + 1, 2 * n), ("mx", s + 1, 2 * n + 1)]
                if s >= 1 and n == NT // 2:
                    script.append(("sum", s - 1))
                if s + 1 < NS and n == 3 * NT // 4:
                    script.append(("mr", s + 1))
                if s == 1 and late and n >= NT // 2 and n % 2 == 1:
                    m = next(i for i, step in enumerate(late[0]) if step[0] == "lo") + 1
                    take = late[0][:m]
                    del late[0][:m]
                    script += take
                    if not late[0]:
                        del late[0]
                if s == NS // 2 and n == NT // 2:
                    script.append(("ln",))
                if s == NS - 1 and n >= NT // 4 and (n - NT // 4) % 2 == 0 and (n - NT // 4) // 2 < 2 * DC:
                    i = (n - NT // 4) // 2
                    script.append((("xT", "cT")[i % 2], i // 2))
        if q >= lag:
            script.append(("pv", q - lag))
            if (q - lag) % KC == KC - 1:
                script.append(("oc", (q - lag) // KC))
    for i in range(2 * DC):
        step = (("xT", "cT")[i % 2], i // 2)
        if step not in script:
            script.append(step)
    script += [("sum", NS - 1)] + [("out", t) for t in range(T)]
    assert not late
    return script


def attention_stage(nc, g, pre, dr, *, heads, head_dim, gate, own_keys=False, norm_ctx=False, rope_k=False,
                    rope_q=False, masked=False, biased=False, out_bias=False):
    G = HALF // head_dim
    INNER = heads * head_dim
    W = 2 if G == 1 else G
    NS = heads // W
    NU = heads // G
    NBK = NU // 2
    KH = 2 if own_keys else 1
    KC = T * KH
    NT = W * KC
    LAG = 1 if G > 1 else 2
    VH = HALF if G == 1 else 32
    NPT = 8 if KH == 1 else 6
    EARLY = NBK if KH == 1 else 3
    OC = 4
    SCALE = head_dim ** -0.5
    F32R = mybir.dt.float32r

    script = attention_script(NS, G, KC, KH, NBK, EARLY, rope_k, rope_q, LAG)
    v_on_act = rope_q

    def stream(step):
        kind = step[0]
        if kind in ("mx", "sum", "out", "kp", "qp", "xT"):
            return "D"
        if kind == "k":
            return "D" if rope_k and step[2] == 0 else "A"
        if kind == "q":
            return "D" if rope_q else "A"
        if kind == "v":
            return "A" if v_on_act else "D"
        return "A" if kind in ("st", "cT") else None

    a_steps = [s for s in script if stream(s) == "A"]
    d_steps = [s for s in script if stream(s) == "D"]
    splits = [s[1:] for s in script if s[0] == "lo"]
    SPLITS = len(splits)
    rotated = [s for s in splits if (s[0] == "k" and rope_k and s[2] == 0) or (s[0] == "q" and rope_q)]
    SU_PER = NS * (NT - W)
    LO_PER, PV_PER = SPLITS, NS * KC
    mx_tiles = [(j, qc, kh) for j in range(W) for qc in range(T) for kh in range(KH)]

    def keys_of(s, j):
        return (2 * s + j, 2 * s + j) if G == 1 else (s, s * G + j)

    with ExitStack() as ctx:
        def sb(name, shape, dt=F32):
            return ctx.enter_context(nc.sbuf_tensor(pre + name, shape, dt))

        def ps(name):
            return ctx.enter_context(nc.psum_tensor(pre + name, [P, 512], F32))

        def sem(name):
            return g.semaphore(pre + name)

        KU = 2 * EARLY
        QU = KU if G == 1 else 3 * W
        wq, wk, wv = (sb(n, [P, DC, INNER]) for n in ("wq", "wk", "wv"))
        wo = sb("wo", [P, OC, D])
        wkp = sb("wkp", [P, DC, INNER]) if rope_k else None
        wqp = sb("wqp", [P, DC, INNER]) if rope_q else None
        cos, sin = (sb("cos", [P, S]), sb("sin", [P, S])) if rope_k else (None, None)
        ones = sb("ones", [P, HALF]) if G == 1 else None
        sel = sb("sel", [P, P]) if G > 1 else None
        hmask = sb("hmask", [P, 4]) if G > 1 else None
        gam = sb("gam", [P, 8]) if norm_ctx else None
        bqk = sb("bqk", [P, 2, NBK]) if biased else None
        bvb = sb("bvb", [P, INNER]) if biased else None
        bob = sb("bob", [P, D]) if out_bias else None
        XN, CN = sb("XN", [P, T, D]), sb("CN", [P, T, D])
        XT, CT = sb("XT", [P, DC, S]), sb("CT", [P, DC, S])
        F = sb("F", [HALF, 2, 2, S])
        TMP = sb("TMP", [HALF, S]) if rope_k else None
        KHI = sb("KHI", [P, KU, KH * S], F32R)
        KLO = sb("KLO", [P, KU, KH * S], F32R)
        QC = sb("QC", [P, NU, S]) if G > 1 else None
        QA = sb("QA", [P, QU, S], F32R)
        QB = sb("QB", [P, QU, S], F32R)
        V = sb("V", [P, KC, heads * VH])
        PT = sb("PT", [P, NPT, S])
        SU = sb("SU", [P, 2, W, S]) if G == 1 else None
        OS = sb("OS", [P, S]) if G > 1 else None
        R = sb("R", [P, S])
        AT = sb("AT", [P, OC, S])
        mpart = sb("mpart", [P, NT])
        negm = sb("negm", [P, W * T], BF16)
        st = statistics(nc, g, ctx, pre)
        if masked:
            mrow = sb("mrow", [P, T, S], I32)
            mbn, mbT = sb("mbn", [P, T, S], BF16), sb("mbT", [P, T, S], BF16)
            many = sb("many", [P, T])

        A = Fills(g, [ps(f"a{i}") for i in range(3)], pre + "A", a_steps, DC)
        Dv = Fills(g, [ps(f"d{i}") for i in range(2)], pre + "D", d_steps, DC)
        bank_o = [ps(f"o{i}") for i in range(2)]
        bank_m = ps("m")

        s_w = sem("weights")
        s_ctx = sem("ctx")
        s_cl = sem("ctxnorm")
        s_zero = sem("padding")
        s_ones = sem("ones")
        s_pad = sem("wo_rows")
        s_mk = sem("mask")
        s_mkt = sem("maskT")
        s_xn = sem("xn")
        s_xt = sem("xT")
        s_ct = sem("cT")
        s_f = sem("rotated")
        s_hi = sem("hi")
        s_lo = sem("lo")
        s_qm = sem("masked_q")
        s_nm = sem("negmax")
        s_mr = sem("maxrow")
        s_mc = sem("maxcopy")
        s_pv = sem("pv")
        s_su = sem("expsum")
        s_os = sem("osum")
        s_at = sem("attnT")
        s_vch = sem("vchain")
        s_pch = sem("pchain")
        s_beat = st["beat"]

        w_loads = [(wk[:, :, :], dr["wk"].rearrange("(c p) n -> p c n", p=P)),
                   (wq[:, :, :], dr["wq"].rearrange("(c p) n -> p c n", p=P)),
                   (wv[:, :, :], dr["wv"].rearrange("(c p) n -> p c n", p=P))]
        if rope_k:
            w_loads += [(wkp[:, :, :], dr["wkp"].rearrange("(c p) n -> p c n", p=P)),
                        (cos[:, :], dr["cos"]), (sin[:, :], dr["sin"])]
        if rope_q:
            w_loads += [(wqp[:, :, :], dr["wqp"].rearrange("(c p) n -> p c n", p=P))]
        if G > 1:
            w_loads += [(sel[:, :], dr["sel"]), (hmask[:, :], dr["hmask"])]
            wo_g = dr["wo"].rearrange("(g j r) n -> j r g n", j=G, r=head_dim)
            w_loads += [(wo[32 * j:32 * j + head_dim, :, :], wo_g[j]) for j in range(G)]
        else:
            w_loads += [(wo[:, :, :], dr["wo"].rearrange("(c p) n -> p c n", p=P))]
        if norm_ctx:
            for i, name in enumerate(("gamma_x", "beta_x", "gamma_l", "beta_l")):
                w_loads += [(gam[:, 2 * i + c:2 * i + c + 1], dr[name].rearrange("(c p o) -> c p o", p=P, o=1)[c])
                            for c in range(DC)]
        if biased:
            for i, name in enumerate(("b_q", "b_k")):
                w_loads += [(bqk[:, i, c:c + 1], dr[name].rearrange("(c p o) -> c p o", p=P, o=1)[c])
                            for c in range(NBK)]
            w_loads += [(bvb[:, :], dr["b_v"].rearrange("(o n) -> o n", o=1).to_broadcast([P, INNER]))]
        if out_bias:
            w_loads += [(bob[:, :], dr["b_o"].rearrange("(o n) -> o n", o=1).to_broadcast([P, D]))]
        if masked:
            w_loads += [(mrow[:, :, :], dr["mask"].rearrange("(t p) k -> p t k", p=P))]
        W_ALL = 16 * len(w_loads)
        ctx_rows = dr["ctx"].rearrange("(n p) d -> p n d", p=P)

        def unit_slot(u):
            return u % KU

        def added(i):
            return i // NT * (NT - W) + max(i % NT - W, i % NT % W) + 1

        def query_slot(h):
            return h % QU

        block = ctx.enter_context(nc.Block())

        @block.sync
        def _(sp):
            sp.dma_start(CN[:, :, :], ctx_rows[:, 0:T, :]).then_inc(s_ctx, 16)
            if G > 1:
                sp.wait_ge(s_pad, 1)
            for dst, src in w_loads:
                sp.dma_start(dst, src).then_inc(s_w, 16)
            sp.wait_ge(A.filled, DC)
            sp.dma_start(CN[:, :, :], ctx_rows[:, T:2 * T, :]).then_inc(s_ctx, 16)
            with sp.Fori(2, B) as b:
                A.wait_filled(sp, b - 2, ("cT", DC - 1))
                sp.dma_start(CN[:, :, :], ctx_rows[:, bass.ds(b * T, T), :]).then_inc(s_ctx, 16)
            sp.wait_ge(A.filled, (B - 2) * A.per + DC + A.at[("cT", DC - 1)] + 1)
            sp.dma_start(CN[:, :, :], ctx_rows[:, 0:T, :]).then_inc(s_ctx, 16)

        @block.gpsimd
        def _(pool):
            pads = [(KLO[HALF:P, :, :], 0.0), (QB[HALF:P, :, :], 0.0)]
            for i, (rows, value) in enumerate(pads):
                nc.gpsimd.memset(rows.bitcast(F32), value).then_inc(s_pch, 1)
                pool.wait_ge(s_pch, i + 1)
            nc.gpsimd.memset(KLO[HALF:HALF + 1, :, :].bitcast(F32), 1.0).then_inc(s_zero, 1)
            if G > 1:
                pool.wait_ge(s_w, W_ALL)
                with pool.Fori(0, B) as b:
                    for s in range(NS):
                        pool.wait_ge(s_lo, b * LO_PER + splits.index(("q", s // 2, 0)) + 1)
                        if s >= 3:
                            A.wait_filled(pool, b, ("st", s - 3, NT - 1))
                        pool.sem_inc(s_beat, 1)
                        for j in range(G):
                            slot = query_slot(s * G + j)
                            nc.gpsimd.tensor_scalar(QA[:, slot, :], QC[:, s, :], hmask[:, j:j + 1], 0.0,
                                                    ALU.mult, ALU.add).then_inc(s_pch, 1)
                            last = nc.gpsimd.tensor_scalar(QB[0:HALF, slot, :], QC[0:HALF, s, :],
                                                           hmask[0:HALF, j:j + 1], 0.0, ALU.mult, ALU.add)
                        last.then_inc(s_qm, 1)
            else:
                with pool.Fori(0, B) as b:
                    for s in range(NS):
                        for n in range(W, NT):
                            i = s * NT + n
                            if n == W and s >= 2:
                                Dv.wait_filled(pool, b, ("sum", s - 2))
                            A.wait_emptied(pool, b, ("st", s, n))
                            total = SU[:, s % 2, n % W, :]
                            if n >= 2 * W:
                                pool.wait_ge(s_su, b * SU_PER + (added(i) - W))
                                so_far = total
                            else:
                                so_far = PT[:, (i - W) % NPT, :]
                            nc.gpsimd.tensor_tensor(total, so_far, PT[:, i % NPT, :], ALU.add).then_inc(s_su, 1)

        @block.tensor
        def _(pe):
            def turn(b, step):
                src = XN if step[0] == "xT" else CN
                F_ = Dv if step[0] == "xT" else A
                out = F_.bank(step) if b is not None else F_.banks[step[1]]
                if b is not None:
                    F_.wait_room(pe, b, step)
                for t in range(T):
                    last = pe.transpose(out[:, t * P:(t + 1) * P], src[:, t, step[1] * P:(step[1] + 1) * P],
                                        g.ident[:, :])
                last.then_inc(F_.filled, 1)

            if masked:
                pe.wait_ge(s_mk, 1)
                for kt in range(T):
                    if kt:
                        pe.wait_ge(s_mk, kt + 1)
                    for qt in range(T):
                        last = pe.matmul(Dv.banks[0][:, qt * P:(qt + 1) * P], mbn[:, qt, kt * P:(kt + 1) * P],
                                         g.ident_b[:, :], start=True, stop=True, skip_group_check=True)
                    last.then_inc(s_mkt, 1)
                pe.wait_ge(s_mk, T + 1)
            pe.wait_ge(s_xn, 1)
            for c in range(DC):
                turn(None, ("xT", c))
            if norm_ctx:
                pe.wait_ge(s_cl, 1)
            else:
                pe.wait_ge(s_ctx, 16)
            for c in range(DC):
                turn(None, ("cT", c))
            pe.wait_ge(s_w, W_ALL)
            pe.wait_ge(s_zero, 1)
            pe.wait_ge(s_ones, 1)
            pe.wait_ge(s_pad, 1 + out_bias)
            with pe.Fori(0, B) as b:
                pe.wait_ge(s_xt, b + 1)
                pe.wait_ge(s_ct, b + 1)
                for step in script:
                    kind = step[0]
                    if kind in ("k", "kp", "q", "qp"):
                        fills = A if stream(step) == "A" else Dv
                        fills.wait_room(pe, b, step)
                        out = fills.bank(step)
                        w = {"k": wk, "kp": wkp, "q": wq, "qp": wqp}[kind]
                        src = CT if kind[0] == "k" and step[2] == 0 else XT
                        for c in range(DC):
                            last = pe.matmul(out[:, :], w[:, c, step[1] * P:(step[1] + 1) * P], src[:, c, :],
                                             start=c == 0, stop=c == DC - 1)
                        last.then_inc(fills.filled, 1)
                    elif kind == "v":
                        fills = A if v_on_act else Dv
                        fills.wait_room(pe, b, step)
                        src, t = (XT, step[1] - T) if step[1] >= T else (CT, step[1])
                        for c in range(DC):
                            last = pe.matmul(fills.bank(step)[:, 0:INNER], src[:, c, t * P:(t + 1) * P], wv[:, c, :],
                                             start=c == 0, stop=c == DC - 1)
                        last.then_inc(fills.filled, 1)
                    elif kind == "mx":
                        s, k = step[1:]
                        j, qc, kh = mx_tiles[k]
                        u, h = keys_of(s, j)
                        if k == 0:
                            gp = s if G == 1 else s // 2
                            pe.wait_ge(s_lo, b * LO_PER + max(splits.index(("q", gp, 0)),
                                                              splits.index(("k", gp, KH - 1))) + 1)
                            if G > 1:
                                pe.wait_ge(s_qm, b * NS + s + 1)
                        Dv.wait_room(pe, b, step)
                        mm = pe.matmul(Dv.bank(step)[:, :], QA[:, query_slot(h), qc * P:(qc + 1) * P],
                                       KHI[:, unit_slot(u), kh * S:kh * S + S], start=True, stop=not masked)
                        if masked:
                            mm = pe.matmul(Dv.bank(step)[:, :], g.ident_b[:, :], mbn[:, qc, :], start=False, stop=True)
                        mm.then_inc(Dv.filled, 1)
                    elif kind == "mr":
                        pe.wait_ge(s_nm, b * NS + step[1] + 1)
                        for j in range(W):
                            for qc in range(T):
                                last = pe.matmul(bank_m[32 * j:32 * j + 1, qc * P:(qc + 1) * P],
                                                 negm[:, j * T + qc:j * T + qc + 1], g.ident_b[:, :],
                                                 start=True, stop=True, skip_group_check=True)
                        last.then_inc(s_mr, 1)
                    elif kind == "st":
                        s, n = step[1:]
                        kc, j = n // W, n % W
                        u, h = keys_of(s, j)
                        if n == 0:
                            pe.wait_ge(s_mc, b * NS + s + 1)
                        A.wait_room(pe, b, step)
                        out = A.bank(step)[:, :]
                        pe.matmul(out, KHI[:, unit_slot(u), kc * P:(kc + 1) * P], QA[:, query_slot(h), :],
                                  start=True, stop=False)
                        mm = pe.matmul(out, KLO[:, unit_slot(u), kc * P:(kc + 1) * P], QB[:, query_slot(h), :],
                                       start=False, stop=not masked)
                        if masked:
                            mm = pe.matmul(out, g.ident_b[:, :], mbT[:, kc, :], start=False, stop=True)
                        mm.then_inc(A.filled, 1)
                    elif kind == "pv":
                        s, kc = step[1] // KC, step[1] % KC
                        A.wait_emptied(pe, b, ("st", s, kc * W + W - 1))
                        if kc == 0 and s >= 2:
                            if G > 1:
                                pe.wait_ge(s_os, b * NS + s - 1)
                            else:
                                pe.wait_ge(s_at, b * NS + s - 1)
                        for j in range(W):
                            u, h = keys_of(s, j)
                            row = VH * j
                            last = pe.matmul(bank_o[s % 2][row:row + VH, :], V[:, kc, h * VH:h * VH + VH],
                                             PT[:, (s * NT + kc * W + j) % NPT, :], start=kc == 0, stop=kc == KC - 1)
                        last.then_inc(s_pv, 1)
                    elif kind == "sum":
                        Dv.wait_room(pe, b, step)
                        out = Dv.bank(step)
                        if G > 1:
                            pe.wait_ge(s_os, b * NS + step[1] + 1)
                            last = pe.matmul(out[:, :], sel[:, :], OS[:, :], start=True, stop=True)
                        else:
                            pe.wait_ge(s_su, b * SU_PER + (step[1] + 1) * (NT - W))
                            for j in range(W):
                                last = pe.matmul(out[HALF * j:HALF * j + HALF, :], ones[:, :], SU[:, step[1] % 2, j, :],
                                                 start=True, stop=True)
                        last.then_inc(Dv.filled, 1)
                    elif kind in ("xT", "cT"):
                        if kind == "xT" and step[1] == 0:
                            pe.wait_ge(s_xn, b + 2)
                        if kind == "cT" and step[1] == 0:
                            if norm_ctx:
                                pe.wait_ge(s_cl, b + 2)
                            else:
                                pe.wait_ge(s_ctx, b * 16 + 32)
                        turn(b, step)
                    elif kind == "out":
                        t = step[1]
                        if t == 0:
                            pe.wait_ge(s_at, b * NS + NS)
                        Dv.wait_room(pe, b, step)
                        for c in range(OC):
                            last = pe.matmul(Dv.bank(step)[:, 0:D], AT[:, c, t * P:(t + 1) * P], wo[:, c, :],
                                             start=c == 0, stop=c == OC - 1)
                        last.then_inc(Dv.filled, 1)

        @block.scalar
        def _(act):
            act.sem_inc(A.emptied, 3)

            def turned(step, out):
                c = step[1]
                if norm_ctx:
                    return nc.scalar.activation(CT[:, c, :], out[:, :], ACT.Identity, bias=gam[:, 2 + c:3 + c],
                                                scale=gam[:, c:c + 1])
                return nc.scalar.copy(CT[:, c, :], out[:, :])

            act.wait_ge(s_w, W_ALL)
            act.wait_ge(s_zero, 1)
            for c in range(DC):
                act.wait_ge(A.filled, c + 1)
                turned(("cT", c), A.banks[c]).then_inc(A.emptied, 1)
            act.wait_ge(A.emptied, 3 + DC)
            act.sem_inc(s_ct, 1)
            with act.Fori(0, B) as b:
                def max_copy(s):
                    act.wait_ge(s_mr, b * NS + s + 1)
                    for j in range(W):
                        h = keys_of(s, j)[1]
                        ins = nc.scalar.copy(QB[HALF:HALF + 1, query_slot(h), :], bank_m[32 * j:32 * j + 1, :])
                    ins.then_inc(s_mc, 1)

                for step in script:
                    kind = step[0]
                    if kind == "hi":
                        what = step[1:]
                        i = splits.index(what)
                        if what in rotated:
                            act.wait_ge(s_f, b * len(rotated) + rotated.index(what) + 1)
                        else:
                            src = (what[0],) + what[1:]
                            A.wait_filled(act, b, src)
                            if i >= 2:
                                act.wait_ge(s_lo, b * LO_PER + i - 1)
                            for e in range(2):
                                rows = slice(e * HALF, e * HALF + HALF)
                                out = A.bank(src)[rows, :]
                                scale = SCALE if what[0] == "q" else 1.0
                                if biased:
                                    ins = nc.scalar.activation(F[:, i % 2, e, :], out, ACT.Identity, scale=scale,
                                                               bias=bqk[rows, int(what[0] == "k"), what[1]:what[1] + 1])
                                else:
                                    ins = nc.scalar.mul(F[:, i % 2, e, :], out, scale)
                            ins.then_inc(A.emptied, 1)
                            A.wait_emptied(act, b, src)
                        for e in range(2):
                            u = 2 * what[1] + e
                            src = F[:, i % 2, e, :]
                            if what[0] == "k":
                                cols = slice(what[2] * S, what[2] * S + S)
                                nc.scalar.copy(KHI[0:HALF, unit_slot(u), cols], src)
                                ins = nc.scalar.copy(KHI[HALF:P, unit_slot(u), cols], src)
                            elif G == 1:
                                nc.scalar.copy(QA[0:HALF, query_slot(u), :], src)
                                ins = nc.scalar.copy(QB[0:HALF, query_slot(u), :], src)
                            else:
                                ins = nc.scalar.copy(QC[0:HALF, u, :].bitcast(F32R), src)
                        ins.then_inc(s_hi, 1)
                    elif kind == "v" and v_on_act:
                        A.wait_filled(act, b, step)
                        dst = V[:, step[1], :].rearrange("p (h v) -> p h v", v=VH)[:, :, 0:head_dim]
                        nc.scalar.copy(dst, A.bank(step)[:, 0:INNER].rearrange("p (h v) -> p h v", v=head_dim))\
                            .then_inc(A.emptied, 1)
                    elif kind == "cT":
                        A.wait_filled(act, b, step)
                        turned(step, A.bank(step)).then_inc(A.emptied, 1)
                        if step[1] == DC - 1:
                            A.wait_emptied(act, b, step)
                            act.sem_inc(s_ct, 1)
                    elif kind == "mr":
                        max_copy(step[1])
                    elif kind == "st":
                        s, n = step[1:]
                        i = s * NT + n
                        A.wait_filled(act, b, step)
                        if i >= NPT:
                            act.wait_ge(s_pv, b * PV_PER + (i - NPT) // W + 1)
                            if G == 1:
                                act.wait_ge(s_su, b * SU_PER + added(i - NPT))
                        nc.scalar.activation(PT[:, i % NPT, :], A.bank(step)[:, :], ACT.Exp).then_inc(A.emptied, 1)
                    elif kind == "oc" and G > 1:
                        act.wait_ge(s_pv, b * PV_PER + (step[1] + 1) * KC)
                        if step[1]:
                            Dv.wait_filled(act, b, ("sum", step[1] - 1))
                            act.wait_ge(s_at, b * NS + step[1])
                        nc.scalar.copy(OS[:, :], bank_o[step[1] % 2][:, :]).then_inc(s_os, 1)

        @block.vector
        def _(dve):
            pre_ch = Chain(dve, s_vch)
            if G > 1:
                nc.vector.memset(wo[:, :, :], 0.0).then_inc(s_pad, 1)
                nc.vector.memset(V[:, :, :], 1.0).then_inc(s_ones, 1)
            else:
                dve.sem_inc(s_pad, 1)
                nc.vector.memset(ones[:, :], 1.0).then_inc(s_ones, 1)
            dve.sem_inc(Dv.emptied, 2)
            if masked:
                dve.wait_ge(s_w, W_ALL)
                pre_ch.link(nc.vector.tensor_copy(PT[:, 0:T, :], mrow[:, :, :]))
                pre_ch.link(nc.vector.tensor_scalar(PT[:, 0:T, :], PT[:, 0:T, :], 0.0, None, ALU.not_equal))
                pre_ch.link(nc.vector.tensor_reduce(many[:, :], PT[:, 0:T, :], AX.X, ALU.max))
                pre_ch.link(nc.vector.tensor_scalar(PT[:, 0:T, :], PT[:, 0:T, :], -1.0, -MASKED, ALU.add, ALU.mult))
                for t in range(T):
                    ins = nc.vector.tensor_scalar(mbn[:, t, :], PT[:, t, :], many[:, t:t + 1], None, ALU.mult)
                    if t < T - 1:
                        pre_ch.link(ins)
                ins.then_inc(s_mk, 1)
                for kt in range(T):
                    dve.wait_ge(s_mkt, kt + 1)
                    nc.vector.tensor_copy(mbT[:, kt, :], Dv.banks[0][:, :]).then_inc(s_mk, 1)

            def norm_x(ch, src):
                layer_norm(nc, ch, src, lambda t: XN[:, t, :], st, keep=many[:, :] if masked else None)
                if norm_ctx:
                    layer_norm(nc, ch, lambda t: XN[:, t, :], lambda t: XN[:, t, :], st)
                dve.sem_inc(s_xn, 1)

            def norm_context(ch):
                layer_norm(nc, ch, lambda t: CN[:, t, :], lambda t: CN[:, t, :], st)
                dve.sem_inc(s_cl, 1)

            def turned(c, out):
                if norm_ctx:
                    return nc.vector.tensor_scalar(XT[:, c, :], out, gam[:, 4 + c:5 + c], gam[:, 6 + c:7 + c],
                                                   ALU.mult, ALU.add)
                return nc.vector.tensor_copy(XT[:, c, :], out)

            norm_x(pre_ch, lambda t: g.X[:, t * D:(t + 1) * D])
            if norm_ctx:
                dve.wait_ge(s_ctx, 16)
                norm_context(pre_ch)
            dve.wait_ge(s_w, W_ALL)
            dve.wait_ge(s_zero, 1)
            if out_bias:
                nc.vector.tensor_scalar(bob[:, :], bob[:, :], g.tg[:, gate:gate + 1], None, ALU.mult).then_inc(s_pad, 1)
            if biased:
                pre_ch.link(nc.vector.tensor_scalar(bqk[:, 0, :], bqk[:, 0, :], SCALE, None, ALU.mult))
            for c in range(DC):
                dve.wait_ge(Dv.filled, c + 1)
                turned(c, Dv.banks[c][:, :]).then_inc(Dv.emptied, 1)
            dve.wait_ge(Dv.emptied, 2 + DC)
            dve.sem_inc(s_xt, 1)
            per = (LN_STEPS * (3 if norm_ctx else 1) + int(masked) + 6 * len(rotated)
                   + (NS if KH == 2 else 0) + NS * 2 + (T if out_bias else 0))

            with dve.Fori(0, B) as b:
                ch = Chain(dve, s_vch, per, b, pre_ch.n)
                for step in script:
                    kind = step[0]
                    fill = stream(step) == "D"
                    if fill:
                        Dv.wait_filled(dve, b, step)
                        out = Dv.bank(step)
                    if kind == "xT":
                        turned(step[1], out[:, :]).then_inc(Dv.emptied, 1)
                        if step[1] == DC - 1:
                            Dv.wait_emptied(dve, b, step)
                            dve.sem_inc(s_xt, 1)
                    elif kind == "v" and fill:
                        dst = V[:, step[1], :].rearrange("p (h v) -> p h v", v=VH)[:, :, 0:head_dim]
                        src = out[:, 0:INNER].rearrange("p (h v) -> p h v", v=head_dim)
                        if biased:
                            ins = nc.vector.tensor_tensor(dst, src, bvb[:, :].rearrange("p (h v) -> p h v", v=head_dim),
                                                          ALU.add)
                        else:
                            ins = nc.vector.tensor_copy(dst, src)
                        ins.then_inc(Dv.emptied, 1)
                    elif kind in ("k", "kp", "q", "qp") and fill:
                        i = splits.index((kind[0],) + step[1:])
                        scale = SCALE if kind[0] == "q" else 1.0
                        if i >= 2 and len(kind) == 1:
                            dve.wait_ge(s_lo, b * LO_PER + i - 1)
                        for e in range(2):
                            rows = slice(e * HALF, e * HALF + HALF)
                            dst = F[:, i % 2, e, :]
                            if len(kind) == 1:
                                ch.step(nc.vector.scalar_tensor_tensor(dst, out[rows, :], scale, cos[rows, :],
                                                                       ALU.mult, ALU.mult))
                                if e == 1:
                                    ch.settle()
                                    dve.sem_inc(Dv.emptied, 1)
                            else:
                                ch.link(nc.vector.scalar_tensor_tensor(TMP[:, :], out[rows, :], scale, sin[rows, :],
                                                                       ALU.mult, ALU.mult))
                                ch.link(nc.vector.tensor_tensor(dst, dst, TMP[:, :], ALU.add))
                        if len(kind) == 2:
                            dve.sem_inc(Dv.emptied, 1)
                            dve.sem_inc(s_f, 1)
                    elif kind == "lo":
                        what = step[1:]
                        i = splits.index(what)
                        dve.wait_ge(s_hi, b * LO_PER + i + 1)
                        for e in range(2):
                            u = 2 * what[1] + e
                            full = F[:, i % 2, e, :]
                            if what[0] == "k":
                                cols = slice(what[2] * S, what[2] * S + S)
                                hi, lo = KHI[0:HALF, unit_slot(u), cols], KLO[0:HALF, unit_slot(u), cols]
                            elif G == 1:
                                hi, lo = QA[0:HALF, query_slot(u), :], QA[HALF:P, query_slot(u), :]
                            else:
                                hi, lo = QC[0:HALF, u, :], QC[HALF:P, u, :]
                            ins = nc.vector.tensor_tensor(lo, full, hi.bitcast(F32), ALU.subtract)
                        ins.then_inc(s_lo, 1)
                    elif kind == "mx":
                        s, k = step[1:]
                        if KH == 1:
                            ins = nc.vector.tensor_reduce(negm[:, k:k + 1], out[:, :], AX.X, ALU.max, negate=True)
                        else:
                            ins = nc.vector.tensor_reduce(mpart[:, k:k + 1], out[:, :], AX.X, ALU.max)
                        ins.then_inc(Dv.emptied, 1)
                        if k == NT - 1:
                            Dv.wait_emptied(dve, b, step)
                            if KH == 2:
                                ch.link(nc.vector.tensor_reduce(negm[:, :], mpart[:, :].rearrange("p (a h) -> p a h", h=KH),
                                                                AX.X, ALU.max, negate=True))
                            dve.sem_inc(s_nm, 1)
                    elif kind == "sum":
                        s = step[1]
                        ch.link(nc.vector.reciprocal(R[:, :], out[:, :]))
                        dve.sem_inc(Dv.emptied, 1)
                        if G == 1:
                            dve.wait_ge(s_pv, b * PV_PER + (s + 1) * KC)
                        src = OS[:, :] if G > 1 else bank_o[s % 2][:, :]
                        ch.link(nc.vector.tensor_tensor(AT[:, s, :], src, R[:, :], ALU.mult))
                        dve.sem_inc(s_at, 1)
                    elif kind == "ln":
                        norm_x(ch, lambda t: g.X[:, bass.ds(b * ROW + (ROW + t * D), D)])
                        if norm_ctx:
                            dve.wait_ge(s_ctx, b * 16 + 32)
                            norm_context(ch)
                    elif kind == "out":
                        row = g.X[:, bass.ds(b * ROW + step[1] * D, D)]
                        ins = nc.vector.scalar_tensor_tensor(row, out[:, 0:D], g.tg[:, gate:gate + 1], row,
                                                             ALU.mult, ALU.add)
                        if out_bias:
                            ch.link(ins)
                            ins = nc.vector.tensor_tensor(row, row, bob[:, :], ALU.add)
                        ins.then_inc(Dv.emptied, 1)
                ch.done()


class Banks:

    def __init__(self, g, banks, name, per):
        self.banks, self.per = banks, per
        self.filled, self.emptied = g.semaphore(name + "_filled"), g.semaphore(name + "_emptied")
        self.i = 0

    def grant(self, eng):
        eng.sem_inc(self.emptied, len(self.banks))

    def start(self, b):
        self.i, self.b = 0, b

    def to_fill(self, pe):
        n, i = len(self.banks), self.i
        self.i += 1
        pe.wait_ge(self.emptied, self.b * self.per + (i + 1 if self.per % n == 0 else max(i + 1, n)))
        return self.banks[i % n]

    def to_empty(self, eng):
        self.i += 1
        eng.wait_ge(self.filled, self.b * self.per + self.i)
        return self.banks[(self.i - 1) % len(self.banks)]

    def end(self):
        assert self.i == self.per, f"the fills of a turn are {self.i}"


def turn_to_columns(nc, pe, banks, XN, ident):
    for c in range(DC):
        out = banks.to_fill(pe)
        for t in range(T):
            last = pe.transpose(out[:, t * P:(t + 1) * P], XN[:, t, c * P:(c + 1) * P], ident)
        last.then_inc(banks.filled, 1)


def statistics(nc, g, ctx, pre):
    return {n: ctx.enter_context(nc.sbuf_tensor(pre + n, [P, w], F32))
            for n, w in (("six", 6 * T), ("mv", 2 * T), ("y", T), ("t", T))} | {"beat": g.semaphore(pre + "beat")}


def low_rank_ffn_stage(nc, g, dr):
    R1, FF = dr["L0_V1"].shape
    FC = FF // P
    with ExitStack() as ctx:
        def sb(name, shape, dt=F32):
            return ctx.enter_context(nc.sbuf_tensor("l0f_" + name, shape, dt))

        def sem(name):
            return g.semaphore("l0f_" + name)

        u1, v1 = sb("u1", [P, DC, R1]), sb("v1", [P, FF])
        u2, v2 = sb("u2", [P, FC, R1]), sb("v2", [P, D])
        b1 = sb("b1", [P, FC])
        XN, XT = sb("XN", [P, T, D]), sb("XT", [P, DC, S])
        LR, HR = sb("LR", [P, S]), sb("HR", [P, S])
        H = sb("H", [P, FC, S])
        st = statistics(nc, g, ctx, "l0f_")
        D_PER, A_PER = DC + 2 + T, FC
        dbanks = Banks(g, [ctx.enter_context(nc.psum_tensor(f"l0f_d{i}", [P, 512], F32)) for i in range(2)], "l0f_d", D_PER)
        abanks = Banks(g, [ctx.enter_context(nc.psum_tensor(f"l0f_a{i}", [P, 512], F32)) for i in range(4)], "l0f_a", A_PER)
        s_w, s_pad, s_v, s_xn = sem("weights"), sem("pads"), sem("chain"), sem("xn")
        loads = [(u1[:, :, :], dr["L0_U1"].rearrange("(c p) r -> p c r", p=P)), (v1[0:R1, :], dr["L0_V1"]),
                 (u2[:, :, :], dr["L0_U2"].rearrange("(c p) r -> p c r", p=P)), (v2[0:R1, :], dr["L0_V2"]),
                 (v2[R1:R1 + 1, :], dr["L0_b2"].rearrange("(o n) -> o n", o=1))]
        b1v = dr["L0_b1"].rearrange("(c p o) -> c p o", p=P, o=1)
        loads += [(b1[:, c:c + 1], b1v[c]) for c in range(FC)]
        W_ALL = 16 * len(loads)
        block = ctx.enter_context(nc.Block())

        @block.sync
        def _(sp):
            sp.wait_ge(s_pad, 2)
            for dst, src in loads:
                sp.dma_start(dst, src).then_inc(s_w, 16)

        @block.vector
        def _(dve):
            nc.vector.memset(v1[:, :], 0.0).then_inc(s_pad, 1)
            nc.vector.memset(v2[:, :], 0.0).then_inc(s_pad, 1)
            ch0 = Chain(dve, s_v)
            ch0.step(nc.vector.memset(LR[:, :], 0.0))
            ch0.link(nc.vector.memset(HR[:, :], 0.0))
            ch0.link(nc.vector.memset(HR[R1:R1 + 1, :], 1.0))
            dbanks.grant(dve)

            def norm(ch, b, off):
                layer_norm(nc, ch, off, lambda t: XN[:, t, :], st)
                dve.sem_inc(s_xn, 1)

            norm(ch0, 0, lambda t: g.X[:, t * D:(t + 1) * D])
            with dve.Fori(0, B) as b:
                ch = Chain(dve, s_v, LN_STEPS, b, ch0.n)
                dbanks.start(b)
                for c in range(DC):
                    nc.vector.tensor_copy(XT[:, c, :], dbanks.to_empty(dve)[:, :]).then_inc(dbanks.emptied, 1)
                nc.vector.tensor_copy(LR[0:R1, :], dbanks.to_empty(dve)[0:R1, :]).then_inc(dbanks.emptied, 1)
                norm(ch, b, lambda t: g.X[:, bass.ds(b * ROW + (ROW + t * D), D)])
                nc.vector.tensor_copy(HR[0:R1, :], dbanks.to_empty(dve)[0:R1, :]).then_inc(dbanks.emptied, 1)
                for t in range(T):
                    row = g.X[:, bass.ds(b * ROW + t * D, D)]
                    nc.vector.scalar_tensor_tensor(row, dbanks.to_empty(dve)[:, 0:D], g.tg[:, 4:5], row,
                                                   ALU.mult, ALU.add).then_inc(dbanks.emptied, 1)
                dbanks.end()
                ch.done()

        @block.scalar
        def _(act):
            abanks.grant(act)
            act.wait_ge(s_w, W_ALL)
            with act.Fori(0, B) as b:
                abanks.start(b)
                for f in range(FC):
                    nc.scalar.activation(H[:, f, :], abanks.to_empty(act)[:, :], ACT.Gelu_apprx_tanh,
                                         bias=b1[:, f:f + 1]).then_inc(abanks.emptied, 1)
                abanks.end()

        @block.tensor
        def _(pe):
            pe.wait_ge(s_w, W_ALL)
            with pe.Fori(0, B) as b:
                dbanks.start(b)
                abanks.start(b)
                pe.wait_ge(s_xn, b + 1)
                turn_to_columns(nc, pe, dbanks, XN, g.ident[:, :])
                out = dbanks.to_fill(pe)
                for c in range(DC):
                    pe.wait_ge(dbanks.emptied, b * D_PER + c + 3)
                    last = pe.matmul(out[0:R1, :], u1[:, c, :], XT[:, c, :], start=c == 0, stop=c == DC - 1)
                last.then_inc(dbanks.filled, 1)
                pe.wait_ge(dbanks.emptied, b * D_PER + DC + 3)
                for f in range(FC):
                    pe.matmul(abanks.to_fill(pe)[:, :], v1[:, f * P:(f + 1) * P], LR[:, :],
                              start=True, stop=True).then_inc(abanks.filled, 1)
                out = dbanks.to_fill(pe)
                for f in range(FC):
                    pe.wait_ge(abanks.emptied, b * A_PER + f + 5)
                    last = pe.matmul(out[0:R1, :], u2[:, f, :], H[:, f, :], start=f == 0, stop=f == FC - 1)
                last.then_inc(dbanks.filled, 1)
                pe.wait_ge(dbanks.emptied, b * D_PER + DC + 4)
                for t in range(T):
                    pe.matmul(dbanks.to_fill(pe)[:, 0:D], HR[:, t * P:(t + 1) * P], v2[:, :],
                              start=True, stop=True).then_inc(dbanks.filled, 1)


TOP2_STEPS = 5 * T + 8


def top2_gates(nc, dve, ch, E, logits, bias, tg, tk, ask_exp, got_exp, emptied):
    L, M8, I8, IF, C = tk["L"], tk["M8"], tk["I8"], tk["IF"], tk["C"]
    for t in range(T):
        ch.step(nc.vector.tensor_tensor(L[:, 8 * t:8 * t + E], logits[:, t * E:(t + 1) * E], bias, ALU.add))
    ch.settle()
    dve.sem_inc(emptied, 1)
    for t in range(T):
        ch.step(nc.vector.max(M8[:, 8 * t:8 * t + 8], L[:, 8 * t:8 * t + 8]))
    ch.settle()
    m = M8[:, :].rearrange("p (t k) -> p t k", k=8)
    ch.link(nc.vector.tensor_tensor(tk["d"][:, :], m[:, :, 1], m[:, :, 0], ALU.subtract))
    dve.sem_inc(ask_exp, 1)
    for t in range(T):
        ch.step(nc.vector.max_index(I8[:, 8 * t:8 * t + 8], M8[:, 8 * t:8 * t + 8], L[:, 8 * t:8 * t + 8]))
    ch.settle()
    ch.link(nc.vector.tensor_copy(IF[:, :], I8[:, :]))
    got_exp()
    w0, w1, e = tk["w0"], tk["w1"], tk["e"]
    ch.link(nc.vector.tensor_scalar(w0[:, :], e[:, :], 1.0, None, ALU.add))
    ch.link(nc.vector.reciprocal(w0[:, :], w0[:, :]))
    ch.link(nc.vector.tensor_tensor(w1[:, :], e[:, :], w0[:, :], ALU.mult))
    ch.link(nc.vector.tensor_scalar(w0[:, :], w0[:, :], tg, None, ALU.mult))
    ch.link(nc.vector.tensor_scalar(w1[:, :], w1[:, :], tg, None, ALU.mult))
    for t in range(T):
        ch.step(nc.vector.tensor_scalar(C[:, t, :], tk["iota"][:, 0:E], IF[:, 8 * t:8 * t + 1], w0[:, t:t + 1],
                                        ALU.is_equal, ALU.mult))
        ch.step(nc.vector.tensor_scalar(tk["C2"][:, t, :], tk["iota"][:, 0:E], IF[:, 8 * t + 1:8 * t + 2],
                                        w1[:, t:t + 1], ALU.is_equal, ALU.mult))
    ch.settle()
    ch.link(nc.vector.tensor_tensor(C[:, :, :], C[:, :, :], tk["C2"][:, :, :], ALU.add))


def top2_buffers(nc, ctx, pre, E):
    def sb(name, shape, dt=F32):
        return ctx.enter_context(nc.sbuf_tensor(pre + name, shape, dt))
    return {"L": sb("L", [P, 8 * T]), "M8": sb("M8", [P, 8 * T]), "I8": sb("I8", [P, 8 * T], mybir.dt.uint32),
            "IF": sb("IF", [P, 8 * T]), "C": sb("C", [P, T, E]), "C2": sb("C2", [P, T, E]), "d": sb("d", [P, T]),
            "e": sb("e", [P, T]), "w0": sb("gate0", [P, T]), "w1": sb("gate1", [P, T]), "iota": sb("iota", [P, 8])}


def top2_gelu_stage(nc, g, dr):
    E, _, HID = dr["L2_W1"].shape
    HC = HID // P
    with ExitStack() as ctx:
        def sb(name, shape, dt=F32):
            return ctx.enter_context(nc.sbuf_tensor("l2f_" + name, shape, dt))

        def sem(name):
            return g.semaphore("l2f_" + name)

        wg, bg = sb("wg", [P, DC, E]), sb("bg", [P, E])
        w1, w2 = sb("w1", [P, E, DC, HID]), sb("w2", [P, E, HC, D])
        b1, b2 = sb("b1", [P, E, HC]), sb("b2", [P, E, D])
        XN, XT = sb("XN", [P, T, D]), sb("XT", [P, DC, S])
        H = sb("H", [P, 2, HC, S])
        st = statistics(nc, g, ctx, "l2f_")
        tk = top2_buffers(nc, ctx, "l2f_", E)
        D_PER, A_PER = DC + 1 + E * 2, E * HC
        dbanks = Banks(g, [ctx.enter_context(nc.psum_tensor(f"l2f_d{i}", [P, 512], F32)) for i in range(3)], "l2f_d", D_PER)
        abanks = Banks(g, [ctx.enter_context(nc.psum_tensor(f"l2f_a{i}", [P, 512], F32)) for i in range(4)], "l2f_a", A_PER)
        s_w, s_v, s_xn = sem("weights"), sem("chain"), sem("xn")
        s_diff, s_exp = sem("diff"), sem("exp")
        loads = [(wg[:, :, :], dr["L2_Wg"].rearrange("(c p) e -> p c e", p=P)),
                 (bg[:, :], dr["L2_bg"].rearrange("(o e) -> o e", o=1).to_broadcast([P, E])),
                 (tk["iota"][:, :], dr["iota8"])]
        for e in range(E):
            loads += [(w1[:, e, :, :], dr["L2_W1"][e].rearrange("(c p) h -> p c h", p=P)),
                      (w2[:, e, :, :], dr["L2_W2"][e].rearrange("(c p) d -> p c d", p=P)),
                      (b2[:, e, :], dr["L2_b2"][e:e + 1, :].to_broadcast([P, D]))]
            loads += [(b1[:, e, c:c + 1], dr["L2_b1"][e].rearrange("(c p o) -> c p o", p=P, o=1)[c]) for c in range(HC)]
        W_ALL = 16 * len(loads)
        block = ctx.enter_context(nc.Block())

        @block.sync
        def _(sp):
            for dst, src in loads:
                sp.dma_start(dst, src).then_inc(s_w, 16)

        @block.vector
        def _(dve):
            ch0 = Chain(dve, s_v)
            ch0.link(nc.vector.memset(tk["L"][:, :], -3e38))
            dbanks.grant(dve)

            def norm(ch, off):
                layer_norm(nc, ch, off, lambda t: XN[:, t, :], st)
                dve.sem_inc(s_xn, 1)

            norm(ch0, lambda t: g.X[:, t * D:(t + 1) * D])
            dve.wait_ge(s_w, W_ALL)
            with dve.Fori(0, B) as b:
                ch = Chain(dve, s_v, TOP2_STEPS + LN_STEPS + 2 * E * T, b, ch0.n)
                dbanks.start(b)
                for c in range(DC):
                    nc.vector.tensor_copy(XT[:, c, :], dbanks.to_empty(dve)[:, :]).then_inc(dbanks.emptied, 1)
                logits = dbanks.to_empty(dve)
                top2_gates(nc, dve, ch, E, logits, bg[:, :], g.tg[:, 6:7], tk, s_diff,
                           lambda: dve.wait_ge(s_exp, b + 1), dbanks.emptied)
                rows = [g.X[:, bass.ds(b * ROW + t * D, D)] for t in range(T)]
                for e in range(E):
                    for t in range(T):
                        ch.step(nc.vector.scalar_tensor_tensor(rows[t], b2[:, e, :], tk["C"][:, t, e:e + 1], rows[t],
                                                               ALU.mult, ALU.add))
                    if e == 1:
                        norm(ch, lambda t: g.X[:, bass.ds(b * ROW + (ROW + t * D), D)])
                    ch.settle()
                    for t in range(T):
                        if t % 2 == 0:
                            out = dbanks.to_empty(dve)
                        ch.step(nc.vector.scalar_tensor_tensor(rows[t], out[:, (t % 2) * D:(t % 2) * D + D],
                                                               tk["C"][:, t, e:e + 1], rows[t], ALU.mult, ALU.add))
                        if t % 2:
                            ch.settle()
                            dve.sem_inc(dbanks.emptied, 1)
                dbanks.end()
                ch.done()

        @block.scalar
        def _(act):
            abanks.grant(act)
            act.wait_ge(s_w, W_ALL)
            with act.Fori(0, B) as b:
                abanks.start(b)
                act.wait_ge(s_diff, b + 1)
                nc.scalar.activation(tk["e"][:, :], tk["d"][:, :], ACT.Exp).then_inc(s_exp, 1)
                for e in range(E):
                    for c in range(HC):
                        out = abanks.to_empty(act)
                        if e >= 2 and c == 0:
                            act.wait_ge(dbanks.filled, b * D_PER + DC + 1 + 2 * (e - 1))
                        nc.scalar.activation(H[:, e % 2, c, :], out[:, :], ACT.Gelu,
                                             bias=b1[:, e, c:c + 1]).then_inc(abanks.emptied, 1)
                abanks.end()

        @block.tensor
        def _(pe):
            pe.wait_ge(s_w, W_ALL)
            with pe.Fori(0, B) as b:
                dbanks.start(b)
                abanks.start(b)
                pe.wait_ge(s_xn, b + 1)
                turn_to_columns(nc, pe, dbanks, XN, g.ident[:, :])
                pe.wait_ge(dbanks.emptied, b * D_PER + DC + 3)
                out = dbanks.to_fill(pe)
                for t in range(T):
                    for c in range(DC):
                        last = pe.matmul(out[:, t * E:(t + 1) * E], XT[:, c, t * P:(t + 1) * P], wg[:, c, :],
                                         start=c == 0, stop=c == DC - 1)
                last.then_inc(dbanks.filled, 1)
                for e in range(E + 1):
                    if e < E:
                        for h in range(HC):
                            out = abanks.to_fill(pe)
                            for c in range(DC):
                                last = pe.matmul(out[:, :], w1[:, e, c, h * P:(h + 1) * P], XT[:, c, :],
                                                 start=c == 0, stop=c == DC - 1)
                            last.then_inc(abanks.filled, 1)
                    if e >= 1:
                        f = e - 1
                        pe.wait_ge(abanks.emptied, b * A_PER + (f + 1) * HC + 4)
                        for t in range(T):
                            if t % 2 == 0:
                                out = dbanks.to_fill(pe)
                            for c in range(HC):
                                last = pe.matmul(out[:, (t % 2) * D:(t % 2) * D + D], H[:, f % 2, c, t * P:(t + 1) * P],
                                                 w2[:, f, c, :], start=c == 0, stop=c == HC - 1,
                                                 skip_group_check=True)
                            if t % 2:
                                last.then_inc(dbanks.filled, 1)
                dbanks.end()


def top2_silu_stage(nc, g, dr):
    E, _, HID = dr["L3_routed_w1"].shape
    SH = dr["L3_shared_w1"].shape[0]
    EA = E + SH
    assert HID == P
    with ExitStack() as ctx:
        def sb(name, shape, dt=F32):
            return ctx.enter_context(nc.sbuf_tensor("l3f_" + name, shape, dt))

        def sem(name):
            return g.semaphore("l3f_" + name)

        wg, bg = sb("wg", [P, DC, E]), sb("bg", [P, E])
        w1, w3, w2 = sb("w1", [P, EA, DC, HID]), sb("w3", [P, EA, DC, HID]), sb("w2", [P, EA, D])
        XN, XT = sb("XN", [P, T, D]), sb("XT", [P, DC, S])
        SG, H = sb("SG", [P, 2, S]), sb("H", [P, 3, S])
        st = statistics(nc, g, ctx, "l3f_")
        tk = top2_buffers(nc, ctx, "l3f_", E)
        D_PER, A_PER = DC + 1 + EA + (E + 1) * 2, EA
        dbanks = Banks(g, [ctx.enter_context(nc.psum_tensor(f"l3f_d{i}", [P, 512], F32)) for i in range(4)], "l3f_d", D_PER)
        abanks = Banks(g, [ctx.enter_context(nc.psum_tensor(f"l3f_a{i}", [P, 512], F32)) for i in range(2)], "l3f_a", A_PER)
        s_w, s_v, s_xn = sem("weights"), sem("chain"), sem("xn")
        s_diff, s_exp = sem("diff"), sem("exp")
        loads = [(wg[:, :, :], dr["L3_router_w"].rearrange("(c p) e -> p c e", p=P)),
                 (bg[:, :], dr["L3_router_b"].rearrange("(o e) -> o e", o=1).to_broadcast([P, E])),
                 (tk["iota"][:, :], dr["iota8"])]
        for n, w in (("w1", w1), ("w3", w3)):
            for e in range(EA):
                src = dr[f"L3_routed_{n}"][e] if e < E else dr[f"L3_shared_{n}"][e - E]
                loads += [(w[:, e, :, :], src.rearrange("(c p) h -> p c h", p=P))]
        loads += [(w2[:, 0:E, :], dr["L3_routed_w2"].rearrange("e h d -> h e d")),
                  (w2[:, E:EA, :], dr["L3_shared_w2"].rearrange("e h d -> h e d"))]
        W_ALL = 16 * len(loads)
        block = ctx.enter_context(nc.Block())
        def h_at(e):
            return DC + 1 + 1 + e + 2 * min(max(e - 1, 0), E)

        out_turns = [[e] for e in range(E)] + [list(range(E, EA))]

        @block.sync
        def _(sp):
            for dst, src in loads:
                sp.dma_start(dst, src).then_inc(s_w, 16)

        @block.vector
        def _(dve):
            ch0 = Chain(dve, s_v)
            ch0.link(nc.vector.memset(tk["L"][:, :], -3e38))
            dbanks.grant(dve)

            def norm(ch, off):
                layer_norm(nc, ch, off, lambda t: XN[:, t, :], st)
                dve.sem_inc(s_xn, 1)

            norm(ch0, lambda t: g.X[:, t * D:(t + 1) * D])
            dve.wait_ge(s_w, W_ALL)
            with dve.Fori(0, B) as b:
                ch = Chain(dve, s_v, TOP2_STEPS + LN_STEPS + (E + 1) * T, b, ch0.n)
                dbanks.start(b)
                for c in range(DC):
                    nc.vector.tensor_copy(XT[:, c, :], dbanks.to_empty(dve)[:, :]).then_inc(dbanks.emptied, 1)
                logits = dbanks.to_empty(dve)
                top2_gates(nc, dve, ch, E, logits, bg[:, :], g.tg[:, 7:8], tk, s_diff,
                           lambda: dve.wait_ge(s_exp, b + 1), dbanks.emptied)
                rows = [g.X[:, bass.ds(b * ROW + t * D, D)] for t in range(T)]

                def product(e):
                    out = dbanks.to_empty(dve)
                    dve.wait_ge(abanks.emptied, b * A_PER + e + 1 + 2)
                    nc.vector.tensor_tensor(H[:, e % 3, :], out[:, :], SG[:, e % 2, :],
                                            ALU.mult).then_inc(dbanks.emptied, 1)

                def add(turn):
                    e = turn[0]
                    for t in range(T):
                        if t % 2 == 0:
                            out = dbanks.to_empty(dve)
                        gate = tk["C"][:, t, e:e + 1] if e < E else g.tg[:, 7:8]
                        ch.step(nc.vector.scalar_tensor_tensor(rows[t], out[:, (t % 2) * D:(t % 2) * D + D], gate,
                                                               rows[t], ALU.mult, ALU.add))
                        if t % 2:
                            ch.settle()
                            dve.sem_inc(dbanks.emptied, 1)

                for e in range(EA):
                    product(e)
                    if 1 <= e <= E:
                        add(out_turns[e - 1])
                    if e == 2:
                        norm(ch, lambda t: g.X[:, bass.ds(b * ROW + (ROW + t * D), D)])
                add(out_turns[E])
                dbanks.end()
                ch.done()

        @block.scalar
        def _(act):
            abanks.grant(act)
            with act.Fori(0, B) as b:
                abanks.start(b)
                act.wait_ge(s_diff, b + 1)
                nc.scalar.activation(tk["e"][:, :], tk["d"][:, :], ACT.Exp).then_inc(s_exp, 1)
                for e in range(EA):
                    out = abanks.to_empty(act)
                    if e >= 2:
                        act.wait_ge(dbanks.emptied, b * D_PER + 4 + h_at(e - 2))
                    nc.scalar.activation(SG[:, e % 2, :], out[:, :], ACT.Silu).then_inc(abanks.emptied, 1)
                abanks.end()

        @block.tensor
        def _(pe):
            pe.wait_ge(s_w, W_ALL)
            with pe.Fori(0, B) as b:
                dbanks.start(b)
                abanks.start(b)
                pe.wait_ge(s_xn, b + 1)
                turn_to_columns(nc, pe, dbanks, XN, g.ident[:, :])
                pe.wait_ge(dbanks.emptied, b * D_PER + DC + 4)
                out = dbanks.to_fill(pe)
                for t in range(T):
                    for c in range(DC):
                        last = pe.matmul(out[:, t * E:(t + 1) * E], XT[:, c, t * P:(t + 1) * P], wg[:, c, :],
                                         start=c == 0, stop=c == DC - 1)
                last.then_inc(dbanks.filled, 1)

                def expert_in(e):
                    for w, banks in ((w1, abanks), (w3, dbanks)):
                        out = banks.to_fill(pe)
                        for c in range(DC):
                            last = pe.matmul(out[:, :], w[:, e, c, :], XT[:, c, :], start=c == 0, stop=c == DC - 1)
                        last.then_inc(banks.filled, 1)

                def expert_out(turn):
                    pe.wait_ge(dbanks.emptied, b * D_PER + 4 + h_at(turn[-1]))
                    for t in range(T):
                        if t % 2 == 0:
                            out = dbanks.to_fill(pe)
                        for e in turn:
                            last = pe.matmul(out[:, (t % 2) * D:(t % 2) * D + D], H[:, e % 3, t * P:(t + 1) * P],
                                             w2[:, e, :], start=e == turn[0], stop=e == turn[-1], skip_group_check=True)
                        if t % 2:
                            last.then_inc(dbanks.filled, 1)

                for e in range(EA):
                    expert_in(e)
                    if 1 <= e <= E:
                        expert_out(out_turns[e - 1])
                expert_out(out_turns[E])
                dbanks.end()


def soft_moe_stage(nc, g, dr):
    NE, _, HO = dr["L1_expert_w"].shape
    SL = dr["L1_phiT"].shape[1]
    NP = SL // NE
    SC = SL // P
    EC = P // NP
    QW = 512
    assert HO == D
    with ExitStack() as outer:
        def keep(name, shape, dt=F32):
            return outer.enter_context(nc.sbuf_tensor("l1f_" + name, shape, dt))

        phi = keep("phi", [P, DC, SL])
        biasb = keep("biasb", [P, SL], BF16)
        onesb = keep("onesb", [P, P], BF16)
        zeros = keep("zeros", [P, QW], BF16)
        XS = keep("XS", [P, SC, D])
        XN = keep("XN", [P, T, D])
        XT = keep("XT", [P, DC, S])
        st = statistics(nc, g, outer, "l1f_")

        def logits_of(pe, out, t, q):
            for c in range(DC):
                pe.matmul(out, XT[:, c, t * P:(t + 1) * P], phi[:, c, q * QW:(q + 1) * QW], start=c == 0, stop=False)
            return pe.matmul(out, onesb[:, :], biasb[:, q * QW:(q + 1) * QW], start=False, stop=True)

        with ExitStack() as ctx:
            def sb(name, shape, dt=F32):
                return ctx.enter_context(nc.sbuf_tensor("l1a_" + name, shape, dt))

            def sem(name):
                return g.semaphore("l1a_" + name)

            brow, part = sb("brow", [1, SL]), sb("part", [1, SL], BF16)
            XG = sb("XG", [P, T, D])
            LC, DW = sb("LC", [P, 3, QW]), sb("DW", [P, 2, QW])
            m, r = sb("m", [P, QW // NP]), sb("r", [P, 2, QW // NP])
            TILES = T * 2
            D_PER = DC + TILES
            dbanks = Banks(g, [ctx.enter_context(nc.psum_tensor(f"l1a_d{i}", [P, 512], F32)) for i in range(4)], "l1a_d", D_PER)
            acc = ctx.enter_context(nc.psum_tensor("l1a_acc", [P, 4, 512], F32))
            s_w, s_v, s_xn, s_xg = sem("weights"), sem("chain"), sem("xn"), sem("xg")
            s_bias = sem("bias")
            s_sub, s_exp, s_sum, s_dw, s_use = sem("shifted"), sem("exp"), sem("sums"), sem("weights_d"), sem("used")
            s_zero, s_acc, s_out, s_beat = sem("acc_zero"), sem("acc_full"), sem("acc_out"), sem("beat2")
            ngroup = QW // NP
            block = ctx.enter_context(nc.Block())

            @block.sync
            def _(sp):
                sp.dma_start(brow[0:1, :], dr["L1_phi_b"].rearrange("(o n) -> o n", o=1)).then_inc(s_w, 16)
                sp.dma_start(phi[:, :, :], dr["L1_phiT"].rearrange("(c p) n -> p c n", p=P)).then_inc(s_w, 16)

            @block.vector
            def _(dve):
                ch0 = Chain(dve, s_v)
                ch0.step(nc.vector.memset(zeros[:, :], 0.0))
                ch0.step(nc.vector.memset(onesb[:, :], 1.0))
                ch0.link(nc.vector.memset(biasb[:, :], 0.0))
                dbanks.grant(dve)
                dve.wait_ge(s_w, 32)
                for k, row in enumerate((0, 32, 64)):
                    ch0.link(nc.vector.tensor_copy(part[:, :], brow[:, :]))
                    ch0.link(nc.vector.tensor_copy(biasb[row:row + 1, :], part[:, :]))
                    ch0.link(nc.vector.tensor_tensor(brow[:, :], brow[:, :], part[:, :], ALU.subtract))

                def norm(ch, off):
                    layer_norm(nc, ch, off, lambda t: XN[:, t, :], st)
                    dve.sem_inc(s_xn, 1)

                dve.sem_inc(s_bias, 1)
                for half in range(2):
                    if half:
                        dve.wait_ge(s_xg, B)
                    chh = Chain(dve, s_v, 0, None)
                    chh.n = ch0.n
                    norm(chh, lambda t: g.X[:, t * D:(t + 1) * D])
                    ch0.n = chh.n
                    per = LN_STEPS + 3 * TILES
                    with dve.Fori(0, B) as b:
                        ch = Chain(dve, s_v, per, b, ch0.n)
                        hb = b + half * B
                        dbanks.start(hb)
                        for c in range(DC):
                            nc.vector.tensor_copy(XT[:, c, :], dbanks.to_empty(dve)[:, :]).then_inc(dbanks.emptied, 1)

                        def total(k):
                            dve.wait_ge(s_dw, hb * TILES + k + 2)
                            dve.wait_ge(s_exp, hb * TILES + k + 1)
                            ch.link(nc.vector.tensor_reduce(r[:, k % 2, :], LC[:, k % 3, :].rearrange("p (n q) -> p n q", q=NP),
                                                            AX.X, ALU.add))
                            nc.vector.reciprocal(r[:, k % 2, :], r[:, k % 2, :]).then_inc(s_sum, 1)

                        for k in range(TILES):
                            out = dbanks.to_empty(dve)[:, :].rearrange("p (n q) -> p n q", q=NP)
                            ch.link(nc.vector.tensor_reduce(m[:, :], out, AX.X, ALU.max))
                            dve.wait_ge(s_dw, hb * TILES + k + 1)
                            ch.link(nc.vector.tensor_tensor(LC[:, k % 3, :].rearrange("p (n q) -> p n q", q=NP), out,
                                                            m[:, :].unsqueeze(2).to_broadcast([P, ngroup, NP]), ALU.subtract))
                            dve.sem_inc(dbanks.emptied, 1)
                            dve.sem_inc(s_sub, 1)
                            if k >= 1:
                                total(k - 1)
                            if k == 3:
                                dve.wait_ge(s_xg, hb + 1)
                                norm(ch, lambda t: g.X[:, bass.ds(b * ROW + (ROW + t * D), D)])
                        total(TILES - 1)
                        dbanks.end()
                        ch.done()
                    ch0.n += B * per
                    dve.sem_inc(s_beat, 1)
                    dve.wait_ge(s_acc, half + 1)
                    for i in range(4):
                        ins = nc.vector.tensor_copy(XS[:, half * 8 + 2 * i:half * 8 + 2 * i + 2, :],
                                                    acc[:, i, :].rearrange("p (a d) -> p a d", a=2))
                    ins.then_inc(s_out, 1)

            @block.scalar
            def _(act):
                for half in range(2):
                    with act.Fori(0, B) as b:
                        hb = b + half * B
                        act.wait_ge(s_xn, b + (half * (B + 1) + 1))
                        act.wait_ge(s_use, hb * TILES + 2)
                        nc.scalar.copy(XG[:, :, :], XN[:, :, :]).then_inc(s_xg, 1)
                        for k in range(TILES):
                            act.wait_ge(s_sub, hb * TILES + k + 1)
                            nc.scalar.activation(LC[:, k % 3, :], LC[:, k % 3, :], ACT.Exp).then_inc(s_exp, 1)

            @block.gpsimd
            def _(pool):
                pool.sem_inc(s_dw, 3)
                for half in range(2):
                    with pool.Fori(0, B) as b:
                        hb = b + half * B
                        for k in range(TILES):
                            pool.wait_ge(s_sum, hb * TILES + k + 1)
                            pool.wait_ge(s_use, hb * TILES + k + 1)
                            nc.gpsimd.tensor_tensor(DW[:, k % 2, :].rearrange("p (n q) -> p n q", q=NP),
                                                    LC[:, k % 3, :].rearrange("p (n q) -> p n q", q=NP),
                                                    r[:, k % 2, :].unsqueeze(2).to_broadcast([P, ngroup, NP]),
                                                    ALU.mult).then_inc(s_dw, 1)

            @block.tensor
            def _(pe):
                pe.sem_inc(s_use, 2)
                pe.wait_ge(s_w, 32)
                pe.wait_ge(s_bias, 1)
                for half in range(2):
                    if half:
                        pe.wait_ge(s_out, 1)
                    pe.wait_ge(s_xn, half * (B + 1) + 1)
                    for i in range(4):
                        pe.matmul(acc[:, i, :], zeros[:, 0:P], zeros[:, :], start=True, stop=False, skip_group_check=True)
                    with pe.Fori(0, B) as b:
                        hb = b + half * B
                        dbanks.start(hb)
                        pe.wait_ge(s_xn, b + (half * (B + 1) + 1))
                        turn_to_columns(nc, pe, dbanks, XN, g.ident[:, :])
                        pe.wait_ge(dbanks.emptied, hb * D_PER + DC + 4)

                        def gather(k):
                            t, q = k // 2, k % 2
                            pe.wait_ge(s_dw, hb * TILES + k + 4)
                            if k == 0:
                                pe.wait_ge(s_xg, hb + 1)
                            for j in range(4):
                                i = q * 4 + j
                                last = pe.matmul(acc[:, i // 2, (i % 2) * D:(i % 2) * D + D], DW[:, k % 2, j * P:(j + 1) * P],
                                                 XG[:, t, :], start=False, stop=False, skip_group_check=True)
                            last.then_inc(s_use, 1)

                        for k in range(TILES + 3):
                            if k < TILES:
                                logits_of(pe, dbanks.to_fill(pe)[:, :], k // 2, half * 2 + k % 2).then_inc(dbanks.filled, 1)
                            if k >= 3:
                                gather(k - 3)
                        dbanks.end()
                    pe.matmul(acc[:, 3, :], zeros[:, 0:P], zeros[:, :], start=False, stop=True,
                              skip_group_check=True).then_inc(s_acc, 1)

        with ExitStack() as ctx:
            def sb(name, shape, dt=F32):
                return ctx.enter_context(nc.sbuf_tensor("l1b_" + name, shape, dt))

            def sem(name):
                return g.semaphore("l1b_" + name)

            TURNS = SC // T
            EW = sb("EW", [P, T, EC * DC, HO])
            EB = sb("EB", [P, T, HO])
            ZT = sb("ZT", [P, DC, S])
            dbanks = Banks(g, [ctx.enter_context(nc.psum_tensor(f"l1b_d{i}", [P, 512], F32)) for i in range(4)], "l1b_d", DC + T)
            s_ew, s_eb, s_v, s_xn = [sem(f"experts{t}") for t in range(T)], sem("bias"), sem("chain"), sem("slots")
            s_th = sem("tanh")
            eb = dr["L1_expert_b"]
            block = ctx.enter_context(nc.Block())

            @block.sync
            def _(sp):
                def load(n, t):
                    sp.dma_start(EW[:, t, :, :], n).then_inc(s_ew[t], 16)

                ew_rows = dr["L1_expert_w"].rearrange("n (c p) h -> p (n c) h", p=P)
                for t in range(T):
                    load(ew_rows[:, t * EC * DC:(t + 1) * EC * DC, :], t)
                for t in range(T):
                    for e in range(EC):
                        n = t * EC + e
                        sp.dma_start(EB[e * NP:(e + 1) * NP, t, :], eb[n:n + 1, :].to_broadcast([NP, HO])).then_inc(s_eb, 16)
                with sp.Fori(1, TURNS) as i:
                    for t in range(T):
                        sp.wait_ge(dbanks.filled, i * (DC + T) + (t + 1 + DC - (DC + T)))
                        load(ew_rows[:, bass.ds(i * (T * EC * DC) + t * EC * DC, EC * DC), :], t)
                    for t in range(T):
                        sp.wait_ge(dbanks.emptied, i * (DC + T) + 4)
                        for e in range(EC):
                            sp.dma_start(EB[e * NP:(e + 1) * NP, t, :],
                                         eb[bass.ds(i * (T * EC) + (t * EC + e), 1), :].to_broadcast([NP, HO])).then_inc(s_eb, 16)

            @block.vector
            def _(dve):
                dbanks.grant(dve)
                with dve.Fori(0, TURNS) as i:
                    ch = Chain(dve, s_v, LN_STEPS + T, i)
                    dbanks.start(i)
                    rows = [XS[:, :, :].rearrange("p s d -> p (s d)")[:, bass.ds(i * ROW + t * D, D)] for t in range(T)]
                    for t in range(T):
                        ch.step(nc.vector.tensor_scalar(rows[t], rows[t], -33000.0, 65000.0, ALU.max, ALU.min))
                    ch.settle()
                    layer_norm(nc, ch, lambda t: rows[t], lambda t: XN[:, t, :], st)
                    dve.sem_inc(s_xn, 1)
                    for c in range(DC):
                        nc.vector.tensor_copy(ZT[:, c, :], dbanks.to_empty(dve)[:, :]).then_inc(dbanks.emptied, 1)
                    dve.wait_ge(s_eb, i * (16 * T * EC) + 16 * T * EC)
                    for t in range(T):
                        nc.vector.tensor_tensor(rows[t], dbanks.to_empty(dve)[:, 0:HO], EB[:, t, :],
                                                ALU.add).then_inc(dbanks.emptied, 1)
                    dbanks.end()
                    ch.done()

            @block.scalar
            def _(act):
                with act.Fori(0, TURNS) as i:
                    act.wait_ge(s_xn, i + 1)
                    nc.scalar.activation(XN[:, :, :], XN[:, :, :], ACT.Tanh).then_inc(s_th, 1)

            @block.tensor
            def _(pe):
                with pe.Fori(0, TURNS) as i:
                    dbanks.start(i)
                    pe.wait_ge(s_th, i + 1)
                    turn_to_columns(nc, pe, dbanks, XN, g.ident[:, :])
                    pe.wait_ge(dbanks.emptied, i * (DC + T) + DC + 4)
                    for t in range(T):
                        pe.wait_ge(s_ew[t], i * 16 + 16)
                        out = dbanks.to_fill(pe)
                        for e in range(EC):
                            for c in range(DC):
                                last = pe.matmul(out[e * NP:(e + 1) * NP, 0:HO],
                                                 ZT[:, c, t * P + e * NP:t * P + (e + 1) * NP], EW[:, t, e * DC + c, :],
                                                 start=c == 0, stop=c == DC - 1)
                        last.then_inc(dbanks.filled, 1)
                    dbanks.end()

        with ExitStack() as ctx:
            def sb(name, shape, dt=F32):
                return ctx.enter_context(nc.sbuf_tensor("l1c_" + name, shape, dt))

            def sem(name):
                return g.semaphore("l1c_" + name)

            QB4 = SL // QW
            LC, CW = sb("LC", [P, 2, SL]), sb("CW", [P, SL])
            CT = sb("CT", [P, 2, SC, P])
            m, r = sb("m", [P, NP]), sb("r", [P, NP])
            lg = ctx.enter_context(nc.psum_tensor("l1c_lg", [P, SL], F32))
            D_PER, A_PER = DC + T, T * QB4
            dbanks = Banks(g, [ctx.enter_context(nc.psum_tensor(f"l1c_d{i}", [P, 512], F32)) for i in range(2)], "l1c_d", D_PER)
            abanks = Banks(g, [ctx.enter_context(nc.psum_tensor(f"l1c_a{i}", [P, 512], F32)) for i in range(2)], "l1c_a", A_PER)
            s_v, s_xn, s_lg = sem("chain"), sem("xn"), sem("logits")
            s_sub, s_exp, s_rec, s_cw = sem("shifted"), sem("exp"), sem("inverse"), sem("combine")
            block = ctx.enter_context(nc.Block())

            def by_slot(ap):
                return ap.rearrange("p (n q) -> p q n", q=NP)

            @block.vector
            def _(dve):
                dbanks.grant(dve)
                dve.sem_inc(s_sub, 1)

                def norm(ch, off):
                    layer_norm(nc, ch, off, lambda t: XN[:, t, :], st)
                    dve.sem_inc(s_xn, 1)

                ch0 = Chain(dve, s_v)
                norm(ch0, lambda t: g.X[:, t * D:(t + 1) * D])
                with dve.Fori(0, B) as b:
                    ch = Chain(dve, s_v, LN_STEPS + 3 * T, b, ch0.n)
                    dbanks.start(b)
                    for c in range(DC):
                        nc.vector.tensor_copy(XT[:, c, :], dbanks.to_empty(dve)[:, :]).then_inc(dbanks.emptied, 1)

                    def add(t):
                        row = g.X[:, bass.ds(b * ROW + t * D, D)]
                        nc.vector.scalar_tensor_tensor(row, dbanks.to_empty(dve)[:, 0:D], g.tg[:, 5:6], row,
                                                       ALU.mult, ALU.add).then_inc(dbanks.emptied, 1)

                    for t in range(T):
                        dve.wait_ge(s_lg, b * T + t + 1)
                        ch.link(nc.vector.tensor_reduce(m[:, :], by_slot(lg[:, :]), AX.X, ALU.max))
                        ch.link(nc.vector.tensor_tensor(LC[:, t % 2, :].rearrange("p (n q) -> p n q", q=NP),
                                                        lg[:, :].rearrange("p (n q) -> p n q", q=NP),
                                                        m[:, :].unsqueeze(1).to_broadcast([P, NE, NP]), ALU.subtract))
                        dve.sem_inc(s_sub, 1)
                        if t >= 1:
                            add(t - 1)
                        if t == 1:
                            norm(ch, lambda t: g.X[:, bass.ds(b * ROW + (ROW + t * D), D)])
                        dve.wait_ge(s_exp, b * T + t + 1)
                        dve.wait_ge(s_cw, b * T + t + 1)
                        ch.link(nc.vector.tensor_reduce(r[:, :], by_slot(LC[:, t % 2, :]), AX.X, ALU.add))
                        nc.vector.reciprocal(r[:, :], r[:, :]).then_inc(s_rec, 1)
                    add(T - 1)
                    dbanks.end()
                    ch.done()

            @block.gpsimd
            def _(pool):
                pool.sem_inc(s_cw, 1)
                with pool.Fori(0, B) as b:
                    for t in range(T):
                        if t >= 1:
                            pool.wait_ge(abanks.filled, b * A_PER + t * QB4)
                        pool.wait_ge(s_rec, b * T + t + 1)
                        nc.gpsimd.tensor_tensor(CW[:, :].rearrange("p (n q) -> p n q", q=NP),
                                                LC[:, t % 2, :].rearrange("p (n q) -> p n q", q=NP),
                                                r[:, :].unsqueeze(1).to_broadcast([P, NE, NP]), ALU.mult).then_inc(s_cw, 1)

            @block.scalar
            def _(act):
                abanks.grant(act)
                with act.Fori(0, B) as b:
                    abanks.start(b)

                    def turned(t):
                        for q in range(QB4):
                            out = abanks.to_empty(act)
                            nc.scalar.copy(CT[:, t % 2, 4 * q:4 * q + 4, :].rearrange("p s t -> p (s t)"),
                                           out[:, :]).then_inc(abanks.emptied, 1)

                    for t in range(T):
                        act.wait_ge(s_sub, b * T + t + 2)
                        nc.scalar.activation(LC[:, t % 2, :], LC[:, t % 2, :], ACT.Exp).then_inc(s_exp, 1)
                        if t >= 1:
                            turned(t - 1)
                    turned(T - 1)
                    abanks.end()

            @block.tensor
            def _(pe):
                with pe.Fori(0, B) as b:
                    dbanks.start(b)
                    abanks.start(b)
                    pe.wait_ge(s_xn, b + 1)
                    turn_to_columns(nc, pe, dbanks, XN, g.ident[:, :])
                    pe.wait_ge(dbanks.emptied, b * D_PER + DC + 2)

                    def spread(t):
                        pe.wait_ge(s_cw, b * T + t + 2)
                        for q in range(QB4):
                            out = abanks.to_fill(pe)
                            for k in range(4):
                                s = 4 * q + k
                                last = pe.transpose(out[:, k * P:(k + 1) * P], CW[:, s * P:(s + 1) * P], g.ident[:, :])
                            last.then_inc(abanks.filled, 1)
                        out = dbanks.to_fill(pe)
                        for s in range(SC):
                            if s % 4 == 0:
                                pe.wait_ge(abanks.emptied, b * A_PER + (t * QB4 + s // 4 + 3))
                            last = pe.matmul(out[:, 0:D], CT[:, t % 2, s, :], XS[:, s, :], start=s == 0, stop=s == SC - 1)
                        last.then_inc(dbanks.filled, 1)

                    for t in range(T):
                        pe.wait_ge(s_sub, b * T + t + 1)
                        for q in range(QB4):
                            last = logits_of(pe, lg[:, q * QW:(q + 1) * QW], t, q)
                        last.then_inc(s_lg, 1)
                        if t >= 1:
                            spread(t - 1)
                    spread(T - 1)
                    dbanks.end()
                    abanks.end()


class Shared:

    def __init__(self, nc):
        self.nc, self.held = nc, []

    def semaphore(self, name):
        self.held.append(self.nc.alloc_semaphore(name))
        return self.held[-1]

    def release(self):
        self.nc.clear_and_free_semaphores(self.held)
        self.nc.all_engine_barrier()
        self.held = []


def program(nc, dr, out):
    with ExitStack() as ctx:
        def sb(name, shape, dt=F32):
            return ctx.enter_context(nc.sbuf_tensor(name, shape, dt))

        g = Shared(nc)
        g.X = sb("X", [P, (B + 1) * ROW])
        g.tg = sb("tg", [P, 8])
        g.ident = sb("ident", [P, P])
        g.ident_b = sb("ident_b", [P, P], BF16)

        with nc.Block() as block:
            s_in, s_graw, s_id = (g.semaphore(n) for n in ("x_in", "gates_in", "ident_in"))

            @block.sync
            def _(sp):
                sp.dma_start(g.tg[:, 0:4], dr["g_xattn"].rearrange("(o n) -> o n", o=1).to_broadcast([P, 4])).then_inc(s_graw, 16)
                sp.dma_start(g.tg[:, 4:8], dr["g_ffn"].rearrange("(o n) -> o n", o=1).to_broadcast([P, 4])).then_inc(s_graw, 16)
                sp.dma_start(g.ident[:, :], dr["ident"]).then_inc(s_id, 16)
                sp.dma_start(g.X[:, 0:B * ROW].rearrange("p (n d) -> p n d", d=D),
                             dr["x"].rearrange("(n p) d -> p n d", p=P)).then_inc(s_in, 16)
                sp.wait_ge(s_in, 16)

            @block.scalar
            def _(act):
                act.wait_ge(s_graw, 32)
                nc.scalar.activation(g.tg[:, :], g.tg[:, :], ACT.Tanh)

            @block.vector
            def _(dve):
                nc.vector.memset(g.X[:, B * ROW:], 0.0)
                dve.wait_ge(s_id, 16)
                nc.vector.tensor_copy(g.ident_b[:, :], g.ident[:, :])

        g.release()
        attention_stage(nc, g, "l0x_", dict(ctx=dr["ctx"], wq=dr["L0_wq"], wk=dr["L0_wk"], wkp=dr["L0_wkp"],
                                            wv=dr["L0_wv"], wo=dr["L0_wo"], cos=dr["L0_cos"], sin=dr["L0_sin"],
                                            gamma_x=dr["L0_gamma_x"], beta_x=dr["L0_beta_x"],
                                            gamma_l=dr["L0_gamma_l"], beta_l=dr["L0_beta_l"]),
                        heads=8, head_dim=64, gate=0, own_keys=True, norm_ctx=True, rope_k=True)
        g.release()
        low_rank_ffn_stage(nc, g, dr)
        g.release()
        attention_stage(nc, g, "l1x_", dict(ctx=dr["ctx"], wq=dr["L1_wq"], wk=dr["L1_wk"], wv=dr["L1_wv"],
                                            wo=dr["L1_wo"], b_o=dr["L1_bo"]),
                        heads=8, head_dim=64, gate=1, out_bias=True)
        g.release()
        soft_moe_stage(nc, g, dr)
        g.release()
        attention_stage(nc, g, "l2x_", dict(ctx=dr["ctx"], wq=dr["L2_wq"], wqp=dr["L2_wqp"], wk=dr["L2_wk"],
                                            wkp=dr["L2_wkp"], wv=dr["L2_wv"], wo=dr["L2_wo"], cos=dr["L2_cos"],
                                            sin=dr["L2_sin"], sel=dr["sel4"], hmask=dr["hmask"], mask=dr["mask"]),
                        heads=16, head_dim=16, gate=2, rope_k=True, rope_q=True, masked=True)
        g.release()
        top2_gelu_stage(nc, g, dr)
        g.release()
        attention_stage(nc, g, "l3x_", dict(ctx=dr["ctx"], wq=dr["L3_wq"], wk=dr["L3_wk"], wv=dr["L3_wv"],
                                            b_q=dr["L3_bq"], b_k=dr["L3_bk"], b_v=dr["L3_bv"], wo=dr["L3_wo"],
                                            b_o=dr["L3_bo"], sel=dr["sel4"], hmask=dr["hmask"]),
                        heads=16, head_dim=16, gate=3, biased=True, out_bias=True)
        g.release()
        top2_silu_stage(nc, g, dr)
        g.release()

        with nc.Block() as block:
            s_out = g.semaphore("x_out")

            @block.sync
            def _(sp):
                sp.dma_start(out.rearrange("(n p) d -> p n d", p=P),
                             g.X[:, 0:B * ROW].rearrange("p (n d) -> p n d", d=D)).then_inc(s_out, 16)
                sp.wait_ge(s_out, 16)


def rotary_tables(head_dim, interleaved):
    inv = (np.float32(1.0) / np.float32(10000.0) ** (np.arange(0, head_dim, 2, dtype=np.float32) / np.float32(head_dim)))
    ang = np.arange(S, dtype=np.float32)[:, None] * inv.astype(np.float32)[None, :]
    ang = np.concatenate([ang, ang], axis=1).astype(np.float64)
    d = np.arange(head_dim)
    sign = np.where(d % 2 == 0, -1.0, 1.0) if interleaved else np.where(d < head_dim // 2, -1.0, 1.0)
    reps = P // head_dim
    return (np.tile(np.cos(ang).T, (reps, 1)).astype(np.float32),
            np.tile((np.sin(ang) * sign).T, (reps, 1)).astype(np.float32))


def partner_columns(n, head_dim, interleaved):
    c = np.arange(n)
    d = c % head_dim
    return c - d + (d ^ 1 if interleaved else (d + head_dim // 2) % head_dim)


def laid_out(inputs):
    a = {k: np.asarray(v) for k, v in inputs.items()}
    r = {"x": a["x"].reshape(B * S, D), "ctx": a["ctx_1024"].reshape(B * S, D),
         "mask": a["mask_1x1xSxS2_ik0"].reshape(S, S), "g_xattn": a["g_xattn"], "g_ffn": a["g_ffn"]}
    inner = a["L0_xattn_Wq"].shape[1]
    r["L0_wq"], r["L0_wo"] = a["L0_xattn_Wq"], a["L0_xattn_Wo"]
    r["L0_wk"], r["L0_wv"] = a["L0_xattn_Wkv"][:, :inner], a["L0_xattn_Wkv"][:, inner:]
    r["L0_wkp"] = r["L0_wk"][:, partner_columns(inner, 64, False)]
    for n in ("gamma_x", "beta_x", "gamma_l", "beta_l"):
        r[f"L0_{n}"] = a[f"L0_xattn_{n}"]
    for n in ("U1", "V1", "b1", "U2", "V2", "b2"):
        r[f"L0_{n}"] = a[f"L0_ffn_{n}"]
    for n in ("Wq", "Wk", "Wv", "Wo"):
        r[f"L1_{n.lower()}"] = a[f"L1_xattn_{n}"]
        r[f"L2_{n.lower()}"] = a[f"L2_xattn_{n.lower()}"].T
    r["L1_bo"] = a["L1_xattn_bo"]
    r["L1_phiT"] = a["L1_ffn_phi_w"].T
    for n in ("phi_b", "expert_w", "expert_b"):
        r[f"L1_{n}"] = a[f"L1_ffn_{n}"]
    swap = partner_columns(D, 16, True)
    r["L2_wqp"], r["L2_wkp"] = r["L2_wq"][:, swap], r["L2_wk"][:, swap]
    for n in ("Wg", "bg", "W1", "b1", "W2", "b2"):
        r[f"L2_{n}"] = a[f"L2_ffn_{n}"]
    r["L3_wq"], r["L3_bq"] = a["L3_xattn_w_q"], a["L3_xattn_b_q"]
    r["L3_wk"], r["L3_wv"] = a["L3_xattn_w_kv"][:, :D], a["L3_xattn_w_kv"][:, D:]
    r["L3_bk"], r["L3_bv"] = a["L3_xattn_b_kv"][:D], a["L3_xattn_b_kv"][D:]
    r["L3_wo"], r["L3_bo"] = a["L3_xattn_w_out"], a["L3_xattn_b_out"]
    for n in ("router_w", "router_b", "routed_w1", "routed_w3", "routed_w2", "shared_w1", "shared_w3", "shared_w2"):
        r[f"L3_{n}"] = a[f"L3_ffn_{n}"]
    r["L0_cos"], r["L0_sin"] = rotary_tables(64, False)
    r["L2_cos"], r["L2_sin"] = rotary_tables(16, True)
    r["ident"] = np.eye(P, dtype=np.float32)
    row = np.arange(P)
    r["sel4"] = (row[:, None] == 32 * (row[None, :] // 32) + 16).astype(np.float32)
    r["iota8"] = np.ones((P, 1), np.float32) * np.arange(8, dtype=np.float32)[None, :]
    r["hmask"] = (row[:, None] % HALF // 16 == np.arange(4)[None, :]).astype(np.float32)
    return {k: np.ascontiguousarray(v) for k, v in r.items()}


def kernel(**inputs):
    import concourse.bacc as _bacc
    from concourse.bass_utils import run_bass_kernel_spmd as _run

    nc = _bacc.Bacc("TRN2", target_bir_lowering=False, num_devices=1)
    arrays = laid_out(inputs)
    dr = {n: nc.dram_tensor(f"in_{n}", a.shape, mybir.dt.from_np(a.dtype), kind="ExternalInput").ap()
          for n, a in arrays.items()}
    out = nc.dram_tensor("out_0", (B * S, D), F32, kind="ExternalOutput").ap()
    program(nc, dr, out)
    r = _run(nc, [{f"in_{n}": a for n, a in arrays.items()}], core_ids=[0])
    return r.results[0]["out_0"].reshape(B, S, D)
```

```python
from contextlib import ExitStack

import numpy as np

import concourse.bass as bass
from concourse import mybir

ALU = mybir.AluOpType
ACT = mybir.ActivationFunctionType
AX = mybir.AxisListType
F32 = mybir.dt.float32
BF16 = mybir.dt.bfloat16
I32 = mybir.dt.int32

P = 128
B, S, D = 8, 512, 256
T = S // P
DC = D // P
ROW = T * D
EPS = 1e-5
RSQRT_SEED = 0x5F3759DF
HALF = 64
MASKED = -1e9


class Chain:

    def __init__(self, eng, sem, per=0, b=None, ahead=0):
        self.eng, self.sem, self.per, self.b, self.n, self.ahead = eng, sem, per, b, 0, ahead

    def value(self):
        return self.n if self.b is None else self.b * self.per + (self.n + self.ahead)

    def step(self, ins):
        self.n += 1
        ins.then_inc(self.sem, 1)

    def settle(self):
        self.eng.wait_ge(self.sem, self.value())

    def link(self, ins):
        self.step(ins)
        self.settle()

    def done(self):
        assert self.n == self.per, f"this loop's steps are {self.n}"


def rsqrt_steps(nc, v, y, t):
    steps = [lambda: nc.vector.tensor_scalar(v, v, EPS, None, ALU.add),
             lambda: nc.vector.tensor_scalar(t.bitcast(I32), v.bitcast(I32), 1, None, ALU.logical_shift_right),
             lambda: nc.vector.tensor_scalar(y.bitcast(I32), t.bitcast(I32), -1.0, float(RSQRT_SEED),
                                             ALU.mult, ALU.add)]
    for _ in range(4):
        steps += [lambda: nc.vector.tensor_tensor(t, y, y, ALU.mult),
                  lambda: nc.vector.tensor_tensor(t, t, v, ALU.mult),
                  lambda: nc.vector.tensor_scalar(t, t, -0.5, 1.5, ALU.mult, ALU.add),
                  lambda: nc.vector.tensor_tensor(y, y, t, ALU.mult)]
    return steps


LN_STEPS = T + T + 19 + T


def layer_norm_pieces(nc, ch, src, dst, st, keep=None):
    var = st["mv"][:, :].rearrange("p (t s) -> p t s", s=2)[:, :, 1]
    y = st["y"][:, 0:T]
    inverse = rsqrt_steps(nc, var, y, st["t"][:, 0:T])
    if keep is not None:
        inverse.append(lambda: nc.vector.tensor_tensor(y, y, keep, ALU.mult))

    def moments():
        ch.eng.sem_inc(st["beat"], 1)
        for t in range(T):
            ch.step(nc.vector.bn_stats(st["six"][:, 6 * t:6 * t + 6], src(t)))
        ch.settle()
        ch.eng.sem_inc(st["beat"], 1)
        for t in range(T):
            ch.step(nc.vector.bn_aggr(st["mv"][:, 2 * t:2 * t + 2], st["six"][:, 6 * t:6 * t + 6]))
        ch.settle()

    def linked(steps):
        for make in steps:
            ch.link(make())

    def apply(tiles):
        for t in tiles:
            ch.step(nc.vector.tensor_scalar(dst(t), src(t), st["mv"][:, 2 * t:2 * t + 1], st["y"][:, t:t + 1],
                                            ALU.subtract, ALU.mult))
        ch.settle()

    return [moments, lambda: linked(inverse[:7]), lambda: linked(inverse[7:14]), lambda: linked(inverse[14:]),
            lambda: apply(range(T // 2)), lambda: apply(range(T // 2, T))]


def layer_norm(nc, ch, src, dst, st, keep=None):
    for piece in layer_norm_pieces(nc, ch, src, dst, st, keep):
        piece()


class Fills:

    def __init__(self, g, banks, name, opening, loop):
        self.banks, self.opening, self.loop = banks, opening, loop
        self.ahead, self.per = len(opening), len(loop)
        self.filled, self.emptied = g.semaphore(name + "_filled"), g.semaphore(name + "_emptied")

    def bank(self, b, step):
        return self.banks[(self.opening if b is None else self.loop).index(step) % len(self.banks)]

    def wait_room(self, pe, b, step):
        n = len(self.banks)
        if b is None:
            pe.wait_ge(self.emptied, max(self.opening.index(step) + 1, n))
        else:
            pe.wait_ge(self.emptied, b * self.per + (self.ahead + max(self.loop.index(step) + 1, n)))

    def filled_at(self, b, step):
        if b is None:
            return self.opening.index(step) + 1
        return b * self.per + (self.ahead + self.loop.index(step) + 1)

    def wait_filled(self, eng, b, step):
        eng.wait_ge(self.filled, self.filled_at(b, step))

    def wait_emptied(self, eng, b, step):
        eng.wait_ge(self.emptied, self.filled_at(b, step) + len(self.banks))


def counted(b, per, n, ahead):
    if b is None:
        return n
    return b * per + (n + per if ahead else n)


FILLS = ("k", "kp", "q", "qp", "v")


def spread(items, first, end):
    at = {}
    for i, item in enumerate(items):
        at.setdefault(first + i * (end - first) // len(items), []).append(item)
    return at


def attention_script(NS, G, KC, KH, NBK, NLN, lag, order, during, masked_at, rope_k, rope_q):
    def projection(gp):
        groups = []
        for half in range(KH):
            kp = [("kp", gp, half)] if rope_k and half == 0 else []
            groups.append([("k", gp, half)] + kp + [("hi", "k", gp, half), ("lo", "k", gp, half)])
        qp = [("qp", gp, 0)] if rope_q else []
        return groups + [[("q", gp, 0)] + qp + [("hi", "q", gp, 0), ("lo", "q", gp, 0)]]

    def staggered(groups):
        held = []
        steps = []
        for grp in groups:
            steps.append([s for s in grp if s[0] != "lo"] + held)
            held = [s for s in grp if s[0] == "lo"]
        return steps + ([held] if held else [])

    def flat(groups):
        return [s for grp in groups for s in grp]

    W = 2 if G == 1 else G
    NT = W * KC
    turns = [[(("xT", "cT")[i % 2], i // 2)] for i in range(2 * DC)]
    early = staggered([grp for gp in order[:during] for grp in projection(gp)])
    rest, values = [], [[("v", kt)] for kt in range(KC)]
    for grp in [grp for gp in order[during:] for grp in projection(gp)]:
        rest += [grp] + values[:1]
        del values[:1]
    rest = staggered(rest + values)
    late = staggered([grp for gp in range(NBK) if gp not in order for grp in projection(gp)])
    maxima = [[("mx", 0, k)] for k in range(NT)]
    max_late = 0 in order[during:]

    def closing(maxima, outputs):
        own = [[("rc", NS - 1, i)] for i in range(4)] + [[("at", NS - 1)]] if outputs else []
        groups = list(rest)
        first = 2 * (KH + 1) if max_late else 0
        outs = [[("out", t)] for t in range(T if outputs else 0)]
        for t in range(len(outs) if G == 1 else 0):
            groups.insert(min(max(first, 4) + 2 * t, len(groups)), [("out", t)])
        n = len(groups)
        at = {}
        for part in (spread(own, 0, min(n, 3 if G > 1 else 4)), spread(maxima, first, n - (G == 1)),
                     spread(outs, min(3, n - 1), n) if G > 1 else {}):
            for k, extra in part.items():
                at.setdefault(k, []).extend(extra)
        steps = [("sum", NS - 1)] if outputs else []
        for i, grp in enumerate(groups):
            steps += grp + flat(at.get(i, []))
        last = max([k for k, step in enumerate(steps) if step[0] == "mx"], default=len(steps) - 1)
        steps.insert(last + 1, ("mr", 0))
        return steps

    opening = flat(turns + early) + closing(maxima, False)
    places = {}

    def put(part):
        for place, groups in part.items():
            places.setdefault(place, []).extend(groups)

    done_at = NT - max(2, NT // 5)
    for s in range(NS - 1):
        begin = s * NT
        first = masked_at if s + 1 == NS - 1 else 0
        put(spread([[("mx", s + 1, k)] for k in range(NT)], begin + first, begin + done_at))
        put({begin + done_at: [[("mr", s + 1)]]})
    for s in range(NS - 1):
        begin, end = ((s + 2) * NT - 1, (s + 2) * NT + lag * W) if s < NS - 2 else ((s + 1) * NT + lag * W + 1, NS * NT)
        put({begin: [[("sum", s)]]})
        put(spread([[("rc", s, i)] for i in range(4)] + [[("at", s)]], begin, end))
    put(spread([[("ln", i)] for i in range(NLN)], 1, (NS - 1) * NT - NT // 2))
    put(spread(late, NT + NT // 4, 2 * NT - NT // 8) if late else {})
    put(spread(turns, (NS - 1) * NT - NT // 2 + 1, (NS - 1) * NT + NT // 8))
    begin = (NS - 1) * NT + NT // 8
    put(spread(early, begin, NS * NT - (NT // 2 if G > 1 else NT // 8)))
    left = maxima
    if not max_late:
        n = 3 * NT // 4 if G > 1 else NT // 2
        left = maxima[NT - n:]
        put(spread(maxima[:NT - n], (NS - 1) * NT + n, NS * NT))
    loop = []
    for q in range(NS * KC + lag):
        s, kc = q // KC, q % KC
        if q < NS * KC:
            for n in range(kc * W, kc * W + W):
                loop.append(("st", s, n))
                loop += flat(places.pop(s * NT + n, []))
        if q >= lag:
            loop.append(("pv", q - lag))
            if (q - lag) % KC == KC - 1:
                loop.append(("oc", (q - lag) // KC))
    loop += closing(left, True)
    assert not places and set(opening) <= set(loop) and len(set(loop)) == len(loop)
    return opening, loop


def attention_stage(nc, g, pre, dr, *, heads, head_dim, gate, own_keys=False, norm_ctx=False, rope_k=False,
                    rope_q=False, masked=False, biased=False, out_bias=False):
    G = HALF // head_dim
    INNER = heads * head_dim
    W = 2 if G == 1 else G
    NS = heads // W
    NU = heads // G
    NBK = NU // 2
    KH = 2 if own_keys else 1
    KC = T * KH
    NT = W * KC
    LAG = 1 if G > 1 else 2
    VH = HALF if G == 1 else 32
    NPT = 6 if KH == 2 else 7 if masked else 8
    EARLY = NBK if KH == 1 else 3
    D_BANKS, O_BANKS = 3, 1
    OC = 4
    SCALE = head_dim ** -0.5
    F32R = mybir.dt.float32r

    NLN = 18 if norm_ctx else 6
    order, during = ([1, 2, 0], 2) if KH == 2 else (list(range(NBK)), NBK - 1)
    opening, script = attention_script(NS, G, KC, KH, NBK, NLN, LAG, order, during, 0, rope_k, rope_q)
    v_on_act = rope_q

    def stream(step):
        kind = step[0]
        if kind in ("mx", "out", "kp", "qp", "xT"):
            return "D"
        if kind == "k":
            return "D" if rope_k and step[2] == 0 else "A"
        if kind == "q":
            return "D" if rope_q else "A"
        if kind == "v":
            return "A" if v_on_act else "D"
        return "A" if kind in ("st", "cT") else None

    def in_stream(steps, name):
        return [s for s in steps if stream(s) == name]

    splits = [s[1:] for s in opening if s[0] == "lo"]
    splits += [s[1:] for s in script if s[0] == "lo" and s not in opening]
    LO_PER = len(splits)
    rotated = [s for s in splits if (s[0] == "k" and rope_k and s[2] == 0) or (s[0] == "q" and rope_q)]
    SU_PER = NS * (NT - W)
    PV_PER = NS * KC
    mx_tiles = [(j, qc, kh) for j in range(W) for qc in range(T) for kh in range(KH)]

    def keys_of(s, j):
        return (2 * s + j, 2 * s + j) if G == 1 else (s, s * G + j)

    with ExitStack() as ctx:
        def sb(name, shape, dt=F32):
            return ctx.enter_context(nc.sbuf_tensor(pre + name, shape, dt))

        def ps(name):
            return ctx.enter_context(nc.psum_tensor(pre + name, [P, 512], F32))

        def sem(name):
            return g.semaphore(pre + name)

        KU = 2 * EARLY
        QU = KU if G == 1 else heads
        wq, wk, wv = (sb(n, [P, DC, INNER]) for n in ("wq", "wk", "wv"))
        wo = sb("wo", [P, OC, D])
        wkp = sb("wkp", [P, DC, INNER]) if rope_k else None
        wqp = sb("wqp", [P, DC, INNER]) if rope_q else None
        cos, sin = (sb("cos", [P, S]), sb("sin", [P, S])) if rope_k else (None, None)
        ones = sb("ones", [P, HALF]) if G == 1 else None
        sel = sb("sel", [P, P]) if G > 1 else None
        hmask = sb("hmask", [P, 4]) if G > 1 else None
        gam = sb("gam", [P, 8]) if norm_ctx else None
        bqk = sb("bqk", [P, 2, NBK]) if biased else None
        bvb = sb("bvb", [P, INNER]) if biased else None
        bob = sb("bob", [P, D]) if out_bias else None
        XN, CN = sb("XN", [P, T, D]), sb("CN", [P, T, D])
        XT, CT = sb("XT", [P, DC, S]), sb("CT", [P, DC, S])
        F = sb("F", [HALF, 2, 2, S])
        TMP = sb("TMP", [HALF, S]) if rope_k else None
        KHI = sb("KHI", [P, KU, KH * S], F32R)
        KLO = sb("KLO", [P, KU, KH * S], F32R)
        QC = sb("QC", [P, 2, S]) if G > 1 else None
        QA = sb("QA", [P, QU, S], F32R)
        QB = sb("QB", [P, QU, S], F32R)
        V = sb("V", [P, KC, heads * VH])
        PT = sb("PT", [P, NPT, S])
        SU = sb("SU", [P, 2, W, S]) if G == 1 else None
        OS = sb("OS", [P, S])
        R = sb("R", [P, S])
        AT = sb("AT", [P, OC, S])
        mpart = sb("mpart", [P, NT])
        negm = sb("negm", [P, W * T], BF16)
        st = statistics(nc, g, ctx, pre)
        if masked:
            mrow = AT[:, :, :].bitcast(I32)
            mbn, mbT = sb("mbn", [P, T, S], BF16), sb("mbT", [P, T, S], BF16)
            many = sb("many", [P, T])

        A = Fills(g, [ps(f"a{i}") for i in range(3)], pre + "A", in_stream(opening, "A"), in_stream(script, "A"))
        Dv = Fills(g, [ps(f"d{i}") for i in range(D_BANKS)], pre + "D", in_stream(opening, "D"), in_stream(script, "D"))
        bank_o = [ps(f"o{i}") for i in range(O_BANKS)]
        bank_m = ps("m")

        s_w = sem("weights")
        s_ctx = sem("ctx")
        s_cl = sem("ctxnorm")
        s_zero = sem("padding")
        s_ones = sem("ones")
        s_pad = sem("wo_rows")
        s_mk = sem("mask")
        s_mkt = sem("maskT")
        s_xn = sem("xn")
        s_xt = sem("xT")
        s_ct = sem("cT")
        s_f = sem("rotated")
        s_hi = sem("hi")
        s_lo = sem("lo")
        s_qm = sem("masked_q")
        s_nm = sem("negmax")
        s_mr = sem("maxrow")
        s_mc = sem("maxcopy")
        s_pv = sem("pv")
        s_su = sem("expsum")
        s_os = sem("osum")
        s_sm = sem("sums")
        s_rc = sem("inverse")
        s_ob = sem("out_bias")
        s_at = sem("attnT")
        s_vch = sem("vchain")
        s_pch = sem("pchain")
        s_beat = st["beat"]

        w_loads = [(wk[:, :, :], dr["wk"].rearrange("(c p) n -> p c n", p=P)),
                   (wq[:, :, :], dr["wq"].rearrange("(c p) n -> p c n", p=P)),
                   (wv[:, :, :], dr["wv"].rearrange("(c p) n -> p c n", p=P))]
        if rope_k:
            w_loads += [(wkp[:, :, :], dr["wkp"].rearrange("(c p) n -> p c n", p=P)),
                        (cos[:, :], dr["cos"]), (sin[:, :], dr["sin"])]
        if rope_q:
            w_loads += [(wqp[:, :, :], dr["wqp"].rearrange("(c p) n -> p c n", p=P))]
        if G > 1:
            w_loads += [(sel[:, :], dr["sel"]), (hmask[:, :], dr["hmask"])]
            wo_g = dr["wo"].rearrange("(g j r) n -> j r g n", j=G, r=head_dim)
            w_loads += [(wo[32 * j:32 * j + head_dim, :, :], wo_g[j]) for j in range(G)]
        else:
            w_loads += [(wo[:, :, :], dr["wo"].rearrange("(c p) n -> p c n", p=P))]
        if norm_ctx:
            for i, name in enumerate(("gamma_x", "beta_x", "gamma_l", "beta_l")):
                w_loads += [(gam[:, 2 * i + c:2 * i + c + 1], dr[name].rearrange("(c p o) -> c p o", p=P, o=1)[c])
                            for c in range(DC)]
        if biased:
            for i, name in enumerate(("b_q", "b_k")):
                w_loads += [(bqk[:, i, c:c + 1], dr[name].rearrange("(c p o) -> c p o", p=P, o=1)[c])
                            for c in range(NBK)]
            w_loads += [(bvb[:, :], dr["b_v"].rearrange("(o n) -> o n", o=1).to_broadcast([P, INNER]))]
        if out_bias:
            w_loads += [(bob[:, :], dr["b_o"].rearrange("(o n) -> o n", o=1).to_broadcast([P, D]))]
        if masked:
            w_loads += [(mrow[:, :, :], dr["mask"].rearrange("(t p) k -> p t k", p=P))]
        W_ALL = 16 * len(w_loads)
        ctx_rows = dr["ctx"].rearrange("(n p) d -> p n d", p=P)

        def unit_slot(u):
            return u % KU

        def added(i):
            return i // NT * (NT - W) + max(i % NT - W, i % NT % W) + 1

        def query_slot(h):
            return h % QU

        def sums_before(step):
            return sum(s[0] == "sum" for s in script[:script.index(step)])

        def ahead(b, step):
            return b is not None and step in opening

        block = ctx.enter_context(nc.Block())

        @block.sync
        def _(sp):
            sp.dma_start(CN[:, :, :], ctx_rows[:, 0:T, :]).then_inc(s_ctx, 16)
            if G > 1:
                sp.wait_ge(s_pad, 1)
            for dst, src in w_loads:
                sp.dma_start(dst, src).then_inc(s_w, 16)
            A.wait_filled(sp, None, ("cT", DC - 1))
            sp.dma_start(CN[:, :, :], ctx_rows[:, T:2 * T, :]).then_inc(s_ctx, 16)
            with sp.Fori(2, B) as b:
                A.wait_filled(sp, b - 2, ("cT", DC - 1))
                sp.dma_start(CN[:, :, :], ctx_rows[:, bass.ds(b * T, T), :]).then_inc(s_ctx, 16)
            A.wait_filled(sp, B - 2, ("cT", DC - 1))
            sp.dma_start(CN[:, :, :], ctx_rows[:, 0:T, :]).then_inc(s_ctx, 16)

        @block.gpsimd
        def _(pool):
            pads = [(KLO[HALF:P, :, :], 0.0), (QB[HALF:P, :, :], 0.0)]
            for i, (rows, value) in enumerate(pads):
                nc.gpsimd.memset(rows.bitcast(F32), value).then_inc(s_pch, 1)
                pool.wait_ge(s_pch, i + 1)
            nc.gpsimd.memset(KLO[HALF:HALF + 1, :, :].bitcast(F32), 1.0).then_inc(s_zero, 1)

            def add_bias(b):
                pool.wait_ge(s_xn, b + 1)
                row = g.X[:, bass.ds(b * ROW, ROW)].rearrange("p (t d) -> p t d", d=D)
                nc.gpsimd.tensor_tensor(row, row, bob[:, :].unsqueeze(1).to_broadcast([P, T, D]),
                                        ALU.add).then_inc(s_ob, 1)

            if G > 1:
                pool.wait_ge(s_w, W_ALL)
                if out_bias:
                    pool.wait_ge(s_pad, 2)
                def mask_queries(b, s):
                    pool.wait_ge(s_lo, counted(b, LO_PER, splits.index(("q", s // 2, 0)) + 1, s < 2))
                    if b is not None and s == 1:
                        A.wait_filled(pool, b, ("st", s, NT - 1))
                    pool.sem_inc(s_beat, 1)
                    for j in range(G):
                        slot = query_slot(s * G + j)
                        nc.gpsimd.tensor_scalar(QA[:, slot, :], QC[:, s % 2, :], hmask[:, j:j + 1], 0.0,
                                                ALU.mult, ALU.add).then_inc(s_pch, 1)
                        last = nc.gpsimd.tensor_scalar(QB[0:HALF, slot, :], QC[0:HALF, s % 2, :],
                                                       hmask[0:HALF, j:j + 1], 0.0, ALU.mult, ALU.add)
                    last.then_inc(s_qm, 1)

                for s in (0, 1):
                    mask_queries(None, s)
                with pool.Fori(0, B) as b:
                    if out_bias:
                        add_bias(b)
                    for s in (2, 3, 0, 1):
                        mask_queries(b, s)
            else:
                if out_bias:
                    pool.wait_ge(s_pad, 2)
                with pool.Fori(0, B) as b:
                    if out_bias:
                        add_bias(b)
                    for s in range(NS):
                        for n in range(W, NT):
                            i = s * NT + n
                            if n == W and s >= 2:
                                pool.wait_ge(s_sm, b * NS + (s - 1))
                            A.wait_emptied(pool, b, ("st", s, n))
                            total = SU[:, s % 2, n % W, :]
                            if n >= 2 * W:
                                pool.wait_ge(s_su, b * SU_PER + (added(i) - W))
                                so_far = total
                            else:
                                so_far = PT[:, (i - W) % NPT, :]
                            nc.gpsimd.tensor_tensor(total, so_far, PT[:, i % NPT, :], ALU.add).then_inc(s_su, 1)

        @block.tensor
        def _(pe):
            def turn(b, step):
                src, banks = (XN, Dv) if step[0] == "xT" else (CN, A)
                banks.wait_room(pe, b, step)
                for t in range(T):
                    last = pe.transpose(banks.bank(b, step)[:, t * P:(t + 1) * P],
                                        src[:, t, step[1] * P:(step[1] + 1) * P], g.ident[:, :])
                last.then_inc(banks.filled, 1)

            if masked:
                pe.wait_ge(s_mk, 1)
                for kt in range(T):
                    if kt:
                        pe.wait_ge(s_mk, kt + 1)
                    for qt in range(T):
                        last = pe.matmul(Dv.banks[0][:, qt * P:(qt + 1) * P], mbn[:, qt, kt * P:(kt + 1) * P],
                                         g.ident_b[:, :], start=True, stop=True, skip_group_check=True)
                    last.then_inc(s_mkt, 1)
                pe.wait_ge(s_mk, T + 1)
            def walk(b, steps):
                for step in steps:
                    kind = step[0]
                    nxt = ahead(b, step)
                    if kind in FILLS and step == next(x for x in steps if x[0] in FILLS and x in opening):
                        if b is None:
                            pe.wait_ge(s_w, W_ALL)
                            pe.wait_ge(s_zero, 1)
                            pe.wait_ge(s_ones, 1)
                            pe.wait_ge(s_pad, 1 + out_bias)
                        pe.wait_ge(s_xt, counted(b, 1, 1, nxt))
                        pe.wait_ge(s_ct, counted(b, 1, 1, nxt))
                    if kind in ("k", "kp", "q", "qp"):
                        fills = A if stream(step) == "A" else Dv
                        fills.wait_room(pe, b, step)
                        out = fills.bank(b, step)
                        w = {"k": wk, "kp": wkp, "q": wq, "qp": wqp}[kind]
                        src = CT if kind[0] == "k" and step[2] == 0 else XT
                        for c in range(DC):
                            last = pe.matmul(out[:, :], w[:, c, step[1] * P:(step[1] + 1) * P], src[:, c, :],
                                             start=c == 0, stop=c == DC - 1)
                        last.then_inc(fills.filled, 1)
                    elif kind == "v":
                        fills = A if v_on_act else Dv
                        fills.wait_room(pe, b, step)
                        src, t = (XT, step[1] - T) if step[1] >= T else (CT, step[1])
                        for c in range(DC):
                            last = pe.matmul(fills.bank(b, step)[:, 0:INNER], src[:, c, t * P:(t + 1) * P], wv[:, c, :],
                                             start=c == 0, stop=c == DC - 1)
                        last.then_inc(fills.filled, 1)
                    elif kind == "mx":
                        s, k = step[1:]
                        j, qc, kh = mx_tiles[k]
                        u, h = keys_of(s, j)
                        if k == 0:
                            gp = s if G == 1 else s // 2
                            n = max(splits.index(("q", gp, 0)), splits.index(("k", gp, KH - 1))) + 1
                            pe.wait_ge(s_lo, counted(b, LO_PER, n, nxt))
                            if G > 1:
                                pe.wait_ge(s_qm, counted(b, NS, s + 1, nxt))
                        Dv.wait_room(pe, b, step)
                        mm = pe.matmul(Dv.bank(b, step)[:, :], QA[:, query_slot(h), qc * P:(qc + 1) * P],
                                       KHI[:, unit_slot(u), kh * S:kh * S + S], start=True, stop=not masked)
                        if masked:
                            mm = pe.matmul(Dv.bank(b, step)[:, :], g.ident_b[:, :], mbn[:, qc, :], start=False, stop=True)
                        mm.then_inc(Dv.filled, 1)
                    elif kind == "mr":
                        if b is not None and sums_before(step):
                            pe.wait_ge(s_rc, b * NS + sums_before(step))
                        pe.wait_ge(s_nm, counted(b, NS, step[1] + 1, nxt))
                        for j in range(W):
                            for qc in range(T):
                                last = pe.matmul(bank_m[32 * j:32 * j + 1, qc * P:(qc + 1) * P],
                                                 negm[:, j * T + qc:j * T + qc + 1], g.ident_b[:, :],
                                                 start=True, stop=True, skip_group_check=True)
                        last.then_inc(s_mr, 1)
                    elif kind == "st":
                        s, n = step[1:]
                        kc, j = n // W, n % W
                        u, h = keys_of(s, j)
                        if n == 0:
                            pe.wait_ge(s_mc, b * NS + s + 1)
                        A.wait_room(pe, b, step)
                        out = A.bank(b, step)[:, :]
                        pe.matmul(out, KHI[:, unit_slot(u), kc * P:(kc + 1) * P], QA[:, query_slot(h), :],
                                  start=True, stop=False)
                        mm = pe.matmul(out, KLO[:, unit_slot(u), kc * P:(kc + 1) * P], QB[:, query_slot(h), :],
                                       start=False, stop=not masked)
                        if masked:
                            mm = pe.matmul(out, g.ident_b[:, :], mbT[:, kc, :], start=False, stop=True)
                        mm.then_inc(A.filled, 1)
                    elif kind == "pv":
                        s, kc = step[1] // KC, step[1] % KC
                        A.wait_emptied(pe, b, ("st", s, kc * W + W - 1))
                        if kc == 0 and s >= O_BANKS:
                            pe.wait_ge(s_os, b * NS + s - O_BANKS + 1)
                        for j in range(W):
                            u, h = keys_of(s, j)
                            row = VH * j
                            last = pe.matmul(bank_o[s % O_BANKS][row:row + VH, :], V[:, kc, h * VH:h * VH + VH],
                                             PT[:, (s * NT + kc * W + j) % NPT, :], start=kc == 0, stop=kc == KC - 1)
                        last.then_inc(s_pv, 1)
                    elif kind == "sum":
                        if step[1] < NS - 2:
                            pe.wait_ge(s_mc, b * NS + step[1] + 3)
                        if sums_before(step):
                            pe.wait_ge(s_rc, b * NS + sums_before(step))
                        if G > 1:
                            pe.wait_ge(s_os, b * NS + step[1] + 1)
                            last = pe.matmul(bank_m[:, :], sel[:, :], OS[:, :], start=True, stop=True)
                        else:
                            pe.wait_ge(s_su, b * SU_PER + (step[1] + 1) * (NT - W))
                            for j in range(W):
                                last = pe.matmul(bank_m[HALF * j:HALF * j + HALF, :], ones[:, :],
                                                 SU[:, step[1] % 2, j, :], start=True, stop=True)
                        last.then_inc(s_sm, 1)
                    elif kind in ("xT", "cT"):
                        if kind == "xT" and step[1] == 0:
                            pe.wait_ge(s_xn, counted(b, 1, 1, nxt))
                        if kind == "cT" and step[1] == 0:
                            if norm_ctx:
                                pe.wait_ge(s_cl, counted(b, 1, 1, nxt))
                            else:
                                pe.wait_ge(s_ctx, counted(b, 16, 16, nxt))
                        turn(b, step)
                    elif kind == "out":
                        t = step[1]
                        if t == 0:
                            pe.wait_ge(s_at, b * NS + NS)
                        Dv.wait_room(pe, b, step)
                        for c in range(OC):
                            last = pe.matmul(Dv.bank(b, step)[:, 0:D], AT[:, c, t * P:(t + 1) * P], wo[:, c, :],
                                             start=c == 0, stop=c == OC - 1)
                        last.then_inc(Dv.filled, 1)

            walk(None, opening)
            with pe.Fori(0, B) as b:
                walk(b, script)

        @block.scalar
        def _(act):
            act.sem_inc(A.emptied, 3)

            def turned(step, out):
                c = step[1]
                if norm_ctx:
                    return nc.scalar.activation(CT[:, c, :], out[:, :], ACT.Identity, bias=gam[:, 2 + c:3 + c],
                                                scale=gam[:, c:c + 1])
                return nc.scalar.copy(CT[:, c, :], out[:, :])

            def max_copy(b, s, nxt):
                act.wait_ge(s_mr, counted(b, NS, s + 1, nxt))
                for j in range(W):
                    h = keys_of(s, j)[1]
                    ins = nc.scalar.copy(QB[HALF:HALF + 1, query_slot(h), :], bank_m[32 * j:32 * j + 1, :])
                ins.then_inc(s_mc, 1)

            def walk(b, steps):
                for step in steps:
                    kind = step[0]
                    nxt = ahead(b, step)
                    if kind == "hi":
                        what = step[1:]
                        i = splits.index(what)
                        if what in rotated:
                            act.wait_ge(s_f, counted(b, len(rotated), rotated.index(what) + 1, nxt))
                        else:
                            src = (what[0],) + what[1:]
                            A.wait_filled(act, b, src)
                            if i >= 2 or nxt:
                                act.wait_ge(s_lo, counted(b, LO_PER, i - 1, nxt))
                            for e in range(2):
                                rows = slice(e * HALF, e * HALF + HALF)
                                out = A.bank(b, src)[rows, :]
                                scale = SCALE if what[0] == "q" else 1.0
                                if biased:
                                    ins = nc.scalar.activation(F[:, i % 2, e, :], out, ACT.Identity, scale=scale,
                                                               bias=bqk[rows, int(what[0] == "k"), what[1]:what[1] + 1])
                                else:
                                    ins = nc.scalar.mul(F[:, i % 2, e, :], out, scale)
                            ins.then_inc(A.emptied, 1)
                            A.wait_emptied(act, b, src)
                        if G > 1 and what[0] == "q" and what[1]:
                            act.wait_ge(s_qm, counted(b, NS, 2 * what[1], nxt))
                        for e in range(2):
                            u = 2 * what[1] + e
                            src = F[:, i % 2, e, :]
                            if what[0] == "k":
                                cols = slice(what[2] * S, what[2] * S + S)
                                nc.scalar.copy(KHI[0:HALF, unit_slot(u), cols], src)
                                ins = nc.scalar.copy(KHI[HALF:P, unit_slot(u), cols], src)
                            elif G == 1:
                                nc.scalar.copy(QA[0:HALF, query_slot(u), :], src)
                                ins = nc.scalar.copy(QB[0:HALF, query_slot(u), :], src)
                            else:
                                ins = nc.scalar.copy(QC[0:HALF, u % 2, :].bitcast(F32R), src)
                        ins.then_inc(s_hi, 1)
                    elif kind == "v" and v_on_act:
                        A.wait_filled(act, b, step)
                        dst = V[:, step[1], :].rearrange("p (h v) -> p h v", v=VH)[:, :, 0:head_dim]
                        nc.scalar.copy(dst, A.bank(b, step)[:, 0:INNER].rearrange("p (h v) -> p h v", v=head_dim))\
                            .then_inc(A.emptied, 1)
                    elif kind == "cT":
                        A.wait_filled(act, b, step)
                        turned(step, A.bank(b, step)).then_inc(A.emptied, 1)
                        if step[1] == DC - 1:
                            A.wait_emptied(act, b, step)
                            act.sem_inc(s_ct, 1)
                    elif kind == "mr":
                        max_copy(b, step[1], nxt)
                    elif kind == "st":
                        s, n = step[1:]
                        i = s * NT + n
                        A.wait_filled(act, b, step)
                        if i >= NPT:
                            act.wait_ge(s_pv, b * PV_PER + (i - NPT) // W + 1)
                            if G == 1:
                                act.wait_ge(s_su, b * SU_PER + added(i - NPT))
                        nc.scalar.activation(PT[:, i % NPT, :], A.bank(b, step)[:, :], ACT.Exp).then_inc(A.emptied, 1)
                    elif kind == "oc":
                        act.wait_ge(s_pv, b * PV_PER + (step[1] + 1) * KC)
                        if step[1]:
                            act.wait_ge(s_at, b * NS + step[1])
                        nc.scalar.copy(OS[:, :], bank_o[step[1] % O_BANKS][:, :]).then_inc(s_os, 1)

            act.wait_ge(s_w, W_ALL)
            act.wait_ge(s_zero, 1)
            walk(None, opening)
            with act.Fori(0, B) as b:
                walk(b, script)

        @block.vector
        def _(dve):
            pre_ch = Chain(dve, s_vch)
            if G > 1:
                nc.vector.memset(wo[:, :, :], 0.0).then_inc(s_pad, 1)
                nc.vector.memset(V[:, :, :], 1.0).then_inc(s_ones, 1)
            else:
                dve.sem_inc(s_pad, 1)
                nc.vector.memset(ones[:, :], 1.0).then_inc(s_ones, 1)
            dve.sem_inc(Dv.emptied, D_BANKS)
            if masked:
                dve.wait_ge(s_w, W_ALL)
                pre_ch.link(nc.vector.tensor_copy(PT[:, 0:T, :], mrow[:, :, :]))
                pre_ch.link(nc.vector.tensor_scalar(PT[:, 0:T, :], PT[:, 0:T, :], 0.0, None, ALU.not_equal))
                pre_ch.link(nc.vector.tensor_reduce(many[:, :], PT[:, 0:T, :], AX.X, ALU.max))
                pre_ch.link(nc.vector.tensor_scalar(PT[:, 0:T, :], PT[:, 0:T, :], -1.0, -MASKED, ALU.add, ALU.mult))
                for t in range(T):
                    ins = nc.vector.tensor_scalar(mbn[:, t, :], PT[:, t, :], many[:, t:t + 1], None, ALU.mult)
                    if t < T - 1:
                        pre_ch.link(ins)
                ins.then_inc(s_mk, 1)
                for kt in range(T):
                    dve.wait_ge(s_mkt, kt + 1)
                    nc.vector.tensor_copy(mbT[:, kt, :], Dv.banks[0][:, :]).then_inc(s_mk, 1)

            def norm_pieces(b, ch):
                if b is None:
                    src = lambda t: g.X[:, t * D:(t + 1) * D]
                else:
                    src = lambda t: g.X[:, bass.ds(b * ROW + (ROW + t * D), D)]
                xn, cn = (lambda t: XN[:, t, :]), (lambda t: CN[:, t, :])
                pieces = layer_norm_pieces(nc, ch, src, xn, st, keep=many[:, :] if masked else None)
                if norm_ctx:
                    pieces += layer_norm_pieces(nc, ch, xn, xn, st)
                return pieces, (layer_norm_pieces(nc, ch, cn, cn, st) if norm_ctx else [])

            def norm(b, ch, i):
                x_pieces, c_pieces = norm_pieces(b, ch)
                if i < len(x_pieces):
                    x_pieces[i]()
                    if i == len(x_pieces) - 1:
                        dve.sem_inc(s_xn, 1)
                else:
                    i -= len(x_pieces)
                    if i == 0:
                        dve.wait_ge(s_ctx, counted(b, 16, 16, True))
                    c_pieces[i]()
                    if i == len(c_pieces) - 1:
                        dve.sem_inc(s_cl, 1)

            def turned(c, out):
                if norm_ctx:
                    return nc.vector.tensor_scalar(XT[:, c, :], out, gam[:, 4 + c:5 + c], gam[:, 6 + c:7 + c],
                                                   ALU.mult, ALU.add)
                return nc.vector.tensor_copy(XT[:, c, :], out)

            for i in range(NLN):
                norm(None, pre_ch, i)
            dve.wait_ge(s_w, W_ALL)
            dve.wait_ge(s_zero, 1)
            if out_bias:
                nc.vector.tensor_scalar(bob[:, :], bob[:, :], g.tg[:, gate:gate + 1], None, ALU.mult).then_inc(s_pad, 1)
            if biased:
                pre_ch.link(nc.vector.tensor_scalar(bqk[:, 0, :], bqk[:, 0, :], SCALE, None, ALU.mult))
            per = (LN_STEPS * (3 if norm_ctx else 1) + int(masked) + 6 * len(rotated)
                   + (NS if KH == 2 else 0) + NS * (T + 1))

            def walk(b, ch, steps):
                for step in steps:
                    nxt = ahead(b, step)
                    kind = step[0]
                    fill = stream(step) == "D"
                    if fill:
                        Dv.wait_filled(dve, b, step)
                        out = Dv.bank(b, step)
                    if kind == "xT":
                        turned(step[1], out[:, :]).then_inc(Dv.emptied, 1)
                        if step[1] == DC - 1:
                            Dv.wait_emptied(dve, b, step)
                            dve.sem_inc(s_xt, 1)
                    elif kind == "v" and fill:
                        dst = V[:, step[1], :].rearrange("p (h v) -> p h v", v=VH)[:, :, 0:head_dim]
                        src = out[:, 0:INNER].rearrange("p (h v) -> p h v", v=head_dim)
                        if biased:
                            ins = nc.vector.tensor_tensor(dst, src, bvb[:, :].rearrange("p (h v) -> p h v", v=head_dim),
                                                          ALU.add)
                        else:
                            ins = nc.vector.tensor_copy(dst, src)
                        ins.then_inc(Dv.emptied, 1)
                    elif kind in ("k", "kp", "q", "qp") and fill:
                        i = splits.index((kind[0],) + step[1:])
                        scale = SCALE if kind[0] == "q" else 1.0
                        if (i >= 2 or nxt) and len(kind) == 1:
                            dve.wait_ge(s_lo, counted(b, LO_PER, i - 1, nxt))
                        for e in range(2):
                            rows = slice(e * HALF, e * HALF + HALF)
                            dst = F[:, i % 2, e, :]
                            if len(kind) == 1:
                                ch.step(nc.vector.scalar_tensor_tensor(dst, out[rows, :], scale, cos[rows, :],
                                                                       ALU.mult, ALU.mult))
                                if e == 1:
                                    ch.settle()
                                    dve.sem_inc(Dv.emptied, 1)
                            else:
                                ch.link(nc.vector.scalar_tensor_tensor(TMP[:, :], out[rows, :], scale, sin[rows, :],
                                                                       ALU.mult, ALU.mult))
                                ch.link(nc.vector.tensor_tensor(dst, dst, TMP[:, :], ALU.add))
                        if len(kind) == 2:
                            dve.sem_inc(Dv.emptied, 1)
                            dve.sem_inc(s_f, 1)
                    elif kind == "lo":
                        what = step[1:]
                        i = splits.index(what)
                        dve.wait_ge(s_hi, counted(b, LO_PER, i + 1, nxt))
                        for e in range(2):
                            u = 2 * what[1] + e
                            full = F[:, i % 2, e, :]
                            if what[0] == "k":
                                cols = slice(what[2] * S, what[2] * S + S)
                                hi, lo = KHI[0:HALF, unit_slot(u), cols], KLO[0:HALF, unit_slot(u), cols]
                            elif G == 1:
                                hi, lo = QA[0:HALF, query_slot(u), :], QA[HALF:P, query_slot(u), :]
                            else:
                                hi, lo = QC[0:HALF, u % 2, :], QC[HALF:P, u % 2, :]
                            ins = nc.vector.tensor_tensor(lo, full, hi.bitcast(F32), ALU.subtract)
                        ins.then_inc(s_lo, 1)
                    elif kind == "mx":
                        s, k = step[1:]
                        if KH == 1:
                            ins = nc.vector.tensor_reduce(negm[:, k:k + 1], out[:, :], AX.X, ALU.max, negate=True)
                        else:
                            ins = nc.vector.tensor_reduce(mpart[:, k:k + 1], out[:, :], AX.X, ALU.max)
                        ins.then_inc(Dv.emptied, 1)
                        if k == NT - 1:
                            Dv.wait_emptied(dve, b, step)
                            if KH == 2:
                                ch.link(nc.vector.tensor_reduce(negm[:, :], mpart[:, :].rearrange("p (a h) -> p a h", h=KH),
                                                                AX.X, ALU.max, negate=True))
                            dve.sem_inc(s_nm, 1)
                    elif kind == "rc":
                        s, i = step[1:]
                        cols = slice(i * P, i * P + P)
                        if i == 0:
                            dve.wait_ge(s_sm, b * NS + s + 1)
                        ch.step(nc.vector.reciprocal(R[:, cols], bank_m[:, cols]))
                        if i == T - 1:
                            ch.settle()
                            dve.sem_inc(s_rc, 1)
                    elif kind == "at":
                        s = step[1]
                        if G == 1:
                            dve.wait_ge(s_os, b * NS + s + 1)
                        ch.link(nc.vector.tensor_tensor(AT[:, s, :], OS[:, :], R[:, :], ALU.mult))
                        dve.sem_inc(s_at, 1)
                    elif kind == "ln":
                        norm(b, ch, step[1])
                    elif kind == "out":
                        row = g.X[:, bass.ds(b * ROW + step[1] * D, D)]
                        if out_bias and step[1] == 0:
                            dve.wait_ge(s_ob, b + 1)
                        ins = nc.vector.scalar_tensor_tensor(row, out[:, 0:D], g.tg[:, gate:gate + 1], row,
                                                             ALU.mult, ALU.add)
                        ins.then_inc(Dv.emptied, 1)

            walk(None, pre_ch, opening)
            with dve.Fori(0, B) as b:
                ch = Chain(dve, s_vch, per, b, pre_ch.n)
                walk(b, ch, script)
                ch.done()


class Banks:

    def __init__(self, g, banks, name, per):
        self.banks, self.per = banks, per
        self.filled, self.emptied = g.semaphore(name + "_filled"), g.semaphore(name + "_emptied")
        self.i = 0

    def grant(self, eng):
        eng.sem_inc(self.emptied, len(self.banks))

    def start(self, b):
        self.i, self.b = 0, b

    def to_fill(self, pe):
        n, i = len(self.banks), self.i
        self.i += 1
        pe.wait_ge(self.emptied, self.b * self.per + (i + 1 if self.per % n == 0 else max(i + 1, n)))
        return self.banks[i % n]

    def to_empty(self, eng):
        self.i += 1
        eng.wait_ge(self.filled, self.b * self.per + self.i)
        return self.banks[(self.i - 1) % len(self.banks)]

    def end(self):
        assert self.i == self.per, f"the fills of a turn are {self.i}"


def turn_to_columns(nc, pe, banks, XN, ident):
    for c in range(DC):
        out = banks.to_fill(pe)
        for t in range(T):
            last = pe.transpose(out[:, t * P:(t + 1) * P], XN[:, t, c * P:(c + 1) * P], ident)
        last.then_inc(banks.filled, 1)


def statistics(nc, g, ctx, pre):
    return {n: ctx.enter_context(nc.sbuf_tensor(pre + n, [P, w], F32))
            for n, w in (("six", 6 * T), ("mv", 2 * T), ("y", T), ("t", T))} | {"beat": g.semaphore(pre + "beat")}


def low_rank_ffn_stage(nc, g, dr):
    R1, FF = dr["L0_V1"].shape
    FC = FF // P
    with ExitStack() as ctx:
        def sb(name, shape, dt=F32):
            return ctx.enter_context(nc.sbuf_tensor("l0f_" + name, shape, dt))

        def sem(name):
            return g.semaphore("l0f_" + name)

        u1, v1 = sb("u1", [P, DC, R1]), sb("v1", [P, FF])
        u2, v2 = sb("u2", [P, FC, R1]), sb("v2", [P, D])
        b1 = sb("b1", [P, FC])
        XN, XT = sb("XN", [P, T, D]), sb("XT", [P, DC, S])
        LR, HR = sb("LR", [P, S]), sb("HR", [P, S])
        H = sb("H", [P, FC, S])
        st = statistics(nc, g, ctx, "l0f_")
        D_PER, A_PER = DC + 2 + T, FC
        dbanks = Banks(g, [ctx.enter_context(nc.psum_tensor(f"l0f_d{i}", [P, 512], F32)) for i in range(2)], "l0f_d", D_PER)
        abanks = Banks(g, [ctx.enter_context(nc.psum_tensor(f"l0f_a{i}", [P, 512], F32)) for i in range(4)], "l0f_a", A_PER)
        s_w, s_pad, s_v, s_xn = sem("weights"), sem("pads"), sem("chain"), sem("xn")
        loads = [(u1[:, :, :], dr["L0_U1"].rearrange("(c p) r -> p c r", p=P)), (v1[0:R1, :], dr["L0_V1"]),
                 (u2[:, :, :], dr["L0_U2"].rearrange("(c p) r -> p c r", p=P)), (v2[0:R1, :], dr["L0_V2"]),
                 (v2[R1:R1 + 1, :], dr["L0_b2"].rearrange("(o n) -> o n", o=1))]
        b1v = dr["L0_b1"].rearrange("(c p o) -> c p o", p=P, o=1)
        loads += [(b1[:, c:c + 1], b1v[c]) for c in range(FC)]
        W_ALL = 16 * len(loads)
        block = ctx.enter_context(nc.Block())

        @block.sync
        def _(sp):
            sp.wait_ge(s_pad, 2)
            for dst, src in loads:
                sp.dma_start(dst, src).then_inc(s_w, 16)

        @block.vector
        def _(dve):
            nc.vector.memset(v1[:, :], 0.0).then_inc(s_pad, 1)
            nc.vector.memset(v2[:, :], 0.0).then_inc(s_pad, 1)
            ch0 = Chain(dve, s_v)
            ch0.step(nc.vector.memset(LR[:, :], 0.0))
            ch0.link(nc.vector.memset(HR[:, :], 0.0))
            ch0.link(nc.vector.memset(HR[R1:R1 + 1, :], 1.0))
            dbanks.grant(dve)

            def norm(ch, b, off):
                layer_norm(nc, ch, off, lambda t: XN[:, t, :], st)
                dve.sem_inc(s_xn, 1)

            norm(ch0, 0, lambda t: g.X[:, t * D:(t + 1) * D])
            with dve.Fori(0, B) as b:
                ch = Chain(dve, s_v, LN_STEPS, b, ch0.n)
                dbanks.start(b)
                for c in range(DC):
                    nc.vector.tensor_copy(XT[:, c, :], dbanks.to_empty(dve)[:, :]).then_inc(dbanks.emptied, 1)
                nc.vector.tensor_copy(LR[0:R1, :], dbanks.to_empty(dve)[0:R1, :]).then_inc(dbanks.emptied, 1)
                norm(ch, b, lambda t: g.X[:, bass.ds(b * ROW + (ROW + t * D), D)])
                nc.vector.tensor_copy(HR[0:R1, :], dbanks.to_empty(dve)[0:R1, :]).then_inc(dbanks.emptied, 1)
                for t in range(T):
                    row = g.X[:, bass.ds(b * ROW + t * D, D)]
                    nc.vector.scalar_tensor_tensor(row, dbanks.to_empty(dve)[:, 0:D], g.tg[:, 4:5], row,
                                                   ALU.mult, ALU.add).then_inc(dbanks.emptied, 1)
                dbanks.end()
                ch.done()

        @block.scalar
        def _(act):
            abanks.grant(act)
            act.wait_ge(s_w, W_ALL)
            with act.Fori(0, B) as b:
                abanks.start(b)
                for f in range(FC):
                    nc.scalar.activation(H[:, f, :], abanks.to_empty(act)[:, :], ACT.Gelu_apprx_tanh,
                                         bias=b1[:, f:f + 1]).then_inc(abanks.emptied, 1)
                abanks.end()

        @block.tensor
        def _(pe):
            pe.wait_ge(s_w, W_ALL)
            with pe.Fori(0, B) as b:
                dbanks.start(b)
                abanks.start(b)
                pe.wait_ge(s_xn, b + 1)
                turn_to_columns(nc, pe, dbanks, XN, g.ident[:, :])
                out = dbanks.to_fill(pe)
                for c in range(DC):
                    pe.wait_ge(dbanks.emptied, b * D_PER + c + 3)
                    last = pe.matmul(out[0:R1, :], u1[:, c, :], XT[:, c, :], start=c == 0, stop=c == DC - 1)
                last.then_inc(dbanks.filled, 1)
                pe.wait_ge(dbanks.emptied, b * D_PER + DC + 3)
                for f in range(FC):
                    pe.matmul(abanks.to_fill(pe)[:, :], v1[:, f * P:(f + 1) * P], LR[:, :],
                              start=True, stop=True).then_inc(abanks.filled, 1)
                out = dbanks.to_fill(pe)
                for f in range(FC):
                    pe.wait_ge(abanks.emptied, b * A_PER + f + 5)
                    last = pe.matmul(out[0:R1, :], u2[:, f, :], H[:, f, :], start=f == 0, stop=f == FC - 1)
                last.then_inc(dbanks.filled, 1)
                pe.wait_ge(dbanks.emptied, b * D_PER + DC + 4)
                for t in range(T):
                    pe.matmul(dbanks.to_fill(pe)[:, 0:D], HR[:, t * P:(t + 1) * P], v2[:, :],
                              start=True, stop=True).then_inc(dbanks.filled, 1)


TOP2_STEPS = 5 * T + 8


def top2_gates(nc, dve, ch, E, logits, bias, tg, tk, ask_exp, got_exp, emptied):
    L, M8, I8, IF, C = tk["L"], tk["M8"], tk["I8"], tk["IF"], tk["C"]
    for t in range(T):
        ch.step(nc.vector.tensor_tensor(L[:, 8 * t:8 * t + E], logits[:, t * E:(t + 1) * E], bias, ALU.add))
    ch.settle()
    dve.sem_inc(emptied, 1)
    for t in range(T):
        ch.step(nc.vector.max(M8[:, 8 * t:8 * t + 8], L[:, 8 * t:8 * t + 8]))
    ch.settle()
    m = M8[:, :].rearrange("p (t k) -> p t k", k=8)
    ch.link(nc.vector.tensor_tensor(tk["d"][:, :], m[:, :, 1], m[:, :, 0], ALU.subtract))
    dve.sem_inc(ask_exp, 1)
    for t in range(T):
        ch.step(nc.vector.max_index(I8[:, 8 * t:8 * t + 8], M8[:, 8 * t:8 * t + 8], L[:, 8 * t:8 * t + 8]))
    ch.settle()
    ch.link(nc.vector.tensor_copy(IF[:, :], I8[:, :]))
    got_exp()
    w0, w1, e = tk["w0"], tk["w1"], tk["e"]
    ch.link(nc.vector.tensor_scalar(w0[:, :], e[:, :], 1.0, None, ALU.add))
    ch.link(nc.vector.reciprocal(w0[:, :], w0[:, :]))
    ch.link(nc.vector.tensor_tensor(w1[:, :], e[:, :], w0[:, :], ALU.mult))
    ch.link(nc.vector.tensor_scalar(w0[:, :], w0[:, :], tg, None, ALU.mult))
    ch.link(nc.vector.tensor_scalar(w1[:, :], w1[:, :], tg, None, ALU.mult))
    for t in range(T):
        ch.step(nc.vector.tensor_scalar(C[:, t, :], tk["iota"][:, 0:E], IF[:, 8 * t:8 * t + 1], w0[:, t:t + 1],
                                        ALU.is_equal, ALU.mult))
        ch.step(nc.vector.tensor_scalar(tk["C2"][:, t, :], tk["iota"][:, 0:E], IF[:, 8 * t + 1:8 * t + 2],
                                        w1[:, t:t + 1], ALU.is_equal, ALU.mult))
    ch.settle()
    ch.link(nc.vector.tensor_tensor(C[:, :, :], C[:, :, :], tk["C2"][:, :, :], ALU.add))


def top2_buffers(nc, ctx, pre, E):
    def sb(name, shape, dt=F32):
        return ctx.enter_context(nc.sbuf_tensor(pre + name, shape, dt))
    return {"L": sb("L", [P, 8 * T]), "M8": sb("M8", [P, 8 * T]), "I8": sb("I8", [P, 8 * T], mybir.dt.uint32),
            "IF": sb("IF", [P, 8 * T]), "C": sb("C", [P, T, E]), "C2": sb("C2", [P, T, E]), "d": sb("d", [P, T]),
            "e": sb("e", [P, T]), "w0": sb("gate0", [P, T]), "w1": sb("gate1", [P, T]), "iota": sb("iota", [P, 8])}


def top2_gelu_stage(nc, g, dr):
    E, _, HID = dr["L2_W1"].shape
    HC = HID // P
    with ExitStack() as ctx:
        def sb(name, shape, dt=F32):
            return ctx.enter_context(nc.sbuf_tensor("l2f_" + name, shape, dt))

        def sem(name):
            return g.semaphore("l2f_" + name)

        wg, bg = sb("wg", [P, DC, E]), sb("bg", [P, E])
        w1, w2 = sb("w1", [P, E, DC, HID]), sb("w2", [P, E, HC, D])
        b1, b2 = sb("b1", [P, E, HC]), sb("b2", [P, E, D])
        XN, XT = sb("XN", [P, T, D]), sb("XT", [P, DC, S])
        H = sb("H", [P, 2, HC, S])
        st = statistics(nc, g, ctx, "l2f_")
        tk = top2_buffers(nc, ctx, "l2f_", E)
        D_PER, A_PER = DC + 1 + E * 2, E * HC
        dbanks = Banks(g, [ctx.enter_context(nc.psum_tensor(f"l2f_d{i}", [P, 512], F32)) for i in range(3)], "l2f_d", D_PER)
        abanks = Banks(g, [ctx.enter_context(nc.psum_tensor(f"l2f_a{i}", [P, 512], F32)) for i in range(4)], "l2f_a", A_PER)
        s_w, s_v, s_xn = sem("weights"), sem("chain"), sem("xn")
        s_diff, s_exp = sem("diff"), sem("exp")
        loads = [(wg[:, :, :], dr["L2_Wg"].rearrange("(c p) e -> p c e", p=P)),
                 (bg[:, :], dr["L2_bg"].rearrange("(o e) -> o e", o=1).to_broadcast([P, E])),
                 (tk["iota"][:, :], dr["iota8"])]
        for e in range(E):
            loads += [(w1[:, e, :, :], dr["L2_W1"][e].rearrange("(c p) h -> p c h", p=P)),
                      (w2[:, e, :, :], dr["L2_W2"][e].rearrange("(c p) d -> p c d", p=P)),
                      (b2[:, e, :], dr["L2_b2"][e:e + 1, :].to_broadcast([P, D]))]
            loads += [(b1[:, e, c:c + 1], dr["L2_b1"][e].rearrange("(c p o) -> c p o", p=P, o=1)[c]) for c in range(HC)]
        W_ALL = 16 * len(loads)
        block = ctx.enter_context(nc.Block())

        @block.sync
        def _(sp):
            for dst, src in loads:
                sp.dma_start(dst, src).then_inc(s_w, 16)

        @block.vector
        def _(dve):
            ch0 = Chain(dve, s_v)
            ch0.link(nc.vector.memset(tk["L"][:, :], -3e38))
            dbanks.grant(dve)

            def norm(ch, off):
                layer_norm(nc, ch, off, lambda t: XN[:, t, :], st)
                dve.sem_inc(s_xn, 1)

            norm(ch0, lambda t: g.X[:, t * D:(t + 1) * D])
            dve.wait_ge(s_w, W_ALL)
            with dve.Fori(0, B) as b:
                ch = Chain(dve, s_v, TOP2_STEPS + LN_STEPS + 2 * E * T, b, ch0.n)
                dbanks.start(b)
                for c in range(DC):
                    nc.vector.tensor_copy(XT[:, c, :], dbanks.to_empty(dve)[:, :]).then_inc(dbanks.emptied, 1)
                logits = dbanks.to_empty(dve)
                top2_gates(nc, dve, ch, E, logits, bg[:, :], g.tg[:, 6:7], tk, s_diff,
                           lambda: dve.wait_ge(s_exp, b + 1), dbanks.emptied)
                rows = [g.X[:, bass.ds(b * ROW + t * D, D)] for t in range(T)]
                for e in range(E):
                    for t in range(T):
                        ch.step(nc.vector.scalar_tensor_tensor(rows[t], b2[:, e, :], tk["C"][:, t, e:e + 1], rows[t],
                                                               ALU.mult, ALU.add))
                    if e == 1:
                        norm(ch, lambda t: g.X[:, bass.ds(b * ROW + (ROW + t * D), D)])
                    ch.settle()
                    for t in range(T):
                        if t % 2 == 0:
                            out = dbanks.to_empty(dve)
                        ch.step(nc.vector.scalar_tensor_tensor(rows[t], out[:, (t % 2) * D:(t % 2) * D + D],
                                                               tk["C"][:, t, e:e + 1], rows[t], ALU.mult, ALU.add))
                        if t % 2:
                            ch.settle()
                            dve.sem_inc(dbanks.emptied, 1)
                dbanks.end()
                ch.done()

        @block.scalar
        def _(act):
            abanks.grant(act)
            act.wait_ge(s_w, W_ALL)
            with act.Fori(0, B) as b:
                abanks.start(b)
                act.wait_ge(s_diff, b + 1)
                nc.scalar.activation(tk["e"][:, :], tk["d"][:, :], ACT.Exp).then_inc(s_exp, 1)
                for e in range(E):
                    for c in range(HC):
                        out = abanks.to_empty(act)
                        if e >= 2 and c == 0:
                            act.wait_ge(dbanks.filled, b * D_PER + DC + 1 + 2 * (e - 1))
                        nc.scalar.activation(H[:, e % 2, c, :], out[:, :], ACT.Gelu,
                                             bias=b1[:, e, c:c + 1]).then_inc(abanks.emptied, 1)
                abanks.end()

        @block.tensor
        def _(pe):
            pe.wait_ge(s_w, W_ALL)
            with pe.Fori(0, B) as b:
                dbanks.start(b)
                abanks.start(b)
                pe.wait_ge(s_xn, b + 1)
                turn_to_columns(nc, pe, dbanks, XN, g.ident[:, :])
                pe.wait_ge(dbanks.emptied, b * D_PER + DC + 3)
                out = dbanks.to_fill(pe)
                for t in range(T):
                    for c in range(DC):
                        last = pe.matmul(out[:, t * E:(t + 1) * E], XT[:, c, t * P:(t + 1) * P], wg[:, c, :],
                                         start=c == 0, stop=c == DC - 1)
                last.then_inc(dbanks.filled, 1)
                for e in range(E + 1):
                    if e < E:
                        for h in range(HC):
                            out = abanks.to_fill(pe)
                            for c in range(DC):
                                last = pe.matmul(out[:, :], w1[:, e, c, h * P:(h + 1) * P], XT[:, c, :],
                                                 start=c == 0, stop=c == DC - 1)
                            last.then_inc(abanks.filled, 1)
                    if e >= 1:
                        f = e - 1
                        pe.wait_ge(abanks.emptied, b * A_PER + (f + 1) * HC + 4)
                        for t in range(T):
                            if t % 2 == 0:
                                out = dbanks.to_fill(pe)
                            for c in range(HC):
                                last = pe.matmul(out[:, (t % 2) * D:(t % 2) * D + D], H[:, f % 2, c, t * P:(t + 1) * P],
                                                 w2[:, f, c, :], start=c == 0, stop=c == HC - 1,
                                                 skip_group_check=True)
                            if t % 2:
                                last.then_inc(dbanks.filled, 1)
                dbanks.end()


def top2_silu_stage(nc, g, dr):
    E, _, HID = dr["L3_routed_w1"].shape
    SH = dr["L3_shared_w1"].shape[0]
    EA = E + SH
    assert HID == P
    with ExitStack() as ctx:
        def sb(name, shape, dt=F32):
            return ctx.enter_context(nc.sbuf_tensor("l3f_" + name, shape, dt))

        def sem(name):
            return g.semaphore("l3f_" + name)

        wg, bg = sb("wg", [P, DC, E]), sb("bg", [P, E])
        w1, w3, w2 = sb("w1", [P, EA, DC, HID]), sb("w3", [P, EA, DC, HID]), sb("w2", [P, EA, D])
        XN, XT = sb("XN", [P, T, D]), sb("XT", [P, DC, S])
        SG, H = sb("SG", [P, 2, S]), sb("H", [P, 3, S])
        st = statistics(nc, g, ctx, "l3f_")
        tk = top2_buffers(nc, ctx, "l3f_", E)
        D_PER, A_PER = DC + 1 + EA + (E + 1) * 2, EA
        dbanks = Banks(g, [ctx.enter_context(nc.psum_tensor(f"l3f_d{i}", [P, 512], F32)) for i in range(4)], "l3f_d", D_PER)
        abanks = Banks(g, [ctx.enter_context(nc.psum_tensor(f"l3f_a{i}", [P, 512], F32)) for i in range(2)], "l3f_a", A_PER)
        s_w, s_v, s_xn = sem("weights"), sem("chain"), sem("xn")
        s_diff, s_exp = sem("diff"), sem("exp")
        loads = [(wg[:, :, :], dr["L3_router_w"].rearrange("(c p) e -> p c e", p=P)),
                 (bg[:, :], dr["L3_router_b"].rearrange("(o e) -> o e", o=1).to_broadcast([P, E])),
                 (tk["iota"][:, :], dr["iota8"])]
        for n, w in (("w1", w1), ("w3", w3)):
            for e in range(EA):
                src = dr[f"L3_routed_{n}"][e] if e < E else dr[f"L3_shared_{n}"][e - E]
                loads += [(w[:, e, :, :], src.rearrange("(c p) h -> p c h", p=P))]
        loads += [(w2[:, 0:E, :], dr["L3_routed_w2"].rearrange("e h d -> h e d")),
                  (w2[:, E:EA, :], dr["L3_shared_w2"].rearrange("e h d -> h e d"))]
        W_ALL = 16 * len(loads)
        block = ctx.enter_context(nc.Block())
        def h_at(e):
            return DC + 1 + 1 + e + 2 * min(max(e - 1, 0), E)

        out_turns = [[e] for e in range(E)] + [list(range(E, EA))]

        @block.sync
        def _(sp):
            for dst, src in loads:
                sp.dma_start(dst, src).then_inc(s_w, 16)

        @block.vector
        def _(dve):
            ch0 = Chain(dve, s_v)
            ch0.link(nc.vector.memset(tk["L"][:, :], -3e38))
            dbanks.grant(dve)

            def norm(ch, off):
                layer_norm(nc, ch, off, lambda t: XN[:, t, :], st)
                dve.sem_inc(s_xn, 1)

            norm(ch0, lambda t: g.X[:, t * D:(t + 1) * D])
            dve.wait_ge(s_w, W_ALL)
            with dve.Fori(0, B) as b:
                ch = Chain(dve, s_v, TOP2_STEPS + LN_STEPS + (E + 1) * T, b, ch0.n)
                dbanks.start(b)
                for c in range(DC):
                    nc.vector.tensor_copy(XT[:, c, :], dbanks.to_empty(dve)[:, :]).then_inc(dbanks.emptied, 1)
                logits = dbanks.to_empty(dve)
                top2_gates(nc, dve, ch, E, logits, bg[:, :], g.tg[:, 7:8], tk, s_diff,
                           lambda: dve.wait_ge(s_exp, b + 1), dbanks.emptied)
                rows = [g.X[:, bass.ds(b * ROW + t * D, D)] for t in range(T)]

                def product(e):
                    out = dbanks.to_empty(dve)
                    dve.wait_ge(abanks.emptied, b * A_PER + e + 1 + 2)
                    nc.vector.tensor_tensor(H[:, e % 3, :], out[:, :], SG[:, e % 2, :],
                                            ALU.mult).then_inc(dbanks.emptied, 1)

                def add(turn):
                    e = turn[0]
                    for t in range(T):
                        if t % 2 == 0:
                            out = dbanks.to_empty(dve)
                        gate = tk["C"][:, t, e:e + 1] if e < E else g.tg[:, 7:8]
                        ch.step(nc.vector.scalar_tensor_tensor(rows[t], out[:, (t % 2) * D:(t % 2) * D + D], gate,
                                                               rows[t], ALU.mult, ALU.add))
                        if t % 2:
                            ch.settle()
                            dve.sem_inc(dbanks.emptied, 1)

                for e in range(EA):
                    product(e)
                    if 1 <= e <= E:
                        add(out_turns[e - 1])
                    if e == 2:
                        norm(ch, lambda t: g.X[:, bass.ds(b * ROW + (ROW + t * D), D)])
                add(out_turns[E])
                dbanks.end()
                ch.done()

        @block.scalar
        def _(act):
            abanks.grant(act)
            with act.Fori(0, B) as b:
                abanks.start(b)
                act.wait_ge(s_diff, b + 1)
                nc.scalar.activation(tk["e"][:, :], tk["d"][:, :], ACT.Exp).then_inc(s_exp, 1)
                for e in range(EA):
                    out = abanks.to_empty(act)
                    if e >= 2:
                        act.wait_ge(dbanks.emptied, b * D_PER + 4 + h_at(e - 2))
                    nc.scalar.activation(SG[:, e % 2, :], out[:, :], ACT.Silu).then_inc(abanks.emptied, 1)
                abanks.end()

        @block.tensor
        def _(pe):
            pe.wait_ge(s_w, W_ALL)
            with pe.Fori(0, B) as b:
                dbanks.start(b)
                abanks.start(b)
                pe.wait_ge(s_xn, b + 1)
                turn_to_columns(nc, pe, dbanks, XN, g.ident[:, :])
                pe.wait_ge(dbanks.emptied, b * D_PER + DC + 4)
                out = dbanks.to_fill(pe)
                for t in range(T):
                    for c in range(DC):
                        last = pe.matmul(out[:, t * E:(t + 1) * E], XT[:, c, t * P:(t + 1) * P], wg[:, c, :],
                                         start=c == 0, stop=c == DC - 1)
                last.then_inc(dbanks.filled, 1)

                def expert_in(e):
                    for w, banks in ((w1, abanks), (w3, dbanks)):
                        out = banks.to_fill(pe)
                        for c in range(DC):
                            last = pe.matmul(out[:, :], w[:, e, c, :], XT[:, c, :], start=c == 0, stop=c == DC - 1)
                        last.then_inc(banks.filled, 1)

                def expert_out(turn):
                    pe.wait_ge(dbanks.emptied, b * D_PER + 4 + h_at(turn[-1]))
                    for t in range(T):
                        if t % 2 == 0:
                            out = dbanks.to_fill(pe)
                        for e in turn:
                            last = pe.matmul(out[:, (t % 2) * D:(t % 2) * D + D], H[:, e % 3, t * P:(t + 1) * P],
                                             w2[:, e, :], start=e == turn[0], stop=e == turn[-1], skip_group_check=True)
                        if t % 2:
                            last.then_inc(dbanks.filled, 1)

                for e in range(EA):
                    expert_in(e)
                    if 1 <= e <= E:
                        expert_out(out_turns[e - 1])
                expert_out(out_turns[E])
                dbanks.end()


def soft_moe_stage(nc, g, dr):
    NE, _, HO = dr["L1_expert_w"].shape
    SL = dr["L1_phiT"].shape[1]
    NP = SL // NE
    SC = SL // P
    EC = P // NP
    QW = 512
    assert HO == D
    with ExitStack() as outer:
        def keep(name, shape, dt=F32):
            return outer.enter_context(nc.sbuf_tensor("l1f_" + name, shape, dt))

        phi = keep("phi", [P, DC, SL])
        biasb = keep("biasb", [P, SL], BF16)
        onesb = keep("onesb", [P, P], BF16)
        zeros = keep("zeros", [P, QW], BF16)
        XS = keep("XS", [P, SC, D])
        XN = keep("XN", [P, T, D])
        XT = keep("XT", [P, DC, S])
        st = statistics(nc, g, outer, "l1f_")

        def logits_of(pe, out, t, q, xT=XT):
            for c in range(DC):
                pe.matmul(out, xT[:, c, t * P:(t + 1) * P], phi[:, c, q * QW:(q + 1) * QW], start=c == 0, stop=False)
            return pe.matmul(out, onesb[:, :], biasb[:, q * QW:(q + 1) * QW], start=False, stop=True)

        with ExitStack() as ctx:
            def sb(name, shape, dt=F32):
                return ctx.enter_context(nc.sbuf_tensor("l1a_" + name, shape, dt))

            def sem(name):
                return g.semaphore("l1a_" + name)

            brow, part = sb("brow", [1, SL]), sb("part", [1, SL], BF16)
            XN2, XT2 = sb("XN2", [P, 2, T, D]), sb("XT2", [P, 2, DC, S])
            RING, LEAD = 4, 3
            LC, DW = sb("LC", [P, RING, QW]), sb("DW", [P, RING, QW])
            m, r = sb("m", [P, QW // NP]), sb("r", [P, RING, QW // NP])
            TILES = T * 2
            HALF_TILES = B * TILES + LEAD
            BEFORE, PER_BATCH = DC + LEAD, DC + TILES
            HALF_FILLS = BEFORE + B * PER_BATCH
            dbanks = [ctx.enter_context(nc.psum_tensor(f"l1a_d{i}", [P, 512], F32)) for i in range(4)]
            acc = ctx.enter_context(nc.psum_tensor("l1a_acc", [P, 4, 512], F32))
            s_df, s_de = sem("d_filled"), sem("d_emptied")
            s_w, s_v, s_xn = sem("weights"), sem("chain"), sem("xn")
            s_bias = sem("bias")
            s_sub, s_exp, s_sum, s_dw, s_use = sem("shifted"), sem("exp"), sem("sums"), sem("weights_d"), sem("used")
            s_acc, s_out = sem("acc_full"), sem("acc_out")
            ngroup = QW // NP
            XT_AT = LEAD + 1
            block = ctx.enter_context(nc.Block())

            def in_slots(ap):
                return ap.rearrange("p (n q) -> p n q", q=NP)

            def fill_of(k):
                return k + (DC if k >= XT_AT else 0)

            @block.sync
            def _(sp):
                sp.dma_start(brow[0:1, :], dr["L1_phi_b"].rearrange("(o n) -> o n", o=1)).then_inc(s_w, 16)
                sp.dma_start(phi[:, :, :], dr["L1_phiT"].rearrange("(c p) n -> p c n", p=P)).then_inc(s_w, 16)

            @block.vector
            def _(dve):
                ch0 = Chain(dve, s_v)
                ch0.step(nc.vector.memset(zeros[:, :], 0.0))
                ch0.step(nc.vector.memset(onesb[:, :], 1.0))
                ch0.link(nc.vector.memset(biasb[:, :], 0.0))
                dve.sem_inc(s_de, 4)
                dve.wait_ge(s_w, 32)
                for k, row in enumerate((0, 32, 64)):
                    ch0.link(nc.vector.tensor_copy(part[:, :], brow[:, :]))
                    ch0.link(nc.vector.tensor_copy(biasb[row:row + 1, :], part[:, :]))
                    ch0.link(nc.vector.tensor_tensor(brow[:, :], brow[:, :], part[:, :], ALU.subtract))

                dve.sem_inc(s_bias, 1)

                def turned(fill, u, c):
                    dve.wait_ge(s_df, fill[0] + 1)
                    nc.vector.tensor_copy(XT2[:, u, c, :], dbanks[fill[1] % 4][:, :]).then_inc(s_de, 1)

                def shift(ch, fill, n, i):
                    dve.wait_ge(s_df, fill[0] + 1)
                    out = in_slots(dbanks[fill[1] % 4][:, :])
                    ch.link(nc.vector.tensor_reduce(m[:, :], out, AX.X, ALU.max))
                    dve.wait_ge(s_dw, n + 1)
                    ch.link(nc.vector.tensor_tensor(in_slots(LC[:, i % RING, :]), out,
                                                    m[:, :].unsqueeze(2).to_broadcast([P, ngroup, NP]), ALU.subtract))
                    dve.sem_inc(s_de, 1)
                    dve.sem_inc(s_sub, 1)

                def total(ch, n, i):
                    dve.wait_ge(s_exp, n + 1)
                    ch.link(nc.vector.tensor_reduce(r[:, i % RING, :], in_slots(LC[:, i % RING, :]), AX.X, ALU.add))
                    nc.vector.reciprocal(r[:, i % RING, :], r[:, i % RING, :]).then_inc(s_sum, 1)

                for half in range(2):
                    tile0, fill0 = half * HALF_TILES, half * HALF_FILLS
                    if half:
                        dve.wait_ge(s_use, tile0 + RING)
                    layer_norm(nc, ch0, lambda t: g.X[:, t * D:(t + 1) * D], lambda t: XN2[:, 0, t, :], st)
                    dve.sem_inc(s_xn, 1)
                    for c in range(DC):
                        turned((fill0 + c, c), 0, c)
                    for i in range(LEAD):
                        shift(ch0, (fill0 + DC + i, DC + i), tile0 + i, i)
                        if i:
                            total(ch0, tile0 + i - 1, i - 1)
                    per = 2 * (LN_STEPS + 3 * TILES)
                    with dve.Fori(0, B // 2) as pair:
                        ch = Chain(dve, s_v, per, pair, ch0.n)
                        for u in range(2):
                            tiles = pair * (2 * TILES) + (tile0 + u * TILES)
                            fills = pair * (2 * PER_BATCH) + (fill0 + BEFORE + u * PER_BATCH)
                            place = BEFORE + u * PER_BATCH
                            pieces = layer_norm_pieces(
                                nc, ch, lambda t: g.X[:, bass.ds(pair * (2 * ROW) + ((u + 1) * ROW + t * D), D)],
                                lambda t: XN2[:, 1 - u, t, :], st)
                            dve.wait_ge(s_use, tiles + RING)
                            for k in range(TILES):
                                if k == XT_AT:
                                    for c in range(DC):
                                        turned((fills + (k + c), place + k + c), 1 - u, c)
                                i = u * TILES + k + LEAD
                                at = fill_of(k)
                                shift(ch, (fills + at, place + at), tiles + (k + LEAD), i)
                                total(ch, tiles + (k + LEAD - 1), i - 1)
                                for piece in pieces[2 * k:2 * k + 2]:
                                    piece()
                                if k == 2:
                                    dve.sem_inc(s_xn, 1)
                        ch.done()
                    ch0.n += B // 2 * per
                    total(ch0, tile0 + HALF_TILES - 1, HALF_TILES - 1)
                    dve.wait_ge(s_acc, half + 1)
                    for i in range(4):
                        ins = nc.vector.tensor_copy(XS[:, half * 8 + 2 * i:half * 8 + 2 * i + 2, :],
                                                    acc[:, i, :].rearrange("p (a d) -> p a d", a=2))
                    ins.then_inc(s_out, 1)

            @block.scalar
            def _(act):
                def exps(n, i):
                    act.wait_ge(s_sub, n + 1)
                    nc.scalar.activation(LC[:, i % RING, :], LC[:, i % RING, :], ACT.Exp).then_inc(s_exp, 1)

                for half in range(2):
                    for i in range(LEAD):
                        exps(half * HALF_TILES + i, i)
                    with act.Fori(0, B) as b:
                        for k in range(TILES):
                            exps(b * TILES + (half * HALF_TILES + LEAD + k), LEAD + k)

            @block.gpsimd
            def _(pool):
                def normalise(n, i):
                    pool.wait_ge(s_sum, n + 1)
                    if i >= LEAD:
                        pool.wait_ge(s_use, n + 1)
                    nc.gpsimd.tensor_tensor(in_slots(DW[:, i % RING, :]), in_slots(LC[:, i % RING, :]),
                                            r[:, i % RING, :].unsqueeze(2).to_broadcast([P, ngroup, NP]),
                                            ALU.mult).then_inc(s_dw, 1)

                pool.sem_inc(s_dw, RING)
                for half in range(2):
                    for i in range(LEAD):
                        normalise(half * HALF_TILES + i, i)
                    with pool.Fori(0, B) as b:
                        for k in range(TILES):
                            normalise(b * TILES + (half * HALF_TILES + LEAD + k), LEAD + k)

            @block.tensor
            def _(pe):
                def turn(fill, u):
                    for c in range(DC):
                        pe.wait_ge(s_de, fill[0] + (c + 1))
                        out = dbanks[(fill[1] + c) % 4]
                        for t in range(T):
                            last = pe.transpose(out[:, t * P:(t + 1) * P], XN2[:, u, t, c * P:(c + 1) * P],
                                                g.ident[:, :])
                        last.then_inc(s_df, 1)

                def logits(fill, u, k, half):
                    pe.wait_ge(s_de, fill[0] + 1)
                    logits_of(pe, dbanks[fill[1] % 4][:, :], k // 2, half * 2 + k % 2, XT2[:, u, :, :])\
                        .then_inc(s_df, 1)

                pe.sem_inc(s_use, RING)
                pe.wait_ge(s_w, 32)
                pe.wait_ge(s_bias, 1)
                for half in range(2):
                    tile0, fill0 = half * HALF_TILES, half * HALF_FILLS
                    if half:
                        pe.wait_ge(s_out, 1)
                        pe.wait_ge(s_de, fill0 + 4)
                    pe.wait_ge(s_xn, half * (B + 1) + 1)
                    for i in range(4):
                        pe.matmul(acc[:, i, :], zeros[:, 0:P], zeros[:, :], start=True, stop=False, skip_group_check=True)
                    turn((fill0, 0), 0)
                    pe.wait_ge(s_de, fill0 + DC + 4)
                    for i in range(LEAD):
                        logits((fill0 + DC + i, DC + i), 0, i, half)
                    with pe.Fori(0, B // 2) as pair:
                        for u in range(2):
                            tiles = pair * (2 * TILES) + (tile0 + u * TILES)
                            fills = pair * (2 * PER_BATCH) + (fill0 + BEFORE + u * PER_BATCH)
                            place = BEFORE + u * PER_BATCH
                            for k in range(TILES):
                                if k == XT_AT:
                                    pe.wait_ge(s_xn, pair * 2 + (half * (B + 1) + u + 2))
                                    turn((fills + k, place + k), 1 - u)
                                ahead = k + LEAD
                                if ahead == TILES:
                                    pe.wait_ge(s_de, fills + (XT_AT + DC + 4))
                                logits((fills + fill_of(k), place + fill_of(k)), u if ahead < TILES else 1 - u,
                                       ahead % TILES, half)
                                t, q = k // 2, k % 2
                                pe.wait_ge(s_dw, tiles + (k + RING + 1))
                                for j in range(4):
                                    i = q * 4 + j
                                    last = pe.matmul(acc[:, i // 2, (i % 2) * D:(i % 2) * D + D],
                                                     DW[:, (u * TILES + k) % RING, j * P:(j + 1) * P],
                                                     XN2[:, u, t, :], start=False, stop=False, skip_group_check=True)
                                last.then_inc(s_use, 1)
                    pe.matmul(acc[:, 3, :], zeros[:, 0:P], zeros[:, :], start=False, stop=True,
                              skip_group_check=True).then_inc(s_acc, 1)
                    pe.wait_ge(s_dw, (half + 1) * HALF_TILES + RING)
                    pe.sem_inc(s_use, LEAD)

        with ExitStack() as ctx:
            def sb(name, shape, dt=F32):
                return ctx.enter_context(nc.sbuf_tensor("l1b_" + name, shape, dt))

            def sem(name):
                return g.semaphore("l1b_" + name)

            TURNS = SC // T
            EW = sb("EW", [P, T, EC * DC, HO])
            EB = sb("EB", [P, T, HO])
            ZT = sb("ZT", [P, DC, S])
            dbanks = Banks(g, [ctx.enter_context(nc.psum_tensor(f"l1b_d{i}", [P, 512], F32)) for i in range(4)], "l1b_d", DC + T)
            s_ew, s_eb, s_v, s_xn = [sem(f"experts{t}") for t in range(T)], sem("bias"), sem("chain"), sem("slots")
            s_th = sem("tanh")
            eb = dr["L1_expert_b"]
            block = ctx.enter_context(nc.Block())

            @block.sync
            def _(sp):
                def load(n, t):
                    sp.dma_start(EW[:, t, :, :], n).then_inc(s_ew[t], 16)

                ew_rows = dr["L1_expert_w"].rearrange("n (c p) h -> p (n c) h", p=P)
                for t in range(T):
                    load(ew_rows[:, t * EC * DC:(t + 1) * EC * DC, :], t)
                for t in range(T):
                    for e in range(EC):
                        n = t * EC + e
                        sp.dma_start(EB[e * NP:(e + 1) * NP, t, :], eb[n:n + 1, :].to_broadcast([NP, HO])).then_inc(s_eb, 16)
                with sp.Fori(1, TURNS) as i:
                    for t in range(T):
                        sp.wait_ge(dbanks.filled, i * (DC + T) + (t + 1 + DC - (DC + T)))
                        load(ew_rows[:, bass.ds(i * (T * EC * DC) + t * EC * DC, EC * DC), :], t)
                    for t in range(T):
                        sp.wait_ge(dbanks.emptied, i * (DC + T) + 4)
                        for e in range(EC):
                            sp.dma_start(EB[e * NP:(e + 1) * NP, t, :],
                                         eb[bass.ds(i * (T * EC) + (t * EC + e), 1), :].to_broadcast([NP, HO])).then_inc(s_eb, 16)

            @block.vector
            def _(dve):
                dbanks.grant(dve)
                with dve.Fori(0, TURNS) as i:
                    ch = Chain(dve, s_v, LN_STEPS + T, i)
                    dbanks.start(i)
                    rows = [XS[:, :, :].rearrange("p s d -> p (s d)")[:, bass.ds(i * ROW + t * D, D)] for t in range(T)]
                    for t in range(T):
                        ch.step(nc.vector.tensor_scalar(rows[t], rows[t], -33000.0, 65000.0, ALU.max, ALU.min))
                    ch.settle()
                    layer_norm(nc, ch, lambda t: rows[t], lambda t: XN[:, t, :], st)
                    dve.sem_inc(s_xn, 1)
                    for c in range(DC):
                        nc.vector.tensor_copy(ZT[:, c, :], dbanks.to_empty(dve)[:, :]).then_inc(dbanks.emptied, 1)
                    dve.wait_ge(s_eb, i * (16 * T * EC) + 16 * T * EC)
                    for t in range(T):
                        nc.vector.tensor_tensor(rows[t], dbanks.to_empty(dve)[:, 0:HO], EB[:, t, :],
                                                ALU.add).then_inc(dbanks.emptied, 1)
                    dbanks.end()
                    ch.done()

            @block.scalar
            def _(act):
                with act.Fori(0, TURNS) as i:
                    act.wait_ge(s_xn, i + 1)
                    nc.scalar.activation(XN[:, :, :], XN[:, :, :], ACT.Tanh).then_inc(s_th, 1)

            @block.tensor
            def _(pe):
                with pe.Fori(0, TURNS) as i:
                    dbanks.start(i)
                    pe.wait_ge(s_th, i + 1)
                    turn_to_columns(nc, pe, dbanks, XN, g.ident[:, :])
                    pe.wait_ge(dbanks.emptied, i * (DC + T) + DC + 4)
                    for t in range(T):
                        pe.wait_ge(s_ew[t], i * 16 + 16)
                        out = dbanks.to_fill(pe)
                        for e in range(EC):
                            for c in range(DC):
                                last = pe.matmul(out[e * NP:(e + 1) * NP, 0:HO],
                                                 ZT[:, c, t * P + e * NP:t * P + (e + 1) * NP], EW[:, t, e * DC + c, :],
                                                 start=c == 0, stop=c == DC - 1)
                        last.then_inc(dbanks.filled, 1)
                    dbanks.end()

        with ExitStack() as ctx:
            def sb(name, shape, dt=F32):
                return ctx.enter_context(nc.sbuf_tensor("l1c_" + name, shape, dt))

            def sem(name):
                return g.semaphore("l1c_" + name)

            QB4 = SL // QW
            LC, CW = sb("LC", [P, 2, SL]), sb("CW", [P, SL])
            CT = sb("CT", [P, 2, SC, P])
            m4, m, r = sb("m4", [P, NP, QB4]), sb("m", [P, NP]), sb("r", [P, NP])
            lg = [ctx.enter_context(nc.psum_tensor(f"l1c_lg{q}", [P, QW], F32)) for q in range(QB4)]
            D_PER, A_PER = DC + T, T * QB4
            dbanks = [ctx.enter_context(nc.psum_tensor(f"l1c_d{i}", [P, 512], F32)) for i in range(2)]
            abanks = [ctx.enter_context(nc.psum_tensor(f"l1c_a{i}", [P, 512], F32)) for i in range(2)]
            s_df, s_de, s_af, s_ae = sem("d_filled"), sem("d_emptied"), sem("a_filled"), sem("a_emptied")
            s_v, s_xn, s_lg = sem("chain"), sem("xn"), sem("logits")
            s_sub, s_exp, s_rec, s_cw = sem("shifted"), sem("exp"), sem("inverse"), sem("combine")
            block = ctx.enter_context(nc.Block())

            def by_slot(ap):
                return ap.rearrange("p (n q) -> p q n", q=NP)

            def fills(b):
                return b * D_PER + DC

            D_AT = {("out", 0): 0, ("out", 1): 1, ("out", 2): 2 + DC, ("out", 3): 3 + DC}
            D_AT.update({("xT", c): 2 + c for c in range(DC)})

            @block.vector
            def _(dve):
                dve.sem_inc(s_de, 2)
                dve.sem_inc(s_sub, QB4)

                ch0 = Chain(dve, s_v)
                layer_norm(nc, ch0, lambda t: g.X[:, t * D:(t + 1) * D], lambda t: XN[:, t, :], st)
                dve.sem_inc(s_xn, 1)

                def turned(b, c):
                    dve.wait_ge(s_df, c + 1 if b is None else fills(b) + (D_AT["xT", c] + 1))
                    nc.vector.tensor_copy(XT[:, c, :], dbanks[c % 2][:, :]).then_inc(s_de, 1)

                def weights(n, t, ch):
                    for q in range(QB4):
                        dve.wait_ge(s_lg, n * QB4 + (q + 1))
                        ch.step(nc.vector.tensor_reduce(m4[:, :, q], by_slot(lg[q][:, :]), AX.X, ALU.max))
                    ch.settle()
                    ch.link(nc.vector.tensor_reduce(m[:, :], m4[:, :, :], AX.X, ALU.max))
                    for q in range(QB4):
                        n_q = QW // NP
                        nc.vector.tensor_tensor(LC[:, t % 2, q * QW:(q + 1) * QW].rearrange("p (n q) -> p n q", q=NP),
                                                lg[q][:, :].rearrange("p (n q) -> p n q", q=NP),
                                                m[:, :].unsqueeze(1).to_broadcast([P, n_q, NP]),
                                                ALU.subtract).then_inc(s_sub, 1)

                def total(n, t, ch):
                    dve.wait_ge(s_exp, n * 2 + 2)
                    dve.wait_ge(s_cw, n + 1)
                    ch.link(nc.vector.tensor_reduce(r[:, :], by_slot(LC[:, t % 2, :]), AX.X, ALU.add))
                    nc.vector.reciprocal(r[:, :], r[:, :]).then_inc(s_rec, 1)

                for c in range(DC):
                    turned(None, c)
                weights(0, 0, ch0)
                total(0, 0, ch0)
                per = LN_STEPS + T * (QB4 + 2)
                with dve.Fori(0, B) as b:
                    ch = Chain(dve, s_v, per, b, ch0.n)
                    pieces = layer_norm_pieces(nc, ch, lambda t: g.X[:, bass.ds(b * ROW + (ROW + t * D), D)],
                                               lambda t: XN[:, t, :], st)
                    for t in range(1, T + 1):
                        weights(b * T + t, t, ch)
                        if t == T - 1:
                            for c in range(DC):
                                turned(b, c)
                        total(b * T + t, t, ch)
                        for piece in pieces[3 * t - 3:3 * t]:
                            piece()
                        if t == 2:
                            dve.sem_inc(s_xn, 1)
                        row = g.X[:, bass.ds(b * ROW + (t - 1) * D, D)]
                        at = D_AT["out", t - 1]
                        dve.wait_ge(s_df, fills(b) + (at + 1))
                        nc.vector.scalar_tensor_tensor(row, dbanks[at % 2][:, 0:D], g.tg[:, 5:6], row,
                                                       ALU.mult, ALU.add).then_inc(s_de, 1)
                    ch.done()

            @block.gpsimd
            def _(pool):
                pool.sem_inc(s_cw, 1)

                def normalise(n, t, first=False):
                    if not first:
                        pool.wait_ge(s_af, n * QB4)
                    pool.wait_ge(s_rec, n + 1)
                    nc.gpsimd.tensor_tensor(CW[:, :].rearrange("p (n q) -> p n q", q=NP),
                                            LC[:, t % 2, :].rearrange("p (n q) -> p n q", q=NP),
                                            r[:, :].unsqueeze(1).to_broadcast([P, NE, NP]), ALU.mult).then_inc(s_cw, 1)

                normalise(0, 0, True)
                with pool.Fori(0, B) as b:
                    for t in range(1, T + 1):
                        normalise(b * T + t, t)

            @block.scalar
            def _(act):
                act.sem_inc(s_ae, 2)

                def exps(n, t, half):
                    cols = slice(half * SL // 2, (half + 1) * SL // 2)
                    act.wait_ge(s_sub, n * QB4 + (QB4 + (half + 1) * QB4 // 2))
                    nc.scalar.activation(LC[:, t % 2, cols], LC[:, t % 2, cols], ACT.Exp).then_inc(s_exp, 1)

                def turned(b, t, q):
                    act.wait_ge(s_af, b * A_PER + (t * QB4 + q + 1))
                    nc.scalar.copy(CT[:, t % 2, 4 * q:4 * q + 4, :].rearrange("p s t -> p (s t)"),
                                   abanks[q % 2][:, :]).then_inc(s_ae, 1)

                exps(0, 0, 0)
                exps(0, 0, 1)
                with act.Fori(0, B) as b:
                    for t in range(1, T + 1):
                        for q in range(2):
                            turned(b, t - 1, q)
                        exps(b * T + t, t, 0)
                        for q in range(2, QB4 - 1):
                            turned(b, t - 1, q)
                        exps(b * T + t, t, 1)
                        turned(b, t - 1, QB4 - 1)

            @block.tensor
            def _(pe):
                def turn(b):
                    for c in range(DC):
                        at = c if b is None else D_AT["xT", c]
                        if b is not None or at >= 2:
                            pe.wait_ge(s_de, fills(b) + (at + 1))
                        else:
                            pe.wait_ge(s_de, 2)
                        for t in range(T):
                            last = pe.transpose(dbanks[at % 2][:, t * P:(t + 1) * P], XN[:, t, c * P:(c + 1) * P],
                                                g.ident[:, :])
                        last.then_inc(s_df, 1)

                def logits(n, t):
                    for q in range(QB4):
                        pe.wait_ge(s_sub, n * QB4 + (q + 1))
                        logits_of(pe, lg[q][:, :], t, q).then_inc(s_lg, 1)

                def spread(b, t):
                    at = D_AT["out", t]
                    out = dbanks[at % 2]
                    pe.wait_ge(s_cw, b * T + (t + 2))
                    for q in range(QB4 + 1):
                        if q < QB4:
                            pe.wait_ge(s_ae, b * A_PER + (t * QB4 + q + 1))
                            for k in range(4):
                                s = 4 * q + k
                                last = pe.transpose(abanks[q % 2][:, k * P:(k + 1) * P], CW[:, s * P:(s + 1) * P],
                                                    g.ident[:, :])
                            last.then_inc(s_af, 1)
                        if q == 1:
                            pe.wait_ge(s_de, fills(b) + (at + 1))
                        if q:
                            pe.wait_ge(s_ae, b * A_PER + (t * QB4 + q + 2))
                            for s in range(4 * q - 4, 4 * q):
                                last = pe.matmul(out[:, 0:D], CT[:, t % 2, s, :], XS[:, s, :],
                                                 start=s == 0, stop=s == SC - 1)
                    last.then_inc(s_df, 1)

                pe.wait_ge(s_xn, 1)
                turn(None)
                pe.wait_ge(s_de, DC + 2)
                logits(0, 0)
                with pe.Fori(0, B) as b:
                    for t in range(1, T):
                        logits(b * T + t, t)
                        if t == T - 1:
                            pe.wait_ge(s_xn, b + 2)
                            turn(b)
                        spread(b, t - 1)
                    pe.wait_ge(s_de, fills(b) + (D_AT["xT", DC - 1] + 1 + 2))
                    logits(b * T + T, 0)
                    spread(b, T - 1)


class Shared:

    def __init__(self, nc):
        self.nc, self.held = nc, []

    def semaphore(self, name):
        self.held.append(self.nc.alloc_semaphore(name))
        return self.held[-1]

    def release(self):
        self.nc.clear_and_free_semaphores(self.held)
        self.nc.all_engine_barrier()
        self.held = []


def program(nc, dr, out):
    with ExitStack() as ctx:
        def sb(name, shape, dt=F32):
            return ctx.enter_context(nc.sbuf_tensor(name, shape, dt))

        g = Shared(nc)
        g.X = sb("X", [P, (B + 1) * ROW])
        g.tg = sb("tg", [P, 8])
        g.ident = sb("ident", [P, P])
        g.ident_b = sb("ident_b", [P, P], BF16)

        with nc.Block() as block:
            s_in, s_graw, s_id = (g.semaphore(n) for n in ("x_in", "gates_in", "ident_in"))

            @block.sync
            def _(sp):
                sp.dma_start(g.tg[:, 0:4], dr["g_xattn"].rearrange("(o n) -> o n", o=1).to_broadcast([P, 4])).then_inc(s_graw, 16)
                sp.dma_start(g.tg[:, 4:8], dr["g_ffn"].rearrange("(o n) -> o n", o=1).to_broadcast([P, 4])).then_inc(s_graw, 16)
                sp.dma_start(g.ident[:, :], dr["ident"]).then_inc(s_id, 16)
                sp.dma_start(g.X[:, 0:B * ROW].rearrange("p (n d) -> p n d", d=D),
                             dr["x"].rearrange("(n p) d -> p n d", p=P)).then_inc(s_in, 16)
                sp.wait_ge(s_in, 16)

            @block.scalar
            def _(act):
                act.wait_ge(s_graw, 32)
                nc.scalar.activation(g.tg[:, :], g.tg[:, :], ACT.Tanh)

            @block.vector
            def _(dve):
                nc.vector.memset(g.X[:, B * ROW:], 0.0)
                dve.wait_ge(s_id, 16)
                nc.vector.tensor_copy(g.ident_b[:, :], g.ident[:, :])

        g.release()
        attention_stage(nc, g, "l0x_", dict(ctx=dr["ctx"], wq=dr["L0_wq"], wk=dr["L0_wk"], wkp=dr["L0_wkp"],
                                            wv=dr["L0_wv"], wo=dr["L0_wo"], cos=dr["L0_cos"], sin=dr["L0_sin"],
                                            gamma_x=dr["L0_gamma_x"], beta_x=dr["L0_beta_x"],
                                            gamma_l=dr["L0_gamma_l"], beta_l=dr["L0_beta_l"]),
                        heads=8, head_dim=64, gate=0, own_keys=True, norm_ctx=True, rope_k=True)
        g.release()
        low_rank_ffn_stage(nc, g, dr)
        g.release()
        attention_stage(nc, g, "l1x_", dict(ctx=dr["ctx"], wq=dr["L1_wq"], wk=dr["L1_wk"], wv=dr["L1_wv"],
                                            wo=dr["L1_wo"], b_o=dr["L1_bo"]),
                        heads=8, head_dim=64, gate=1, out_bias=True)
        g.release()
        soft_moe_stage(nc, g, dr)
        g.release()
        attention_stage(nc, g, "l2x_", dict(ctx=dr["ctx"], wq=dr["L2_wq"], wqp=dr["L2_wqp"], wk=dr["L2_wk"],
                                            wkp=dr["L2_wkp"], wv=dr["L2_wv"], wo=dr["L2_wo"], cos=dr["L2_cos"],
                                            sin=dr["L2_sin"], sel=dr["sel4"], hmask=dr["hmask"], mask=dr["mask"]),
                        heads=16, head_dim=16, gate=2, rope_k=True, rope_q=True, masked=True)
        g.release()
        top2_gelu_stage(nc, g, dr)
        g.release()
        attention_stage(nc, g, "l3x_", dict(ctx=dr["ctx"], wq=dr["L3_wq"], wk=dr["L3_wk"], wv=dr["L3_wv"],
                                            b_q=dr["L3_bq"], b_k=dr["L3_bk"], b_v=dr["L3_bv"], wo=dr["L3_wo"],
                                            b_o=dr["L3_bo"], sel=dr["sel4"], hmask=dr["hmask"]),
                        heads=16, head_dim=16, gate=3, biased=True, out_bias=True)
        g.release()
        top2_silu_stage(nc, g, dr)
        g.release()

        with nc.Block() as block:
            s_out = g.semaphore("x_out")

            @block.sync
            def _(sp):
                sp.dma_start(out.rearrange("(n p) d -> p n d", p=P),
                             g.X[:, 0:B * ROW].rearrange("p (n d) -> p n d", d=D)).then_inc(s_out, 16)
                sp.wait_ge(s_out, 16)


def rotary_tables(head_dim, interleaved):
    inv = (np.float32(1.0) / np.float32(10000.0) ** (np.arange(0, head_dim, 2, dtype=np.float32) / np.float32(head_dim)))
    ang = np.arange(S, dtype=np.float32)[:, None] * inv.astype(np.float32)[None, :]
    ang = np.concatenate([ang, ang], axis=1).astype(np.float64)
    d = np.arange(head_dim)
    sign = np.where(d % 2 == 0, -1.0, 1.0) if interleaved else np.where(d < head_dim // 2, -1.0, 1.0)
    reps = P // head_dim
    return (np.tile(np.cos(ang).T, (reps, 1)).astype(np.float32),
            np.tile((np.sin(ang) * sign).T, (reps, 1)).astype(np.float32))


def partner_columns(n, head_dim, interleaved):
    c = np.arange(n)
    d = c % head_dim
    return c - d + (d ^ 1 if interleaved else (d + head_dim // 2) % head_dim)


def laid_out(inputs):
    a = {k: np.asarray(v) for k, v in inputs.items()}
    r = {"x": a["x"].reshape(B * S, D), "ctx": a["ctx_1024"].reshape(B * S, D),
         "mask": a["mask_1x1xSxS2_ik0"].reshape(S, S), "g_xattn": a["g_xattn"], "g_ffn": a["g_ffn"]}
    inner = a["L0_xattn_Wq"].shape[1]
    r["L0_wq"], r["L0_wo"] = a["L0_xattn_Wq"], a["L0_xattn_Wo"]
    r["L0_wk"], r["L0_wv"] = a["L0_xattn_Wkv"][:, :inner], a["L0_xattn_Wkv"][:, inner:]
    r["L0_wkp"] = r["L0_wk"][:, partner_columns(inner, 64, False)]
    for n in ("gamma_x", "beta_x", "gamma_l", "beta_l"):
        r[f"L0_{n}"] = a[f"L0_xattn_{n}"]
    for n in ("U1", "V1", "b1", "U2", "V2", "b2"):
        r[f"L0_{n}"] = a[f"L0_ffn_{n}"]
    for n in ("Wq", "Wk", "Wv", "Wo"):
        r[f"L1_{n.lower()}"] = a[f"L1_xattn_{n}"]
        r[f"L2_{n.lower()}"] = a[f"L2_xattn_{n.lower()}"].T
    r["L1_bo"] = a["L1_xattn_bo"]
    r["L1_phiT"] = a["L1_ffn_phi_w"].T
    for n in ("phi_b", "expert_w", "expert_b"):
        r[f"L1_{n}"] = a[f"L1_ffn_{n}"]
    swap = partner_columns(D, 16, True)
    r["L2_wqp"], r["L2_wkp"] = r["L2_wq"][:, swap], r["L2_wk"][:, swap]
    for n in ("Wg", "bg", "W1", "b1", "W2", "b2"):
        r[f"L2_{n}"] = a[f"L2_ffn_{n}"]
    r["L3_wq"], r["L3_bq"] = a["L3_xattn_w_q"], a["L3_xattn_b_q"]
    r["L3_wk"], r["L3_wv"] = a["L3_xattn_w_kv"][:, :D], a["L3_xattn_w_kv"][:, D:]
    r["L3_bk"], r["L3_bv"] = a["L3_xattn_b_kv"][:D], a["L3_xattn_b_kv"][D:]
    r["L3_wo"], r["L3_bo"] = a["L3_xattn_w_out"], a["L3_xattn_b_out"]
    for n in ("router_w", "router_b", "routed_w1", "routed_w3", "routed_w2", "shared_w1", "shared_w3", "shared_w2"):
        r[f"L3_{n}"] = a[f"L3_ffn_{n}"]
    r["L0_cos"], r["L0_sin"] = rotary_tables(64, False)
    r["L2_cos"], r["L2_sin"] = rotary_tables(16, True)
    r["ident"] = np.eye(P, dtype=np.float32)
    row = np.arange(P)
    r["sel4"] = (row[:, None] == 32 * (row[None, :] // 32) + 16).astype(np.float32)
    r["iota8"] = np.ones((P, 1), np.float32) * np.arange(8, dtype=np.float32)[None, :]
    r["hmask"] = (row[:, None] % HALF // 16 == np.arange(4)[None, :]).astype(np.float32)
    return {k: np.ascontiguousarray(v) for k, v in r.items()}


def kernel(**inputs):
    import concourse.bacc as _bacc
    from concourse.bass_utils import run_bass_kernel_spmd as _run

    nc = _bacc.Bacc("TRN2", target_bir_lowering=False, num_devices=1)
    arrays = laid_out(inputs)
    dr = {n: nc.dram_tensor(f"in_{n}", a.shape, mybir.dt.from_np(a.dtype), kind="ExternalInput").ap()
          for n, a in arrays.items()}
    out = nc.dram_tensor("out_0", (B * S, D), F32, kind="ExternalOutput").ap()
    program(nc, dr, out)
    r = _run(nc, [{f"in_{n}": a for n, a in arrays.items()}], core_ids=[0])
    return r.results[0]["out_0"].reshape(B, S, D)
```
